# Optimizing a Trainium2 kernel written in Bass

```python
import numpy as np
import jax
import jax.numpy as jnp

def _softmax(x, axis=-1):
    return jax.nn.softmax(x, axis=axis)

def _gelu(x):
    return jax.nn.gelu(x, approximate=True)

def _silu(x):
    return jax.nn.silu(x)

def _sigmoid(x):
    return jax.nn.sigmoid(x)

def _layernorm(x, axis=-1, eps=1e-05):
    m = jnp.mean(x, axis=axis, keepdims=True)
    v = jnp.var(x, axis=axis, keepdims=True)
    return (x - m) / jnp.sqrt(v + eps)

def _scatter_add(tgt, idx, src, axis=0):
    return tgt.at[idx].add(src)

def _segment_sum(src, seg, n):
    return jax.ops.segment_sum(src, seg, n)
kernel_name = 'mk_xattn_seq_d2_seqx_r8_342913'

def setup_inputs(seed: int=0):
    np.random.seed(seed)
    _w = jnp.asarray

    def _rec_inputs():
        import jax
        import jax.numpy as jnp
        _rk = jax.random.key(seed)
        x = 7.22e-05 + 1 * jax.random.normal(jax.random.fold_in(_rk, 1), (64, 64, 256), jnp.float32)
        _lenS = 64 - jax.random.randint(jax.random.fold_in(_rk, 7), (64,), 0, max(1, 64 // 4) + 1, jnp.int32)
        _lenS2 = 64 - jax.random.randint(jax.random.fold_in(_rk, 8), (64,), 0, max(1, 64 // 4) + 1, jnp.int32)
        _ctx_2048P = jax.random.normal(jax.random.fold_in(_rk, 11), (64, 16, 256), jnp.float32)
        _ctx_2048c = jax.random.dirichlet(jax.random.fold_in(_rk, 511), 0.3 * jnp.ones((16,), jnp.float32), (64, 64))
        _ctx_2048t = jnp.einsum('bsk,bkd->bsd', _ctx_2048c, _ctx_2048P)
        _ctx_2048t = _ctx_2048t * jax.lax.rsqrt(jnp.mean(jnp.square(_ctx_2048t)) + 1e-12) * 0.953939
        ctx_2048 = 0.000189249 + 0.0999589 * (_ctx_2048t + 0.3 * jax.random.normal(jax.random.fold_in(_rk, 611), (64, 64, 256), jnp.float32))
        return (x, ctx_2048)
    x, ctx_2048 = _rec_inputs()

    def _L0_xattn_setup():
        import jax, jax.numpy as jnp
        import numpy as np
        E, H, L, B = (256, 32, 128, 4)
        S = E // H
        DM, DD = (32, 64)

        def _ln(x, w, b, eps=1e-05):
            m = x.mean(-1, keepdims=True)
            v = ((x - m) ** 2).mean(-1, keepdims=True)
            return (x - m) / jnp.sqrt(v + eps) * w + b

        def _block(x, state, ln1_w, ln1_b, ln2_w, ln2_b, maa_x, maa_w1, maa_w2, maa_stack, time_decay, td_w1, td_w2, u, Wr, Wk, Wv, Wg, Wo, gn_w, gn_b, ffn_maa_k, ffn_maa_r, Wfk, Wfr, Wfv):
            b, l, e = x.shape
            h = u.shape[0]
            s_ = e // h
            xa = _ln(x, ln1_w, ln1_b)
            sx = jnp.concatenate([state[:, 1:2] - xa[:, :1], xa[:, :-1] - xa[:, 1:]], axis=1)
            xxx = jnp.tanh((xa + sx * maa_x) @ maa_w1).reshape(b, l, 5, DM)
            xxx = jnp.einsum('blfd,fde->blfe', xxx, maa_w2)
            xm = xa[:, :, None] + sx[:, :, None] * (maa_stack + xxx)
            xk, xw, xv, xr, xg = (xm[:, :, j] for j in range(5))
            w = jnp.exp(-jnp.exp(time_decay + jnp.tanh(xw @ td_w1) @ td_w2)).reshape(b, l, h, s_)
            r = (xr @ Wr.T).reshape(b, l, h, s_)
            k = (xk @ Wk.T).reshape(b, l, h, s_)
            v = (xv @ Wv.T).reshape(b, l, h, s_)
            g = jax.nn.silu(xg @ Wg.T)
            s0 = state[:, 2:2 + s_].reshape(b, h, s_, s_)

            def step(s, rkvw):
                r_t, k_t, v_t, w_t = rkvw
                a = k_t[..., :, None] * v_t[..., None, :]
                out = jnp.einsum('bhi,bhij->bhj', r_t, u * a + s)
                s = a + w_t[..., :, None] * s
                return (s, out)
            rkvw = tuple((jnp.moveaxis(t, 1, 0) for t in (r, k, v, w)))
            _, out = jax.lax.scan(step, s0, rkvw)
            out = jnp.moveaxis(out, 0, 1).reshape(b, l, e)
            og = out.reshape(b, l, h, s_)
            m = og.mean(-1, keepdims=True)
            va = ((og - m) ** 2).mean(-1, keepdims=True)
            og = ((og - m) / jnp.sqrt(va + 1e-05)).reshape(b, l, e) * gn_w + gn_b
            x1 = x + og * g @ Wo.T
            xc = _ln(x1, ln2_w, ln2_b)
            sx2 = jnp.concatenate([state[:, 0:1] - xc[:, :1], xc[:, :-1] - xc[:, 1:]], axis=1)
            xk2 = xc + sx2 * ffn_maa_k
            xr2 = xc + sx2 * ffn_maa_r
            rr = jax.nn.sigmoid(xr2 @ Wfr.T)
            kk = jnp.square(jax.nn.relu(xk2 @ Wfk.T))
            return x1 + rr * (kk @ Wfv.T)
        key = jax.random.key(seed)
        ks = jax.random.split(key, 24)
        sc = 0.02
        d = {'x': jax.random.normal(ks[0], (B, L, E), jnp.float32), 'state': jax.random.normal(ks[1], (B, 2 + S, E), jnp.float32) * 0.1, 'ln1_w': jnp.ones((E,), jnp.float32), 'ln1_b': jnp.zeros((E,), jnp.float32), 'ln2_w': jnp.ones((E,), jnp.float32), 'ln2_b': jnp.zeros((E,), jnp.float32), 'maa_x': jax.random.normal(ks[2], (E,), jnp.float32) * 0.1, 'maa_w1': jax.random.normal(ks[3], (E, 5 * DM), jnp.float32) * sc, 'maa_w2': jax.random.normal(ks[4], (5, DM, E), jnp.float32) * sc, 'maa_stack': jax.random.normal(ks[5], (1, 5, E), jnp.float32) * 0.1, 'time_decay': jax.random.normal(ks[6], (E,), jnp.float32) * 0.5, 'td_w1': jax.random.normal(ks[7], (E, DD), jnp.float32) * sc, 'td_w2': jax.random.normal(ks[8], (DD, E), jnp.float32) * sc, 'u': jax.random.normal(ks[9], (H, S, 1), jnp.float32) * 0.1, 'Wr': jax.random.normal(ks[10], (E, E), jnp.float32) * sc, 'Wk': jax.random.normal(ks[11], (E, E), jnp.float32) * sc, 'Wv': jax.random.normal(ks[12], (E, E), jnp.float32) * sc, 'Wg': jax.random.normal(ks[13], (E, E), jnp.float32) * sc, 'Wo': jax.random.normal(ks[14], (E, E), jnp.float32) * sc, 'gn_w': jnp.ones((E,), jnp.float32), 'gn_b': jnp.zeros((E,), jnp.float32), 'ffn_maa_k': jax.random.normal(ks[15], (E,), jnp.float32) * 0.1, 'ffn_maa_r': jax.random.normal(ks[16], (E,), jnp.float32) * 0.1, 'Wfk': jax.random.normal(ks[17], (E, E), jnp.float32) * sc, 'Wfr': jax.random.normal(ks[18], (E, E), jnp.float32) * sc, 'Wfv': jax.random.normal(ks[19], (E, E), jnp.float32) * sc}
        return d
    _L0_xattn_all = _L0_xattn_setup()
    _L0_xattn_in = {k: v for k, v in _L0_xattn_all.items() if k in ('ln1_w', 'ln1_b', 'ln2_w', 'ln2_b', 'maa_x', 'maa_w1', 'maa_w2', 'maa_stack', 'time_decay', 'td_w1', 'td_w2', 'u', 'Wr', 'Wk', 'Wv', 'Wg', 'Wo', 'gn_w', 'gn_b', 'ffn_maa_k', 'ffn_maa_r', 'Wfk', 'Wfr', 'Wfv')}
    del _L0_xattn_all

    def _L1_xattn_setup():
        import jax, jax.numpy as jnp
        import numpy as np
        N_HEAD = 32
        EPS = 1e-05

        def _ln(x, w, b):
            m = jnp.mean(x, axis=-1, keepdims=True)
            v = jnp.mean((x - m) ** 2, axis=-1, keepdims=True)
            return (x - m) * jax.lax.rsqrt(v + EPS) * w + b

        def _forward(x, state, i, ln1_w, ln1_b, ln2_w, ln2_b, maa_x, maa_w, maa_k, maa_v, maa_r, maa_g, maa_w1, maa_w2, time_decay, decay_w1, decay_w2, faaaa, Wr, Wk, Wv, Wg, Wo, gn_w, gn_b, fmaa_k, fmaa_r, fWk, fWr, fWv):
            B, L, C = x.shape
            H = N_HEAD
            S = C // H
            i0 = (2 + S) * i
            xa = _ln(x, ln1_w, ln1_b)
            sx = jnp.concatenate([state[:, i0 + 1][:, None], xa[:, :-1]], axis=1) - xa
            xxx = xa + sx * maa_x
            t = jnp.tanh(xxx @ maa_w1).reshape(B, L, 5, -1)
            m = jnp.einsum('blfd,fdc->blfc', t, maa_w2)
            mw, mk, mv, mr, mg = (m[:, :, j] for j in range(5))
            xw = xa + sx * (maa_w + mw)
            xk = xa + sx * (maa_k + mk)
            xv = xa + sx * (maa_v + mv)
            xr = xa + sx * (maa_r + mr)
            xg = xa + sx * (maa_g + mg)
            w = time_decay + jnp.tanh(xw @ decay_w1) @ decay_w2
            w = jnp.exp(-jnp.exp(w)).reshape(B, L, H, S)
            r = (xr @ Wr.T).reshape(B, L, H, S)
            k = (xk @ Wk.T).reshape(B, L, H, S)
            v = (xv @ Wv.T).reshape(B, L, H, S)
            g = jax.nn.silu(xg @ Wg.T)
            s0 = state[:, i0 + 2:i0 + 2 + S].reshape(B, H, S, S)

            def step(s, inp):
                k_l, v_l, w_l, r_l = inp
                a = k_l[..., :, None] * v_l[..., None, :]
                out = jnp.einsum('bhs,bhst->bht', r_l, faaaa * a + s)
                s_new = a + w_l[..., None] * s
                return (s_new, out)
            seq = tuple((z.transpose(1, 0, 2, 3) for z in (k, v, w, r)))
            _, outs = jax.lax.scan(step, s0, seq)
            y = outs.transpose(1, 0, 2, 3)
            gm = jnp.mean(y, axis=-1, keepdims=True)
            gv = jnp.mean((y - gm) ** 2, axis=-1, keepdims=True)
            y = ((y - gm) * jax.lax.rsqrt(gv + EPS)).reshape(B, L, C) * gn_w + gn_b
            x = x + y * g @ Wo.T
            xc = _ln(x, ln2_w, ln2_b)
            sxc = jnp.concatenate([state[:, i0][:, None], xc[:, :-1]], axis=1) - xc
            xk2 = xc + sxc * fmaa_k
            xr2 = xc + sxc * fmaa_r
            rr = jax.nn.sigmoid(xr2 @ fWr.T)
            kk = jnp.square(jax.nn.relu(xk2 @ fWk.T))
            x = x + rr * (kk @ fWv.T)
            return x
        key = jax.random.key(seed)
        B, L, C, H = (8, 64, 256, N_HEAD)
        S = C // H
        DM, DD = (32, 64)
        ks = jax.random.split(key, 32)
        n = lambda k, shp, s=1.0: jax.random.normal(k, shp, dtype=jnp.float32) * s
        u = lambda k, shp: jax.random.uniform(k, shp, dtype=jnp.float32)
        inp = {'x': n(ks[0], (B, L, C)), 'state': n(ks[1], (B, 2 + S, C), 0.1), 'i': 0, 'ln1_w': jnp.ones((C,), jnp.float32), 'ln1_b': jnp.zeros((C,), jnp.float32), 'ln2_w': jnp.ones((C,), jnp.float32), 'ln2_b': jnp.zeros((C,), jnp.float32), 'maa_x': u(ks[2], (C,)), 'maa_w': u(ks[3], (C,)), 'maa_k': u(ks[4], (C,)), 'maa_v': u(ks[5], (C,)), 'maa_r': u(ks[6], (C,)), 'maa_g': u(ks[7], (C,)), 'maa_w1': n(ks[8], (C, 5 * DM), 0.02), 'maa_w2': n(ks[9], (5, DM, C), 0.02), 'time_decay': n(ks[10], (C,), 0.5), 'decay_w1': n(ks[11], (C, DD), 0.02), 'decay_w2': n(ks[12], (DD, C), 0.02), 'faaaa': n(ks[13], (H, S, 1), 0.1), 'Wr': n(ks[14], (C, C), 0.02), 'Wk': n(ks[15], (C, C), 0.02), 'Wv': n(ks[16], (C, C), 0.02), 'Wg': n(ks[17], (C, C), 0.02), 'Wo': n(ks[18], (C, C), 0.02), 'gn_w': jnp.ones((C,), jnp.float32), 'gn_b': jnp.zeros((C,), jnp.float32), 'fmaa_k': u(ks[19], (C,)), 'fmaa_r': u(ks[20], (C,)), 'fWk': n(ks[21], (C, C), 0.02), 'fWr': n(ks[22], (C, C), 0.02), 'fWv': n(ks[23], (C, C), 0.02)}
        return inp
    _L1_xattn_all = _L1_xattn_setup()
    _L1_xattn_in = {k: v for k, v in _L1_xattn_all.items() if k in ('ln1_w', 'ln1_b', 'ln2_w', 'ln2_b', 'maa_x', 'maa_w', 'maa_k', 'maa_v', 'maa_r', 'maa_g', 'maa_w1', 'maa_w2', 'time_decay', 'decay_w1', 'decay_w2', 'faaaa', 'Wr', 'Wk', 'Wv', 'Wg', 'Wo', 'gn_w', 'gn_b', 'fmaa_k', 'fmaa_r', 'fWk', 'fWr', 'fWv')}
    del _L1_xattn_all
    return {'x': x, 'ctx_2048': ctx_2048, 'L0_xattn_ln1_w': _L0_xattn_in['ln1_w'], 'L0_xattn_ln1_b': _L0_xattn_in['ln1_b'], 'L0_xattn_ln2_w': _L0_xattn_in['ln2_w'], 'L0_xattn_ln2_b': _L0_xattn_in['ln2_b'], 'L0_xattn_maa_x': _L0_xattn_in['maa_x'], 'L0_xattn_maa_w1': _L0_xattn_in['maa_w1'], 'L0_xattn_maa_w2': _L0_xattn_in['maa_w2'], 'L0_xattn_maa_stack': _L0_xattn_in['maa_stack'], 'L0_xattn_time_decay': _L0_xattn_in['time_decay'], 'L0_xattn_td_w1': _L0_xattn_in['td_w1'], 'L0_xattn_td_w2': _L0_xattn_in['td_w2'], 'L0_xattn_u': _L0_xattn_in['u'], 'L0_xattn_Wr': _L0_xattn_in['Wr'], 'L0_xattn_Wk': _L0_xattn_in['Wk'], 'L0_xattn_Wv': _L0_xattn_in['Wv'], 'L0_xattn_Wg': _L0_xattn_in['Wg'], 'L0_xattn_Wo': _L0_xattn_in['Wo'], 'L0_xattn_gn_w': _L0_xattn_in['gn_w'], 'L0_xattn_gn_b': _L0_xattn_in['gn_b'], 'L0_xattn_ffn_maa_k': _L0_xattn_in['ffn_maa_k'], 'L0_xattn_ffn_maa_r': _L0_xattn_in['ffn_maa_r'], 'L0_xattn_Wfk': _L0_xattn_in['Wfk'], 'L0_xattn_Wfr': _L0_xattn_in['Wfr'], 'L0_xattn_Wfv': _L0_xattn_in['Wfv'], 'L1_xattn_ln1_w': _L1_xattn_in['ln1_w'], 'L1_xattn_ln1_b': _L1_xattn_in['ln1_b'], 'L1_xattn_ln2_w': _L1_xattn_in['ln2_w'], 'L1_xattn_ln2_b': _L1_xattn_in['ln2_b'], 'L1_xattn_maa_x': _L1_xattn_in['maa_x'], 'L1_xattn_maa_w': _L1_xattn_in['maa_w'], 'L1_xattn_maa_k': _L1_xattn_in['maa_k'], 'L1_xattn_maa_v': _L1_xattn_in['maa_v'], 'L1_xattn_maa_r': _L1_xattn_in['maa_r'], 'L1_xattn_maa_g': _L1_xattn_in['maa_g'], 'L1_xattn_maa_w1': _L1_xattn_in['maa_w1'], 'L1_xattn_maa_w2': _L1_xattn_in['maa_w2'], 'L1_xattn_time_decay': _L1_xattn_in['time_decay'], 'L1_xattn_decay_w1': _L1_xattn_in['decay_w1'], 'L1_xattn_decay_w2': _L1_xattn_in['decay_w2'], 'L1_xattn_faaaa': _L1_xattn_in['faaaa'], 'L1_xattn_Wr': _L1_xattn_in['Wr'], 'L1_xattn_Wk': _L1_xattn_in['Wk'], 'L1_xattn_Wv': _L1_xattn_in['Wv'], 'L1_xattn_Wg': _L1_xattn_in['Wg'], 'L1_xattn_Wo': _L1_xattn_in['Wo'], 'L1_xattn_gn_w': _L1_xattn_in['gn_w'], 'L1_xattn_gn_b': _L1_xattn_in['gn_b'], 'L1_xattn_fmaa_k': _L1_xattn_in['fmaa_k'], 'L1_xattn_fmaa_r': _L1_xattn_in['fmaa_r'], 'L1_xattn_fWk': _L1_xattn_in['fWk'], 'L1_xattn_fWr': _L1_xattn_in['fWr'], 'L1_xattn_fWv': _L1_xattn_in['fWv']}

def reference(x, ctx_2048, L0_xattn_ln1_w, L0_xattn_ln1_b, L0_xattn_ln2_w, L0_xattn_ln2_b, L0_xattn_maa_x, L0_xattn_maa_w1, L0_xattn_maa_w2, L0_xattn_maa_stack, L0_xattn_time_decay, L0_xattn_td_w1, L0_xattn_td_w2, L0_xattn_u, L0_xattn_Wr, L0_xattn_Wk, L0_xattn_Wv, L0_xattn_Wg, L0_xattn_Wo, L0_xattn_gn_w, L0_xattn_gn_b, L0_xattn_ffn_maa_k, L0_xattn_ffn_maa_r, L0_xattn_Wfk, L0_xattn_Wfr, L0_xattn_Wfv, L1_xattn_ln1_w, L1_xattn_ln1_b, L1_xattn_ln2_w, L1_xattn_ln2_b, L1_xattn_maa_x, L1_xattn_maa_w, L1_xattn_maa_k, L1_xattn_maa_v, L1_xattn_maa_r, L1_xattn_maa_g, L1_xattn_maa_w1, L1_xattn_maa_w2, L1_xattn_time_decay, L1_xattn_decay_w1, L1_xattn_decay_w2, L1_xattn_faaaa, L1_xattn_Wr, L1_xattn_Wk, L1_xattn_Wv, L1_xattn_Wg, L1_xattn_Wo, L1_xattn_gn_w, L1_xattn_gn_b, L1_xattn_fmaa_k, L1_xattn_fmaa_r, L1_xattn_fWk, L1_xattn_fWr, L1_xattn_fWv):
    import jax
    import jax.numpy as jnp

    def _L0_xattn_ref(x, state, ln1_w, ln1_b, ln2_w, ln2_b, maa_x, maa_w1, maa_w2, maa_stack, time_decay, td_w1, td_w2, u, Wr, Wk, Wv, Wg, Wo, gn_w, gn_b, ffn_maa_k, ffn_maa_r, Wfk, Wfr, Wfv):
        import jax, jax.numpy as jnp
        import numpy as np
        E, H, L, B = (256, 32, 128, 4)
        S = E // H
        DM, DD = (32, 64)

        def _ln(x, w, b, eps=1e-05):
            m = x.mean(-1, keepdims=True)
            v = ((x - m) ** 2).mean(-1, keepdims=True)
            return (x - m) / jnp.sqrt(v + eps) * w + b

        def _block(x, state, ln1_w, ln1_b, ln2_w, ln2_b, maa_x, maa_w1, maa_w2, maa_stack, time_decay, td_w1, td_w2, u, Wr, Wk, Wv, Wg, Wo, gn_w, gn_b, ffn_maa_k, ffn_maa_r, Wfk, Wfr, Wfv):
            b, l, e = x.shape
            h = u.shape[0]
            s_ = e // h
            xa = _ln(x, ln1_w, ln1_b)
            sx = jnp.concatenate([state[:, 1:2] - xa[:, :1], xa[:, :-1] - xa[:, 1:]], axis=1)
            xxx = jnp.tanh((xa + sx * maa_x) @ maa_w1).reshape(b, l, 5, DM)
            xxx = jnp.einsum('blfd,fde->blfe', xxx, maa_w2)
            xm = xa[:, :, None] + sx[:, :, None] * (maa_stack + xxx)
            xk, xw, xv, xr, xg = (xm[:, :, j] for j in range(5))
            w = jnp.exp(-jnp.exp(time_decay + jnp.tanh(xw @ td_w1) @ td_w2)).reshape(b, l, h, s_)
            r = (xr @ Wr.T).reshape(b, l, h, s_)
            k = (xk @ Wk.T).reshape(b, l, h, s_)
            v = (xv @ Wv.T).reshape(b, l, h, s_)
            g = jax.nn.silu(xg @ Wg.T)
            s0 = state[:, 2:2 + s_].reshape(b, h, s_, s_)

            def step(s, rkvw):
                r_t, k_t, v_t, w_t = rkvw
                a = k_t[..., :, None] * v_t[..., None, :]
                out = jnp.einsum('bhi,bhij->bhj', r_t, u * a + s)
                s = a + w_t[..., :, None] * s
                return (s, out)
            rkvw = tuple((jnp.moveaxis(t, 1, 0) for t in (r, k, v, w)))
            _, out = jax.lax.scan(step, s0, rkvw)
            out = jnp.moveaxis(out, 0, 1).reshape(b, l, e)
            og = out.reshape(b, l, h, s_)
            m = og.mean(-1, keepdims=True)
            va = ((og - m) ** 2).mean(-1, keepdims=True)
            og = ((og - m) / jnp.sqrt(va + 1e-05)).reshape(b, l, e) * gn_w + gn_b
            x1 = x + og * g @ Wo.T
            xc = _ln(x1, ln2_w, ln2_b)
            sx2 = jnp.concatenate([state[:, 0:1] - xc[:, :1], xc[:, :-1] - xc[:, 1:]], axis=1)
            xk2 = xc + sx2 * ffn_maa_k
            xr2 = xc + sx2 * ffn_maa_r
            rr = jax.nn.sigmoid(xr2 @ Wfr.T)
            kk = jnp.square(jax.nn.relu(xk2 @ Wfk.T))
            return x1 + rr * (kk @ Wfv.T)
        return _block(x, state, ln1_w, ln1_b, ln2_w, ln2_b, maa_x, maa_w1, maa_w2, maa_stack, time_decay, td_w1, td_w2, u, Wr, Wk, Wv, Wg, Wo, gn_w, gn_b, ffn_maa_k, ffn_maa_r, Wfk, Wfr, Wfv)

    def _L1_xattn_ref(x, state, i, ln1_w, ln1_b, ln2_w, ln2_b, maa_x, maa_w, maa_k, maa_v, maa_r, maa_g, maa_w1, maa_w2, time_decay, decay_w1, decay_w2, faaaa, Wr, Wk, Wv, Wg, Wo, gn_w, gn_b, fmaa_k, fmaa_r, fWk, fWr, fWv):
        import jax, jax.numpy as jnp
        import numpy as np
        N_HEAD = 32
        EPS = 1e-05

        def _ln(x, w, b):
            m = jnp.mean(x, axis=-1, keepdims=True)
            v = jnp.mean((x - m) ** 2, axis=-1, keepdims=True)
            return (x - m) * jax.lax.rsqrt(v + EPS) * w + b

        def _forward(x, state, i, ln1_w, ln1_b, ln2_w, ln2_b, maa_x, maa_w, maa_k, maa_v, maa_r, maa_g, maa_w1, maa_w2, time_decay, decay_w1, decay_w2, faaaa, Wr, Wk, Wv, Wg, Wo, gn_w, gn_b, fmaa_k, fmaa_r, fWk, fWr, fWv):
            B, L, C = x.shape
            H = N_HEAD
            S = C // H
            i0 = (2 + S) * i
            xa = _ln(x, ln1_w, ln1_b)
            sx = jnp.concatenate([state[:, i0 + 1][:, None], xa[:, :-1]], axis=1) - xa
            xxx = xa + sx * maa_x
            t = jnp.tanh(xxx @ maa_w1).reshape(B, L, 5, -1)
            m = jnp.einsum('blfd,fdc->blfc', t, maa_w2)
            mw, mk, mv, mr, mg = (m[:, :, j] for j in range(5))
            xw = xa + sx * (maa_w + mw)
            xk = xa + sx * (maa_k + mk)
            xv = xa + sx * (maa_v + mv)
            xr = xa + sx * (maa_r + mr)
            xg = xa + sx * (maa_g + mg)
            w = time_decay + jnp.tanh(xw @ decay_w1) @ decay_w2
            w = jnp.exp(-jnp.exp(w)).reshape(B, L, H, S)
            r = (xr @ Wr.T).reshape(B, L, H, S)
            k = (xk @ Wk.T).reshape(B, L, H, S)
            v = (xv @ Wv.T).reshape(B, L, H, S)
            g = jax.nn.silu(xg @ Wg.T)
            s0 = state[:, i0 + 2:i0 + 2 + S].reshape(B, H, S, S)

            def step(s, inp):
                k_l, v_l, w_l, r_l = inp
                a = k_l[..., :, None] * v_l[..., None, :]
                out = jnp.einsum('bhs,bhst->bht', r_l, faaaa * a + s)
                s_new = a + w_l[..., None] * s
                return (s_new, out)
            seq = tuple((z.transpose(1, 0, 2, 3) for z in (k, v, w, r)))
            _, outs = jax.lax.scan(step, s0, seq)
            y = outs.transpose(1, 0, 2, 3)
            gm = jnp.mean(y, axis=-1, keepdims=True)
            gv = jnp.mean((y - gm) ** 2, axis=-1, keepdims=True)
            y = ((y - gm) * jax.lax.rsqrt(gv + EPS)).reshape(B, L, C) * gn_w + gn_b
            x = x + y * g @ Wo.T
            xc = _ln(x, ln2_w, ln2_b)
            sxc = jnp.concatenate([state[:, i0][:, None], xc[:, :-1]], axis=1) - xc
            xk2 = xc + sxc * fmaa_k
            xr2 = xc + sxc * fmaa_r
            rr = jax.nn.sigmoid(xr2 @ fWr.T)
            kk = jnp.square(jax.nn.relu(xk2 @ fWk.T))
            x = x + rr * (kk @ fWv.T)
            return x
        return _forward(x, state, i, ln1_w, ln1_b, ln2_w, ln2_b, maa_x, maa_w, maa_k, maa_v, maa_r, maa_g, maa_w1, maa_w2, time_decay, decay_w1, decay_w2, faaaa, Wr, Wk, Wv, Wg, Wo, gn_w, gn_b, fmaa_k, fmaa_r, fWk, fWr, fWv)
    x = _L0_xattn_ref(x, ctx_2048, L0_xattn_ln1_w, L0_xattn_ln1_b, L0_xattn_ln2_w, L0_xattn_ln2_b, L0_xattn_maa_x, L0_xattn_maa_w1, L0_xattn_maa_w2, L0_xattn_maa_stack, L0_xattn_time_decay, L0_xattn_td_w1, L0_xattn_td_w2, L0_xattn_u, L0_xattn_Wr, L0_xattn_Wk, L0_xattn_Wv, L0_xattn_Wg, L0_xattn_Wo, L0_xattn_gn_w, L0_xattn_gn_b, L0_xattn_ffn_maa_k, L0_xattn_ffn_maa_r, L0_xattn_Wfk, L0_xattn_Wfr, L0_xattn_Wfv)
    x = _L1_xattn_ref(x, ctx_2048, 0, L1_xattn_ln1_w, L1_xattn_ln1_b, L1_xattn_ln2_w, L1_xattn_ln2_b, L1_xattn_maa_x, L1_xattn_maa_w, L1_xattn_maa_k, L1_xattn_maa_v, L1_xattn_maa_r, L1_xattn_maa_g, L1_xattn_maa_w1, L1_xattn_maa_w2, L1_xattn_time_decay, L1_xattn_decay_w1, L1_xattn_decay_w2, L1_xattn_faaaa, L1_xattn_Wr, L1_xattn_Wk, L1_xattn_Wv, L1_xattn_Wg, L1_xattn_Wo, L1_xattn_gn_w, L1_xattn_gn_b, L1_xattn_fmaa_k, L1_xattn_fmaa_r, L1_xattn_fWk, L1_xattn_fWr, L1_xattn_fWv)
    return x

_drawn_inputs = setup_inputs


def setup_inputs(seed=0):
    import zlib

    import numpy as np

    out = dict(_drawn_inputs(seed))
    spreads = {'L0_xattn_ln1_w': (1.0, 0.552),
     'L0_xattn_ln1_b': (0.0, 0.559),
     'L0_xattn_ln2_w': (1.0, 0.6),
     'L0_xattn_ln2_b': (0.0, 0.8),
     'L0_xattn_gn_w': (1.0, 0.6),
     'L0_xattn_gn_b': (0.0, 0.8),
     'L1_xattn_ln1_w': (1.0, 0.6),
     'L1_xattn_ln1_b': (0.0, 0.562),
     'L1_xattn_ln2_w': (1.0, 0.6),
     'L1_xattn_ln2_b': (0.0, 0.8),
     'L1_xattn_gn_w': (1.0, 0.6),
     'L1_xattn_gn_b': (0.0, 0.8)}
    factors = {'ctx_2048': 5.034,
     'L0_xattn_maa_x': 8.0,
     'L0_xattn_maa_w1': 6.894,
     'L0_xattn_maa_w2': 6.877,
     'L0_xattn_time_decay': 2.745,
     'L0_xattn_td_w1': 8.0,
     'L0_xattn_td_w2': 8.0,
     'L0_xattn_u': 5.32,
     'L0_xattn_ffn_maa_k': 8.0,
     'L0_xattn_ffn_maa_r': 8.0,
     'L0_xattn_Wfk': 2.97,
     'L0_xattn_Wfr': 8.0,
     'L0_xattn_Wfv': 2.751,
     'L1_xattn_maa_x': 8.0,
     'L1_xattn_maa_w': 8.0,
     'L1_xattn_maa_w1': 8.0,
     'L1_xattn_maa_w2': 8.0,
     'L1_xattn_time_decay': 3.791,
     'L1_xattn_decay_w1': 8.0,
     'L1_xattn_decay_w2': 8.0,
     'L1_xattn_faaaa': 7.375,
     'L1_xattn_fmaa_k': 7.354,
     'L1_xattn_fmaa_r': 8.0,
     'L1_xattn_fWk': 4.231,
     'L1_xattn_fWr': 8.0,
     'L1_xattn_fWv': 3.84}
    for name, (base, spread) in spreads.items():
        noise = np.random.default_rng([zlib.crc32(name.encode()), seed]).standard_normal(out[name].shape)
        drawn = base * np.exp(spread * noise) if base else spread * noise
        out[name] = jnp.asarray(drawn.astype(out[name].dtype))
    for name, factor in factors.items():
        out[name] = (out[name] * factor).astype(out[name].dtype)
    return out
```

```python
from contextlib import ExitStack

import numpy as np

import concourse.bass as bass
from concourse import mybir

F32 = mybir.dt.float32
I32 = mybir.dt.int32
ALU = mybir.AluOpType
ACT = mybir.ActivationFunctionType

P = 128
BATCH, SEQ, C = 64, 64, 256
HEADS, HS = 32, 8
DM = 32
DD = 64
NMIX = 5
LAYERS = 2
EPS = 1e-5

HALVES = C // P
HPH = HEADS // HALVES
ROWS = 8
TILES = BATCH // ROWS
TOK = ROWS * SEQ
BLK = TOK // P
ITEMS = LAYERS * TILES
STEPS = HALVES * HS
QUADS = STEPS // 4
ROUNDS = STEPS + 2

MW, MK, MV, MR, MG = range(NMIX)
MIX_NAMES = ("mw", "mk", "mv", "mr", "mg")


def columns(parts):
    at, out = 0, {}
    for name, n in parts:
        out[name] = (at, at + n)
        at += n
    out["total"] = at
    return out


COLS_A = columns([("w1a", 2 * P), ("w1b", 2 * P), ("w2", NMIX * 2 * P), ("td1", 2 * P), ("td2", 2 * P),
                  ("wk", 2 * C), ("wv", 2 * C), ("wr", 2 * C), ("wg", 2 * C),
                  ("ln_w", 2), ("ln_b", 2), ("maa_x", 2), ("maa", 2 * NMIX), ("decay", 2), ("u", 2)])
COLS_C = columns([("wo", 2 * C), ("fk", 2 * C), ("fr", 2 * C), ("fv", 2 * C),
                  ("gn_w", 2), ("gn_b", 2), ("ln_w", 2), ("ln_b", 2), ("mix_k", 2), ("mix_r", 2)])
COLS_K = columns([("ident", P), ("spread", HS * P), ("gather", 2 * 32), ("center", P), ("headsum", P),
                  ("var", 2 * 32), ("rstd", 8 * P)])
HALF_STATE = HS * ROWS + ROWS
STATE_COLS = HALVES * (HALF_STATE + ROWS)


def packed_channel(pi):
    jj, rest = divmod(pi, 32)
    jq, head = divmod(rest, HPH)
    return head * HS + 4 * jq + jj


PACKED = np.array([packed_channel(pi) for pi in range(P)])


def build(nc, x, state, weights_a, weights_c, consts, out):
    mid = nc.dram_tensor("layer0_out", [BATCH * SEQ, C], F32, kind="Internal").ap()
    tiled = lambda t: t.rearrange("(g q p) c -> g p q c", p=P, q=BLK)
    x_t, mid_t, out_t = tiled(x), tiled(mid), tiled(out)

    with ExitStack() as ctx:
        def sb(name, shape, dt=F32):
            return ctx.enter_context(nc.sbuf_tensor(name, shape, dt))

        def sem(name):
            return ctx.enter_context(nc.semaphore(name))

        wa = sb("wa", [P, COLS_A["total"]])
        wc = sb("wc", [P, COLS_C["total"]])
        kc = sb("kc", [P, COLS_K["total"]])
        x_in = sb("x_in", [P, BLK, C])
        states = sb("states", [P, 2, HALVES * HALF_STATE])
        stats_a = sb("stats_a", [P, BLK, 6])
        mv_a = sb("mv_a", [P, BLK, 2])
        veps_a = sb("veps_a", [P, BLK])
        rstd_a = sb("rstd_a", [P, BLK])
        mhalf = sb("mhalf", [P, BLK])
        held = sb("held", [P, 1])
        eps_t = sb("eps_t", [P, BLK])
        xhat = sb("xhat", [P, BLK, C])
        z_half = xhat[:, :, :].rearrange("p q c -> p (q c)").rearrange("p (h t) -> p h t", h=2)
        xa = sb("xa", [P, HALVES, ROWS, SEQ + 1])
        sx = sb("sx", [P, HALVES, TOK])
        xx = sb("xx", [P, HALVES, TOK])
        t_mix = sb("t_mix", [P, 2, TOK])
        xf = sb("xf", [P, 2, HALVES, TOK])
        th = sb("th", [P, TOK])
        e_dec = sb("e_dec", [P, HALVES, TOK])
        w_prev = sb("w_prev", [P, 2, HALVES, TOK])
        k_sb = sb("k_sb", [P, 2, HALVES, TOK])
        v_sb = sb("v_sb", [P, 2, HALVES, TOK])
        r_sb = sb("r_sb", [P, 2, HALVES, TOK])
        ruk = sb("ruk", [P, HALVES, TOK])
        bonus = sb("bonus", [P, 2, HALVES, TOK])
        gate = sb("gate", [P, 2, HALVES, TOK])
        a_in = sb("a_in", [P, 4, TOK])
        S = sb("S", [P, 4, TOK])
        rS = sb("rS", [P, 8, TOK])
        y_sb = sb("y_sb", [P, HALVES, TOK])
        x_res = sb("x_res", [P, BLK, C])
        row_c = sb("row_c", [P, HALVES * ROWS])
        c_one = sb("c_one", [P, 2 * TOK])
        c_two = sb("c_two", [P, HALVES, TOK])
        nw = sb("nw", [P, 3, P])
        o_sb = sb("o_sb", [P, HALVES, TOK])
        x1 = sb("x1", [P, BLK, C])
        xc = sb("xc", [P, HALVES, ROWS, SEQ + 1])
        xr2 = sb("xr2", [P, HALVES, TOK])
        kk = sb("kk", [P, HALVES, TOK])
        o_tile = sb("o_tile", [P, BLK, C])
        stats_c = sb("stats_c", [P, BLK, 6])
        mv_c = sb("mv_c", [P, BLK, 2])
        veps_c = sb("veps_c", [P, BLK])
        rstd_c = sb("rstd_c", [P, BLK])
        sq = c_one[:, :].rearrange("p (h t) -> p h t", h=2)
        x1hat = c_one[:, :].rearrange("p (q c) -> p q c", c=C)
        rr = x1hat
        bank = [ctx.enter_context(nc.psum_tensor(f"bank{i}", [P, TOK], F32)) for i in range(8)]
        bank_a, bank_c, bank_v, bank_y = bank[0:3], bank[3:5], bank[5:7], bank[7]

        def cols(t, table, name, i=0, n=None):
            a, b = table[name]
            return t[:, a + i * n:a + (i + 1) * n] if n else t[:, a:b]

        def A_(name, i=0, n=P):
            return cols(wa, COLS_A, name, i, n)

        def C_(name, i=0, n=P):
            return cols(wc, COLS_C, name, i, n)

        def K_(name, i=0, n=P):
            return cols(kc, COLS_K, name, i, n)

        def proj(table, t, name, k, m):
            a = table[name][0] + k * C + m * P
            return t[:, a:a + P]

        ident = K_("ident")

        consts_loaded = sem("consts_loaded")
        wa_valid, wc_valid = sem("wa_valid"), sem("wc_valid")
        wa_loaded, wc_loaded = sem("wa_loaded"), sem("wc_loaded")
        x_loaded, states_loaded = sem("x_loaded"), sem("states_loaded")
        res_loaded, row_loaded, stored = sem("res_loaded"), sem("row_loaded"), sem("stored")
        init_done = sem("init_done")
        a_stats, a_mv, a_veps, a_rstd, a_xhat = map(sem, ("a_stats", "a_mv", "a_veps", "a_rstd", "a_xhat"))
        a_tr, a_prev, a_xa, a_sx, a_xx = map(sem, ("a_tr", "a_prev", "a_xa", "a_sx", "a_xx"))
        a_T, a_t, a_m, a_stt, a_xf = map(sem, ("a_T", "a_t", "a_m", "a_stt", "a_xf"))
        a_td1, a_th, a_td2, a_e, a_w = map(sem, ("a_td1", "a_th", "a_td2", "a_e", "a_w"))
        p_k, p_v, p_r, p_g = map(sem, ("p_k", "p_v", "p_r", "p_g"))
        a_k, a_v, a_r, a_ruk, a_ds, a_bonus = map(sem, ("a_k", "a_v", "a_r", "a_ruk", "a_ds", "a_bonus"))
        a_thg, a_z, a_gate_done = map(sem, ("a_thg", "a_z", "a_gate_done"))
        b_s0, b_v, b_a, b_S, b_rS = map(sem, ("b_s0", "b_v", "b_a", "b_S", "b_rS"))
        b_red, b_y = sem("b_red"), sem("b_y")
        c_cen, c_yc, c_sq, c_var, c_nw = map(sem, ("c_cen", "c_yc", "c_sq", "c_var", "c_nw"))
        c_R, c_o1, c_o, c_wo, c_x1 = map(sem, ("c_R", "c_o1", "c_o", "c_wo", "c_x1"))
        c_stats, c_mv, c_veps, c_rstd, c_xh = map(sem, ("c_stats", "c_mv", "c_veps", "c_rstd", "c_xh"))
        c_tr, c_prev, c_xc, c_sx, c_xk, c_xr = map(sem, ("c_tr", "c_prev", "c_xc", "c_sx", "c_xk", "c_xr"))
        c_fk, c_relu, c_kk, c_fr, c_rr, c_fv, c_tmp, c_out = map(
            sem, ("c_fk", "c_relu", "c_kk", "c_fr", "c_rr", "c_fv", "c_tmp", "c_out"))
        NEWTON = 12

        def count(n, per, k):
            v = n * per + k
            return max(v, 0) if isinstance(v, int) else v

        A_USES = ("tr0", "tr1", "t0", "t1", "mw0", "mw1", "mk0", "mk1", "td1", "mv0", "mv1", "td20", "td21", "k0", "k1",
                  "mr0", "mr1", "v0", "v1", "mg0", "mg1", "r0", "r1", "ds0", "ds1", "g0", "g1")
        assert len(A_USES) % 3 == 0
        in_bank_a = {name: bank_a[u % 3] for u, name in enumerate(A_USES)}

        def run_slots(eng, rounds):
            rounds(0, None, None, 0)
            rounds(1, 0, None, 1)
            rounds(2, 1, 0, 0)
            with eng.Fori(0, (ITEMS - 4) // 2) as i:
                s = 2 * i + 3
                rounds(s, s - 1, s - 2, 1)
                rounds(s + 1, s, s - 1, 0)
            rounds(ITEMS - 1, ITEMS - 2, ITEMS - 3, 1)
            rounds(None, ITEMS - 1, ITEMS - 2, 0)
            rounds(None, None, ITEMS - 1, 1)

        block = ctx.enter_context(nc.Block())

        @block.sync
        def _(sp):
            sp.dma_start(x_in[:, :, :], x_t[0]).then_inc(x_loaded, 16)
            sp.dma_start(kc[:, :], consts).then_inc(consts_loaded, 16)
            sp.dma_start(wa[:, :], weights_a[0]).then_inc(wa_loaded, 16)
            sp.dma_start(states[:, 0, :], state[0, :, :HALVES * HALF_STATE]).then_inc(states_loaded, 16)
            sp.dma_start(wc[:, :], weights_c[0]).then_inc(wc_loaded, 16)
            sp.wait_ge(wa_loaded, 16)
            sp.sem_inc(wa_valid, TILES)
            sp.wait_ge(wc_loaded, 16)
            sp.sem_inc(wc_valid, TILES)

            def load_a(n, g, src, parity):
                sp.wait_ge(a_xhat, count(n - 1, BLK, BLK))
                sp.dma_start(x_in[:, :, :], src[g]).then_inc(x_loaded, 16)
                sp.wait_ge(b_s0, count(n - 2, STEPS, STEPS))
                sp.wait_ge(a_prev, count(n - 2, 1, 1))
                sp.dma_start(states[:, parity, :], state[g, :, :HALVES * HALF_STATE]).then_inc(states_loaded, 16)

            def load_c(n, g, src):
                sp.wait_ge(c_x1, count(n - 1, 2, 2))
                sp.dma_start(x_res[:, :, :], src[g]).then_inc(res_loaded, 16)
                sp.wait_ge(c_prev, count(n - 1, 1, 1))
                sp.dma_start(row_c[:, :], state[g, :, HALVES * HALF_STATE:]).then_inc(row_loaded, 16)

            def store(n, g, dst):
                sp.wait_ge(c_out, count(n, 2, 2))
                sp.dma_start(dst[g], o_tile[:, :, :]).then_inc(stored, 16)

            for s in range(ITEMS + 2):
                n = s + 1
                if n < ITEMS:
                    if n >= TILES:
                        sp.wait_ge(stored, count(n - TILES, 16, 16))
                    load_a(n, n % TILES, x_t if n < TILES else mid_t, n % 2)
                if n == TILES:
                    sp.wait_ge(p_g, count(TILES - 1, 2, 2))
                    sp.wait_ge(a_e, count(TILES - 1, 2, 2))
                    sp.wait_ge(a_stt, count(TILES - 1, 10, 10))
                    sp.wait_ge(a_ruk, count(TILES - 1, 2, 2))
                    sp.dma_start(wa[:, :], weights_a[1]).then_inc(wa_loaded, 16)
                    sp.wait_ge(wa_loaded, 32)
                    sp.sem_inc(wa_valid, TILES)
                n = s - 1
                if 0 <= n < ITEMS:
                    load_c(n, n % TILES, x_t if n < TILES else mid_t)
                n = s - 2
                if 0 <= n < ITEMS:
                    store(n, n % TILES, mid_t if n < TILES else out_t)
                if n == TILES - 1:
                    sp.wait_ge(c_fv, count(TILES - 1, 2, 2))
                    sp.dma_start(wc[:, :], weights_c[1]).then_inc(wc_loaded, 16)
                    sp.wait_ge(wc_loaded, 32)
                    sp.sem_inc(wc_valid, TILES)
            sp.wait_ge(stored, 16 * ITEMS)

        @block.tensor
        def _(pe):
            def mm(o, l, r, start=True, stop=True):
                return pe.matmul(o, l, r, start=start, stop=stop, skip_group_check=True)

            def a_transpose(n, c):
                pe.wait_ge(a_xhat, count(n, BLK, BLK))
                pe.wait_ge(a_bonus, count(n - 1, 2, 2))
                pe.wait_ge(a_z, count(n - 1, 2, 2))
                for h in range(HALVES):
                    for q in range(BLK):
                        m = pe.transpose(in_bank_a[f"tr{h}"][:, q * P:(q + 1) * P], xhat[:, q, h * P:(h + 1) * P],
                                         ident)
                    m.then_inc(a_tr, 1)

            def a_rank1(n, c):
                pe.wait_ge(a_xx, count(n, 2, 2))
                for k in range(HALVES):
                    m = mm(in_bank_a["t0"][:, :], A_("w1a", k), xx[:, k, :], k == 0, k == 1)
                m.then_inc(a_T, 1)
                pe.wait_ge(a_xa, count(n, 2, 1))
                for k in range(HALVES):
                    m = mm(in_bank_a["t1"][:, :], A_("w1b", k), xx[:, k, :], k == 0, k == 1)
                m.then_inc(a_T, 1)

            def a_rank2(n, c, f, h):
                mm(in_bank_a[f"{MIX_NAMES[f]}{h}"][:, :], A_("w2", 2 * f + h), t_mix[:, 0 if f < 4 else 1, :])\
                    .then_inc(a_m, 1)

            def a_rank2_w(n, c):
                pe.wait_ge(a_xa, count(n, 2, 2))
                pe.wait_ge(a_t, count(n, 2, 1))
                a_rank2(n, c, MW, 0)
                a_rank2(n, c, MW, 1)

            def a_rank2_k(n, c):
                pe.wait_ge(a_t, count(n, 2, 2))
                a_rank2(n, c, MK, 0)
                pe.wait_ge(a_stt, count(n, 10, 1))
                a_rank2(n, c, MK, 1)

            def a_decay1(n, c):
                pe.wait_ge(a_xf, count(n, 10, 2))
                pe.wait_ge(a_stt, count(n, 10, 2))
                for k in range(HALVES):
                    m = mm(in_bank_a["td1"][:, :], A_("td1", k), xf[:, 0, k, :], k == 0, k == 1)
                m.then_inc(a_td1, 1)

            def a_rank2_v(n, c):
                pe.wait_ge(a_stt, count(n, 10, 3))
                a_rank2(n, c, MV, 0)
                pe.wait_ge(a_stt, count(n, 10, 4))
                a_rank2(n, c, MV, 1)

            def a_decay2(n, c):
                pe.wait_ge(a_th, count(n, 1, 1))
                mm(in_bank_a["td20"][:, :], A_("td2", 0), th[:, :]).then_inc(a_td2, 1)
                pe.wait_ge(a_stt, count(n, 10, 5))
                mm(in_bank_a["td21"][:, :], A_("td2", 1), th[:, :]).then_inc(a_td2, 1)

            def a_proj(n, c, f, name, h, done):
                for k in range(HALVES):
                    m = mm(in_bank_a[f"{name}{h}"][:, :], proj(COLS_A, wa, "w" + name, k, h), xf[:, f % 2, k, :],
                           k == 0, k == 1)
                m.then_inc(done, 1)

            def a_proj_k(n, c):
                pe.wait_ge(a_xf, count(n, 10, 2 * MK + 2))
                pe.wait_ge(a_stt, count(n, 10, 6))
                a_proj(n, c, MK, "k", 0, p_k)
                pe.wait_ge(a_e, count(n, 2, 1))
                a_proj(n, c, MK, "k", 1, p_k)

            def a_rank2_r(n, c):
                pe.wait_ge(a_e, count(n, 2, 2))
                a_rank2(n, c, MR, 0)
                pe.wait_ge(a_k, count(n, 2, 1))
                a_rank2(n, c, MR, 1)

            def a_proj_v(n, c):
                pe.wait_ge(a_xf, count(n, 10, 2 * MV + 2))
                pe.wait_ge(a_k, count(n, 2, 2))
                a_proj(n, c, MV, "v", 0, p_v)
                pe.wait_ge(a_stt, count(n, 10, 7))
                a_proj(n, c, MV, "v", 1, p_v)

            def a_rank2_g(n, c):
                pe.wait_ge(a_stt, count(n, 10, 8))
                a_rank2(n, c, MG, 0)
                pe.wait_ge(a_v, count(n, 2, 1))
                a_rank2(n, c, MG, 1)

            def a_proj_r(n, c):
                pe.wait_ge(a_xf, count(n, 10, 2 * MR + 2))
                pe.wait_ge(a_v, count(n, 2, 2))
                a_proj(n, c, MR, "r", 0, p_r)
                pe.wait_ge(a_stt, count(n, 10, 9))
                a_proj(n, c, MR, "r", 1, p_r)

            def a_headsum(n, c):
                pe.wait_ge(a_ruk, count(n, 2, 1))
                pe.wait_ge(a_stt, count(n, 10, 10))
                mm(in_bank_a["ds0"][:, :], K_("headsum"), ruk[:, 0, :]).then_inc(a_ds, 1)
                pe.wait_ge(a_ruk, count(n, 2, 2))
                pe.wait_ge(a_r, count(n, 2, 1))
                mm(in_bank_a["ds1"][:, :], K_("headsum"), ruk[:, 1, :]).then_inc(a_ds, 1)

            def a_proj_g(n, c):
                pe.wait_ge(a_xf, count(n, 10, 2 * MG + 2))
                pe.wait_ge(a_r, count(n, 2, 2))
                a_proj(n, c, MG, "g", 0, p_g)
                pe.wait_ge(a_bonus, count(n, 2, 1))
                a_proj(n, c, MG, "g", 1, p_g)

            def b_spread(n, c, i):
                h, j = divmod(i, HS)
                if i == 0:
                    pe.wait_ge(a_v, count(n, 2, 2))
                if i >= 2:
                    pe.wait_ge(b_a, count(n, STEPS, i - 1))
                else:
                    pe.wait_ge(b_a, count(n - 1, STEPS, STEPS))
                mm(bank_v[i % 2][:, :], K_("spread", j), v_sb[:, c, h, :]).then_inc(b_v, 1)

            def b_reduce(n, c, q):
                h, jq = divmod(q, 2)
                pe.wait_ge(b_rS, count(n, STEPS, 4 * q + 4))
                if jq == 0:
                    if h == 1:
                        pe.wait_ge(b_y, count(n, 2, 1))
                    else:
                        pe.wait_ge(b_y, count(n - 1, 2, 2))
                for jj in range(4):
                    m = mm(bank_y[32 * jj:32 * jj + 32, :], K_("gather", jq, 32), rS[:, 4 * (q % 2) + jj, :],
                           jq == 0, jq == 1)
                m.then_inc(b_red, 1)

            def c_center(n, c):
                for h in range(HALVES):
                    pe.wait_ge(b_y, count(n, 2, h + 1))
                    pe.wait_ge(c_tmp, count(n - 1, 2, 2))
                    mm(bank_c[h][:, :], K_("center"), y_sb[:, h, :]).then_inc(c_cen, 1)

            def c_variance(n, c):
                pe.wait_ge(c_sq, count(n, 2, 2))
                pe.wait_ge(c_yc, count(n, 2, 1))
                for q in range(BLK):
                    for h in range(HALVES):
                        m = mm(bank_c[0][32 * q:32 * q + 32, 0:P], K_("var", h, 32), sq[:, h, q * P:(q + 1) * P],
                               h == 0, h == 1)
                m.then_inc(c_var, 1)

            def c_rstd_spread(n, c):
                pe.wait_ge(c_nw, count(n, NEWTON, NEWTON))
                pe.wait_ge(c_yc, count(n, 2, 2))
                for h in range(HALVES):
                    for q in range(BLK):
                        m = mm(bank_c[1 - h][:, q * P:(q + 1) * P], K_("rstd", 4 * h + q), nw[:, 1, :])
                    m.then_inc(c_R, 1)

            def c_out_proj(n, c):
                pe.wait_ge(c_o, count(n, 2, 2))
                for b in range(2):
                    for q in (2 * b, 2 * b + 1):
                        for k in range(HALVES):
                            m = mm(bank_c[1 - b][:, (q % 2) * C:(q % 2 + 1) * C], o_sb[:, k, q * P:(q + 1) * P],
                                   C_("wo", k, C), k == 0, k == 1)
                    m.then_inc(c_wo, 1)

            def c_transpose(n, c):
                pe.wait_ge(c_xh, count(n, BLK, BLK))
                pe.wait_ge(c_x1, count(n, 2, 2))
                for h in range(HALVES):
                    for q in range(BLK):
                        m = pe.transpose(bank_c[1 - h][:, q * P:(q + 1) * P], x1hat[:, q, h * P:(h + 1) * P], ident)
                    m.then_inc(c_tr, 1)

            def c_ffn_key(n, c):
                pe.wait_ge(c_xk, count(n, 2, 2))
                pe.wait_ge(c_xc, count(n, 2, 2))
                for h in range(HALVES):
                    for k in range(HALVES):
                        m = mm(bank_c[1 - h][:, :], proj(COLS_C, wc, "fk", k, h), o_sb[:, k, :], k == 0, k == 1)
                    m.then_inc(c_fk, 1)

            def token_major(n, lhs, w, done, freed):
                for b in range(2):
                    pe.wait_ge(freed, count(n, 2, b + 1))
                    for q in (2 * b, 2 * b + 1):
                        for k in range(HALVES):
                            m = mm(bank_c[1 - b][:, (q % 2) * C:(q % 2 + 1) * C], lhs[:, k, q * P:(q + 1) * P],
                                   C_(w, k, C), k == 0, k == 1)
                    m.then_inc(done, 1)

            def c_ffn_gate(n, c):
                pe.wait_ge(c_xr, count(n, 2, 2))
                token_major(n, xr2, "fr", c_fr, c_relu)

            def c_ffn_value(n, c):
                pe.wait_ge(c_kk, count(n, 2, 2))
                token_major(n, kk, "fv", c_fv, c_rr)

            def rounds(na, nb, nc_, c):
                for r in range(ROUNDS):
                    if nb is not None:
                        if r == 0:
                            b_spread(nb, 1 - c, 0)
                        if r + 1 < STEPS:
                            b_spread(nb, 1 - c, r + 1)
                        if r >= 5 and (r - 5) % 4 == 0:
                            b_reduce(nb, 1 - c, (r - 5) // 4)
                    if nc_ is not None:
                        step = {0: c_center, 2: c_variance, 4: c_rstd_spread, 6: c_out_proj, 10: c_transpose,
                                13: c_ffn_key, 14: c_ffn_gate, 15: c_ffn_value}.get(r)
                        if step:
                            step(nc_, c)
                    if na is not None:
                        for step in {3: (a_transpose,), 5: (a_rank1,), 6: (a_rank2_w,), 7: (a_rank2_k,),
                                     8: (a_decay1, a_rank2_v), 9: (a_decay2, a_proj_k), 10: (a_rank2_r,),
                                     11: (a_proj_v, a_rank2_g), 12: (a_proj_r,), 14: (a_headsum,),
                                     15: (a_proj_g,)}.get(r, ()):
                            step(na, c)

            pe.wait_ge(consts_loaded, 16)
            run_slots(pe, rounds)

        @block.scalar
        def _(act):
            act.wait_ge(init_done, 4)

            def shift_row(t, src, done):
                act.copy(t[:, :, :, 0], src).then_inc(done, 1)

            def a_affine(n, c):
                act.wait_ge(states_loaded, count(n, 16, 16))
                act.wait_ge(a_xf, count(n - 1, 10, 10))
                shift_row(xa, states[:, c, :].rearrange("p (h x) -> p h x", h=HALVES)[:, :, HS * ROWS:], a_prev)
                act.wait_ge(wa_valid, count(n, 1, 1))
                for h in range(HALVES):
                    act.wait_ge(a_tr, count(n, 2, h + 1))
                    act.activation(xa[:, h, :, 1:], in_bank_a[f"tr{h}"][:, :].rearrange("p (b t) -> p b t", t=SEQ),
                                   ACT.Identity, bias=A_("ln_b", h, 1), scale=A_("ln_w", h, 1)).then_inc(a_xa, 1)

            def a_tanh(n, c):
                act.wait_ge(a_m, count(n - 1, 10, 10))
                for i in range(2):
                    act.wait_ge(a_T, count(n, 2, i + 1))
                    act.activation(t_mix[:, i, :], in_bank_a[f"t{i}"][:, :], ACT.Tanh).then_inc(a_t, 1)

            def a_decay_tanh(n, c):
                act.wait_ge(a_td1, count(n, 1, 1))
                act.wait_ge(a_td2, count(n - 1, 2, 2))
                act.activation(th[:, :], in_bank_a["td1"][:, :], ACT.Tanh).then_inc(a_th, 1)

            def a_decay_exp(n, c):
                act.wait_ge(b_S, count(n - 2, STEPS, STEPS))
                act.wait_ge(a_w, count(n - 1, 2, 2))
                for h in range(HALVES):
                    act.wait_ge(a_td2, count(n, 2, h + 1))
                    act.activation(e_dec[:, h, :], in_bank_a[f"td2{h}"][:, :], ACT.Exp,
                                   bias=A_("decay", h, 1)).then_inc(a_e, 1)
                for h in range(HALVES):
                    act.wait_ge(a_e, count(n, 2, h + 1))
                    act.activation(w_prev[:, c, h, :].rearrange("p (b t) -> p b t", t=SEQ)[:, :, 1:],
                                   e_dec[:, h, :].rearrange("p (b t) -> p b t", t=SEQ)[:, :, :SEQ - 1],
                                   ACT.Exp, scale=-1.0).then_inc(a_w, 1)

            def a_copy(n, c, name, dst, ready, done, freed, per):
                act.wait_ge(freed, count(n - 2, per, per))
                for h in range(HALVES):
                    act.wait_ge(ready, count(n, 2, h + 1))
                    act.copy(dst[:, c, h, :], in_bank_a[f"{name}{h}"][:, :]).then_inc(done, 1)

            def a_gate(n, c):
                act.wait_ge(a_gate_done, count(n - 1, 2, 2))
                for h in range(HALVES):
                    act.wait_ge(p_g, count(n, 2, h + 1))
                    act.activation(xx[:, h, :], in_bank_a[f"g{h}"][:, :], ACT.Tanh, scale=0.5).then_inc(a_thg, 1)
                    act.activation(z_half[:, h, :], in_bank_a[f"g{h}"][:, :], ACT.Copy, scale=0.5).then_inc(a_z, 1)

            def b_init(n, c, i):
                h, j = divmod(i, HS)
                if i >= 4:
                    act.wait_ge(b_S, count(n, STEPS, i - 3))
                else:
                    act.wait_ge(b_S, count(n - 1, STEPS, STEPS))
                src = states[:, c, h * HALF_STATE + j * ROWS:h * HALF_STATE + (j + 1) * ROWS]
                act.copy(a_in[:, i % 4, :].rearrange("p (b t) -> p b t", t=SEQ)[:, :, 0], src).then_inc(b_s0, 1)

            def c_squares(n, c):
                act.wait_ge(c_tmp, count(n - 1, 2, 2))
                act.wait_ge(c_xr, count(n - 1, 2, 2))
                for h in range(HALVES):
                    act.wait_ge(c_cen, count(n, 2, h + 1))
                    act.activation(c_two[:, h, :], bank_c[h][:, :], ACT.Copy).then_inc(c_yc, 1)
                for h in range(HALVES):
                    act.wait_ge(c_yc, count(n, 2, h + 1))
                    act.activation(sq[:, h, :], c_two[:, h, :], ACT.Square).then_inc(c_sq, 1)

            def c_affine(n, c):
                act.wait_ge(wc_valid, count(n, 1, 1))
                act.wait_ge(c_xr, count(n - 1, 2, 2))
                act.wait_ge(row_loaded, count(n, 16, 16))
                shift_row(xc, row_c[:, :].rearrange("p (h b) -> p h b", h=HALVES), c_prev)
                for h in range(HALVES):
                    act.wait_ge(c_tr, count(n, 2, h + 1))
                    act.activation(xc[:, h, :, 1:], bank_c[1 - h][:, :].rearrange("p (b t) -> p b t", t=SEQ),
                                   ACT.Identity, bias=C_("ln_b", h, 1), scale=C_("ln_w", h, 1)).then_inc(c_xc, 1)

            def c_relu_(n, c):
                act.wait_ge(c_fv, count(n - 1, 2, 2))
                for h in range(HALVES):
                    act.wait_ge(c_fk, count(n, 2, h + 1))
                    act.activation(kk[:, h, :], bank_c[1 - h][:, :], ACT.Relu).then_inc(c_relu, 1)

            def c_sigmoid(n, c):
                act.wait_ge(c_tr, count(n, 2, 2))
                for b in range(2):
                    act.wait_ge(c_fr, count(n, 2, b + 1))
                    act.activation(rr[:, 2 * b:2 * b + 2, :], bank_c[1 - b][:, :].rearrange("p (q c) -> p q c", c=C),
                                   ACT.Tanh, scale=0.5).then_inc(c_rr, 1)

            def rounds(na, nb, nc_, c):
                for r in range(ROUNDS):
                    if nb is not None:
                        if r == 0:
                            act.wait_ge(states_loaded, count(nb, 16, 16))
                            b_init(nb, 1 - c, 0)
                        if r + 1 < STEPS:
                            b_init(nb, 1 - c, r + 1)
                    if nc_ is not None:
                        step = {0: c_squares, 10: c_affine, 13: c_relu_, 14: c_sigmoid}.get(r)
                        if step:
                            step(nc_, c)
                    if na is not None:
                        if r == 3:
                            a_affine(na, c)
                        if r == 5:
                            a_tanh(na, c)
                        if r == 8:
                            a_decay_tanh(na, c)
                        if r == 9:
                            a_decay_exp(na, c)
                            a_copy(na, c, "k", k_sb, p_k, a_k, b_a, STEPS)
                        if r == 11:
                            a_copy(na, c, "v", v_sb, p_v, a_v, b_v, STEPS)
                        if r == 12:
                            a_copy(na, c, "r", r_sb, p_r, a_r, b_rS, STEPS)
                        if r == 15:
                            a_gate(na, c)

            run_slots(act, rounds)

        @block.gpsimd
        def _(pool):
            def rstd(n, mv, veps, rs, mv_sem, veps_sem, rs_sem, used, per):
                pool.wait_ge(mv_sem, count(n, BLK, BLK))
                pool.wait_ge(used, count(n - 1, per, per))
                pool.tensor_tensor(veps[:, :], mv[:, :, 1], eps_t[:, :], ALU.add).then_inc(veps_sem, 1)
                pool.wait_ge(veps_sem, count(n, 1, 1))
                pool.tensor_tensor(rs[:, :], veps[:, :], mhalf[:, :], ALU.pow).then_inc(rs_sem, 1)

            def shift(n, src, dst, ready, prev, done, freed, per, k):
                pool.wait_ge(prev, count(n, 1, 1))
                pool.wait_ge(freed, count(k, per, per))
                for h in range(HALVES):
                    pool.wait_ge(ready, count(n, 2, h + 1))
                    pool.tensor_tensor(dst[:, h, :].rearrange("p (b t) -> p b t", t=SEQ), src[:, h, :, :SEQ],
                                       src[:, h, :, 1:], ALU.subtract).then_inc(done, 1)

            def a_mix_add(n, c, f):
                for h in range(HALVES):
                    o = xf[:, f % 2, h, :].rearrange("p (b t) -> p b t", t=SEQ)
                    pool.wait_ge(a_stt, count(n, 10, 2 * f + h + 1))
                    pool.tensor_tensor(o, o, xa[:, h, :, 1:], ALU.add).then_inc(a_xf, 1)

            def b_product(n, c, i):
                if i == 0:
                    pool.wait_ge(a_r, count(n, 2, 2))
                pool.wait_ge(b_S, count(n, STEPS, i + 1))
                if i % 4 == 0:
                    if i >= 8:
                        pool.wait_ge(b_red, count(n, QUADS, i // 4 - 1))
                    else:
                        pool.wait_ge(b_red, count(n - 1, QUADS, QUADS))
                pool.tensor_tensor(rS[:, i % 8, :], S[:, i % 4, :], r_sb[:, c, i // HS, :], ALU.mult).then_inc(b_rS, 1)

            def c_square_relu(n, c):
                for h in range(HALVES):
                    pool.wait_ge(c_relu, count(n, 2, h + 1))
                    pool.tensor_tensor(kk[:, h, :], kk[:, h, :], kk[:, h, :], ALU.mult).then_inc(c_kk, 1)

            def rounds(na, nb, nc_, c):
                for r in range(ROUNDS):
                    if nb is not None and 1 <= r <= STEPS:
                        b_product(nb, 1 - c, r - 1)
                    if nc_ is not None:
                        if r == 8:
                            rstd(nc_, mv_c, veps_c, rstd_c, c_mv, c_veps, c_rstd, c_xh, BLK)
                        if r == 11:
                            pool.wait_ge(c_o, count(nc_, 2, 2))
                            shift(nc_, xc, c_two, c_xc, c_prev, c_sx, c_xr, 2, nc_ - 1)
                        if r == 14:
                            c_square_relu(nc_, c)
                    if na is not None:
                        if r == 1:
                            rstd(na, mv_a, veps_a, rstd_a, a_mv, a_veps, a_rstd, a_xhat, BLK)
                        if r == 4:
                            shift(na, xa, sx, a_xa, a_prev, a_sx, a_stt, 10, na - 1)
                        for f, at in ((MW, 7), (MK, 8), (MV, 9), (MR, 10), (MG, 12)):
                            if r == at:
                                a_mix_add(na, c, f)

            pool.memset(mhalf[:, :], -0.5).then_inc(init_done, 1)
            pool.memset(eps_t[:, :], EPS).then_inc(init_done, 1)
            pool.memset(w_prev[:, 0, :, :], 0.0).then_inc(init_done, 1)
            pool.memset(w_prev[:, 1, :, :], 0.0).then_inc(init_done, 1)
            pool.wait_ge(init_done, 4)
            run_slots(pool, rounds)

        @block.vector
        def _(dve):
            def stats(n, src, st, mv, st_sem, mv_sem, used):
                dve.wait_ge(used, count(n - 1, BLK, BLK))
                for q in range(BLK):
                    dve.bn_stats(st[:, q, :], src[:, q, :]).then_inc(st_sem, 1)
                dve.wait_ge(st_sem, count(n, BLK + 1, BLK))
                dve.tensor_copy(held[:, :], st[:, BLK - 1, 0:1]).then_inc(st_sem, 1)
                for q in range(BLK):
                    dve.bn_aggr(mv[:, q, :], st[:, q, :]).then_inc(mv_sem, 1)

            def norm(n, src, dst, mv, rs, rs_sem, done):
                dve.wait_ge(rs_sem, count(n, 1, 1))
                for q in range(BLK):
                    dve.tensor_scalar(dst[:, q, :], src[:, q, :], mv[:, q, 0:1], rs[:, q:q + 1], ALU.subtract,
                                      ALU.mult).then_inc(done, 1)

            def a_stats_(n, c):
                dve.wait_ge(x_loaded, count(n, 16, 16))
                stats(n, x_in, stats_a, mv_a, a_stats, a_mv, a_xhat)

            def a_norm(n, c):
                dve.wait_ge(a_gate_done, count(n - 1, 2, 2))
                norm(n, x_in, xhat, mv_a, rstd_a, a_rstd, a_xhat)

            def a_xx_(n, c):
                dve.wait_ge(a_gate_done, count(n - 1, 2, 2))
                for h in range(HALVES):
                    dve.wait_ge(a_sx, count(n, 2, h + 1))
                    dve.scalar_tensor_tensor(xx[:, h, :].rearrange("p (b t) -> p b t", t=SEQ),
                                             sx[:, h, :].rearrange("p (b t) -> p b t", t=SEQ), A_("maa_x", h, 1),
                                             xa[:, h, :, 1:], ALU.mult, ALU.add).then_inc(a_xx, 1)

            def a_mix(n, c, f):
                name = MIX_NAMES[f]
                if f == MV:
                    dve.wait_ge(a_td1, count(n, 1, 1))
                elif f == MR:
                    dve.wait_ge(p_k, count(n, 2, 2))
                elif f == MG:
                    dve.wait_ge(p_v, count(n, 2, 2))
                elif f == MW:
                    dve.wait_ge(p_g, count(n - 1, 2, 2))
                else:
                    dve.wait_ge(p_r, count(n - 1, 2, 2))
                for h in range(HALVES):
                    dve.wait_ge(a_m, count(n, 10, 2 * f + h + 1))
                    dve.scalar_tensor_tensor(xf[:, f % 2, h, :], in_bank_a[f"{name}{h}"][:, :], A_("maa", 2 * f + h, 1),
                                             sx[:, h, :], ALU.add, ALU.mult).then_inc(a_stt, 1)

            def a_ruk_(n, c):
                dve.wait_ge(a_k, count(n, 2, 2))
                dve.wait_ge(a_ds, count(n - 1, 2, 2))
                for h in range(HALVES):
                    dve.wait_ge(a_r, count(n, 2, h + 1))
                    dve.scalar_tensor_tensor(ruk[:, h, :], r_sb[:, c, h, :], A_("u", h, 1), k_sb[:, c, h, :],
                                             ALU.mult, ALU.mult).then_inc(a_ruk, 1)

            def a_bonus_(n, c):
                dve.wait_ge(a_v, count(n, 2, 2))
                dve.wait_ge(b_y, count(n - 2, 2, 2))
                for h in range(HALVES):
                    dve.wait_ge(a_ds, count(n, 2, h + 1))
                    dve.tensor_tensor(bonus[:, c, h, :], in_bank_a[f"ds{h}"][:, :], v_sb[:, c, h, :],
                                      ALU.mult).then_inc(a_bonus, 1)

            def a_gate_(n, c):
                dve.wait_ge(c_o, count(n - 2, 2, 2))
                for h in range(HALVES):
                    dve.wait_ge(a_thg, count(n, 2, h + 1))
                    dve.wait_ge(a_z, count(n, 2, h + 1))
                    dve.scalar_tensor_tensor(gate[:, c, h, :], xx[:, h, :], 1.0, z_half[:, h, :], ALU.add,
                                             ALU.mult).then_inc(a_gate_done, 1)

            def b_outer(n, c, i):
                h = i // HS
                if i == 0:
                    dve.wait_ge(a_k, count(n, 2, 2))
                dve.wait_ge(b_v, count(n, STEPS, i + 1))
                if i >= 4:
                    dve.wait_ge(b_S, count(n, STEPS, i - 3))
                else:
                    dve.wait_ge(b_S, count(n - 1, STEPS, STEPS))
                cut = lambda t, a: t.rearrange("p (b t) -> p b t", t=SEQ)[:, :, a:a + SEQ - 1]
                dve.tensor_tensor(cut(a_in[:, i % 4, :], 1), cut(bank_v[i % 2][:, :], 0), cut(k_sb[:, c, h, :], 0),
                                  ALU.mult).then_inc(b_a, 1)

            def b_scan(n, c, i):
                if i == 0:
                    dve.wait_ge(a_w, count(n, 2, 2))
                dve.wait_ge(b_a, count(n, STEPS, i + 1))
                dve.wait_ge(b_s0, count(n, STEPS, i + 1))
                if i >= 4:
                    dve.wait_ge(b_rS, count(n, STEPS, i - 3))
                else:
                    dve.wait_ge(b_rS, count(n - 1, STEPS, STEPS))
                dve.tensor_tensor_scan(S[:, i % 4, :], w_prev[:, c, i // HS, :], a_in[:, i % 4, :], 0.0,
                                       ALU.mult, ALU.add).then_inc(b_S, 1)

            def b_out(n, c, h):
                dve.wait_ge(b_red, count(n, QUADS, 2 * h + 2))
                dve.wait_ge(a_bonus, count(n, 2, h + 1))
                dve.wait_ge(c_cen, count(n - 1, 2, 2))
                dve.tensor_tensor(y_sb[:, h, :], bank_y[:, :], bonus[:, c, h, :], ALU.add).then_inc(b_y, 1)

            def c_newton(n, c):
                v, y, t = nw[:, 0, :], nw[:, 1, :], nw[:, 2, :]
                dve.wait_ge(c_var, count(n, 1, 1))
                dve.wait_ge(c_R, count(n - 1, 2, 2))
                k = 0

                def then(ins):
                    nonlocal k
                    k += 1
                    ins.then_inc(c_nw, 1)
                    dve.wait_ge(c_nw, count(n, NEWTON, k))

                then(dve.tensor_scalar(v, bank_c[0][:, 0:P], EPS, None, ALU.add))
                then(dve.tensor_scalar(t.bitcast(I32), v.bitcast(I32), 1, None, ALU.logical_shift_right))
                then(dve.tensor_scalar(y.bitcast(I32), t.bitcast(I32), -1.0, float(0x5F3759DF), ALU.mult, ALU.add))
                for _ in range(3):
                    then(dve.tensor_tensor(t, y, y, ALU.mult))
                    then(dve.scalar_tensor_tensor(t, t, -0.5, v, ALU.mult, ALU.mult))
                    then(dve.scalar_tensor_tensor(y, t, 1.5, y, ALU.add, ALU.mult))

            def c_gated(n, c):
                dve.wait_ge(wc_valid, count(n, 1, 1))
                dve.wait_ge(c_fk, count(n - 1, 2, 2))
                for h in range(HALVES):
                    dve.wait_ge(c_R, count(n, 2, h + 1))
                    dve.scalar_tensor_tensor(o_sb[:, h, :], bank_c[1 - h][:, :], C_("gn_w", h, 1), c_two[:, h, :],
                                             ALU.mult, ALU.mult).then_inc(c_o1, 1)
                for h in range(HALVES):
                    dve.wait_ge(c_o1, count(n, 2, h + 1))
                    dve.scalar_tensor_tensor(o_sb[:, h, :], o_sb[:, h, :], C_("gn_b", h, 1), gate[:, c, h, :],
                                             ALU.add, ALU.mult).then_inc(c_o, 1)

            def c_residual(n, c):
                dve.wait_ge(res_loaded, count(n, 16, 16))
                dve.wait_ge(c_out, count(n - 1, 2, 2))
                for b in range(2):
                    dve.wait_ge(c_wo, count(n, 2, b + 1))
                    dve.tensor_tensor(x1[:, 2 * b:2 * b + 2, :], bank_c[1 - b][:, :].rearrange("p (q c) -> p q c", c=C),
                                      x_res[:, 2 * b:2 * b + 2, :], ALU.add).then_inc(c_x1, 1)
                dve.wait_ge(c_x1, count(n, 2, 2))
                stats(n, x1, stats_c, mv_c, c_stats, c_mv, c_xh)

            def c_norm(n, c):
                dve.wait_ge(c_var, count(n, 1, 1))
                norm(n, x1, x1hat, mv_c, rstd_c, c_rstd, c_xh)

            def c_mix(n, c):
                dve.wait_ge(c_fr, count(n - 1, 2, 2))
                dve.wait_ge(c_wo, count(n, 2, 2))
                for dst, w, done in ((o_sb, "mix_k", c_xk), (xr2, "mix_r", c_xr)):
                    for h in range(HALVES):
                        dve.wait_ge(c_sx, count(n, 2, h + 1))
                        dve.scalar_tensor_tensor(dst[:, h, :].rearrange("p (b t) -> p b t", t=SEQ),
                                                 c_two[:, h, :].rearrange("p (b t) -> p b t", t=SEQ), C_(w, h, 1),
                                                 xc[:, h, :, 1:], ALU.mult, ALU.add).then_inc(done, 1)

            def c_output(n, c):
                dve.wait_ge(stored, count(n - 1, 16, 16))
                for b in range(2):
                    dve.wait_ge(c_fv, count(n, 2, b + 1))
                    dve.wait_ge(c_rr, count(n, 2, b + 1))
                    dve.scalar_tensor_tensor(rr[:, 2 * b:2 * b + 2, :], rr[:, 2 * b:2 * b + 2, :], 1.0,
                                             bank_c[1 - b][:, :].rearrange("p (q c) -> p q c", c=C), ALU.add,
                                             ALU.mult).then_inc(c_tmp, 1)
                for b in range(2):
                    dve.wait_ge(c_tmp, count(n, 2, b + 1))
                    dve.scalar_tensor_tensor(o_tile[:, 2 * b:2 * b + 2, :], rr[:, 2 * b:2 * b + 2, :], 0.5,
                                             x1[:, 2 * b:2 * b + 2, :], ALU.mult, ALU.add).then_inc(c_out, 1)

            def rounds(na, nb, nc_, c):
                for r in range(ROUNDS):
                    if nb is not None:
                        if r < STEPS:
                            b_outer(nb, 1 - c, r)
                        if 1 <= r <= STEPS:
                            b_scan(nb, 1 - c, r - 1)
                        if r == 10:
                            b_out(nb, 1 - c, 0)
                    if nc_ is not None:
                        step = {3: c_newton, 5: c_gated, 7: c_residual, 9: c_norm, 12: c_mix, 16: c_output}.get(r)
                        if step:
                            step(nc_, c)
                    if na is not None:
                        if r == 0:
                            a_stats_(na, c)
                        if r == 2:
                            a_norm(na, c)
                        if r == 4:
                            a_xx_(na, c)
                        for f, at in ((MW, 6), (MK, 7), (MV, 8), (MR, 10), (MG, 11)):
                            if r == at:
                                a_mix(na, c, f)
                        if r == 13:
                            a_ruk_(na, c)
                        if r == 14:
                            a_bonus_(na, c)
                        if r == 16:
                            a_gate_(na, c)
                    if nb is not None and r == ROUNDS - 1:
                        b_out(nb, 1 - c, 1)

            dve.wait_ge(init_done, 4)
            run_slots(dve, rounds)


def by_rows(w):
    return np.concatenate([w[k * P:(k + 1) * P] for k in range(w.shape[0] // P)], axis=1)


def vec(*vs):
    return np.concatenate([np.asarray(v).reshape(HALVES, P).T for v in vs], axis=1)


def packed(a, axis):
    return np.take(a, np.concatenate([PACKED + h * P for h in range(HALVES)]), axis=axis)


def stage_a(maa_x, maa, w1, w2, decay, td1, td2, u, wr, wk, wv, wg, ln_w, ln_b, order):
    w1 = w1.reshape(C, NMIX, DM)[:, order]
    rank2 = np.zeros((NMIX, HALVES, P, P), np.float32)
    for f in range(NMIX):
        for h in range(HALVES):
            at = DM * f if f < 4 else 0
            rank2[f, h, at:at + DM] = w2[order[f]][:, h * P:(h + 1) * P]
    td2_rows = np.zeros((P, C), np.float32)
    td2_rows[:DD] = td2
    return np.concatenate([
        by_rows(w1[:, :4].reshape(C, 4 * DM)), by_rows(np.tile(w1[:, 4], (1, 4))),
        rank2.transpose(2, 0, 1, 3).reshape(P, -1), by_rows(np.tile(td1, (1, 2))), td2_rows,
        by_rows(wk.T), by_rows(packed(wv.T, 1)), by_rows(wr.T), by_rows(packed(wg.T, 1)),
        vec(ln_w, ln_b, maa_x, *maa, decay, u.reshape(C)),
    ], axis=1)


def stage_c(wo, fk, fr, fv, gn_w, gn_b, ln_w, ln_b, mix_k, mix_r):
    return np.concatenate([
        by_rows(packed(wo.T, 0)), by_rows(fk.T), by_rows(fr.T), by_rows(fv.T),
        vec(packed(gn_w, 0), packed(gn_b, 0), ln_w, ln_b, mix_k, mix_r),
    ], axis=1)


def constants():
    out = np.zeros((P, COLS_K["total"]), np.float32)
    put = lambda name, i, m: out.__setitem__((slice(None), slice(COLS_K[name][0] + i * m.shape[1],
                                                                 COLS_K[name][0] + (i + 1) * m.shape[1])), m)
    ch = np.arange(P)
    head, col = ch // HS, ch % HS
    p_head, p_col = PACKED // HS, PACKED % HS
    put("ident", 0, np.eye(P, dtype=np.float32))
    for j in range(HS):
        put("spread", j, ((p_head[:, None] == head[None]) & (p_col[:, None] == j)).astype(np.float32))
    for jq in range(2):
        m = np.zeros((P, 32), np.float32)
        m[ch, HPH * jq + head] = 1
        put("gather", jq, m)
    same = (p_head[:, None] == p_head[None]).astype(np.float32)
    put("center", 0, np.eye(P, dtype=np.float32) - same / np.float32(HS))
    put("headsum", 0, (head[:, None] == p_head[None]).astype(np.float32))
    for h in range(HALVES):
        m = np.zeros((P, 32), np.float32)
        m[ch, HPH * h + p_head] = 1 / HS
        put("var", h, m)
        for q in range(BLK):
            m = np.zeros((P, P), np.float32)
            m[32 * q + HPH * h + p_head, ch] = 1
            put("rstd", 4 * h + q, m)
    return out


def kernel(**inputs):
    import concourse.bacc as bacc
    from concourse.bass_utils import run_bass_kernel_spmd

    a = {k: np.asarray(v) for k, v in inputs.items()}
    l0 = {k[len("L0_xattn_"):]: v for k, v in a.items() if k.startswith("L0_xattn_")}
    l1 = {k[len("L1_xattn_"):]: v for k, v in a.items() if k.startswith("L1_xattn_")}
    stack = l0["maa_stack"].reshape(NMIX, C)
    order0 = [1, 0, 2, 3, 4]
    order1 = [0, 1, 2, 3, 4]
    weights_a = np.stack([
        stage_a(l0["maa_x"], [stack[i] for i in order0], l0["maa_w1"], l0["maa_w2"], l0["time_decay"], l0["td_w1"],
                l0["td_w2"], l0["u"], l0["Wr"], l0["Wk"], l0["Wv"], l0["Wg"], l0["ln1_w"], l0["ln1_b"], order0),
        stage_a(l1["maa_x"], [l1["maa_w"], l1["maa_k"], l1["maa_v"], l1["maa_r"], l1["maa_g"]], l1["maa_w1"],
                l1["maa_w2"], l1["time_decay"], l1["decay_w1"], l1["decay_w2"], l1["faaaa"], l1["Wr"], l1["Wk"],
                l1["Wv"], l1["Wg"], l1["ln1_w"], l1["ln1_b"], order1)])
    weights_c = np.stack([
        stage_c(l0["Wo"], l0["Wfk"], l0["Wfr"], l0["Wfv"], l0["gn_w"], l0["gn_b"], l0["ln2_w"], l0["ln2_b"],
                l0["ffn_maa_k"], l0["ffn_maa_r"]),
        stage_c(l1["Wo"], l1["fWk"], l1["fWr"], l1["fWv"], l1["gn_w"], l1["gn_b"], l1["ln2_w"], l1["ln2_b"],
                l1["fmaa_k"], l1["fmaa_r"])])
    ctx = a["ctx_2048"]
    s0 = ctx[:, 2:2 + HS].reshape(TILES, ROWS, HALVES, HPH, HS, HS).transpose(0, 3, 4, 2, 5, 1)
    s0 = s0.reshape(TILES, P, HALVES, HS * ROWS)
    rows = ctx[:, :2].reshape(TILES, ROWS, 2, HALVES, P).transpose(2, 0, 4, 3, 1)
    state = np.concatenate([np.concatenate([s0, rows[1]], axis=3).reshape(TILES, P, HALVES * HALF_STATE),
                            rows[0].reshape(TILES, P, HALVES * ROWS)], axis=2)
    arrays = {
        "x": a["x"].reshape(BATCH * SEQ, C), "state": state, "weights_a": weights_a, "weights_c": weights_c,
        "consts": constants(),
    }
    arrays = {k: np.ascontiguousarray(v) for k, v in arrays.items()}
    nc = bacc.Bacc("TRN2", target_bir_lowering=False, num_devices=1)
    args = [nc.dram_tensor(k, v.shape, F32, kind="ExternalInput").ap() for k, v in arrays.items()]
    out = nc.dram_tensor("out", [BATCH * SEQ, C], F32, kind="ExternalOutput").ap()
    build(nc, *args, out)
    r = run_bass_kernel_spmd(nc, [arrays], core_ids=[0])
    return r.results[0]["out"].reshape(BATCH, SEQ, C)
```

```python
from contextlib import ExitStack

import numpy as np

import concourse.bass as bass
from concourse import mybir

F32 = mybir.dt.float32
I32 = mybir.dt.int32
F32R = mybir.dt.float32r
ALU = mybir.AluOpType
ACT = mybir.ActivationFunctionType

P = 128
BATCH, SEQ, C = 64, 64, 256
HEADS, HS = 32, 8
DM = 32
DD = 64
NMIX = 5
LAYERS = 2
EPS = 1e-5

HALVES = C // P
HPH = HEADS // HALVES
ROWS = 8
TILES = BATCH // ROWS
TOK = ROWS * SEQ
BLK = TOK // P
ITEMS = LAYERS * TILES
STEPS = HALVES * HS
QUADS = STEPS // 4
T_DMAS, V_DMAS = 6, 4
TICKS = 1440

MW, MK, MV, MR, MG = range(NMIX)
MIX_NAMES = ("mw", "mk", "mv", "mr", "mg")


def columns(parts):
    at, out = 0, {}
    for name, n in parts:
        out[name] = (at, at + n)
        at += n
    out["total"] = at
    return out


COLS_A = columns([("w1a", 2 * P), ("w1b", 2 * P), ("td1", 2 * P), ("td2", 2 * P),
                  ("wk", 2 * C), ("wv", 2 * C), ("wr", 2 * C), ("wg", 2 * C),
                  ("ln_w", 2), ("ln_b", 2), ("maa_x", 2), ("maa", 2 * NMIX), ("decay", 2), ("u", 2)])
COLS_C = columns([("wo", 2 * C), ("fk", 2 * C), ("fr", 2 * C), ("fv", 2 * C),
                  ("gn_w", 2), ("gn_b", 2), ("ln_w", 2), ("ln_b", 2), ("mix_k", 2), ("mix_r", 2)])
COLS_K = columns([("ident", P), ("spread", 4 * P), ("gather", 2 * 32), ("center", P), ("headsum", P),
                  ("var", 2 * 32), ("rstd", 8 * P)])
HALF_STATE = HS * ROWS + ROWS
STATE_COLS = HALVES * (HALF_STATE + ROWS)
RANK2_COLS = NMIX * HALVES * P


def packed_channel(pi):
    jj, rest = divmod(pi, 32)
    jq, head = divmod(rest, HPH)
    return head * HS + 4 * jq + jj


PACKED = np.array([packed_channel(pi) for pi in range(P)])


def build(nc, x, state, weights_a, weights_2, weights_c, consts, out):
    rank2_l1 = nc.dram_tensor("rank2_l1", [3 * DM, RANK2_COLS], F32, kind="Internal").ap()
    mid = nc.dram_tensor("layer0_out", [BATCH * SEQ, C], F32, kind="Internal").ap()
    tiled = lambda t: t.rearrange("(g q p) c -> g p q c", p=P, q=BLK)
    x_t, mid_t, out_t = tiled(x), tiled(mid), tiled(out)

    with ExitStack() as ctx:
        def sb(name, shape, dt=F32):
            return ctx.enter_context(nc.sbuf_tensor(name, shape, dt))

        def sem(name):
            return ctx.enter_context(nc.semaphore(name))

        wa = sb("wa", [P, COLS_A["total"]])
        wc = sb("wc", [P, COLS_C["total"]])
        kc = sb("kc", [P, COLS_K["total"]])
        x_in = sb("x_in", [P, BLK, C])
        states = sb("states", [P, 2, HALVES * HALF_STATE])
        stats_a = sb("stats_a", [P, BLK, 6])
        mv_a = sb("mv_a", [P, BLK, 2])
        veps_a = sb("veps_a", [P, BLK])
        rstd_a = sb("rstd_a", [P, BLK])
        mhalf = sb("mhalf", [P, BLK])
        held = sb("held", [P, 1])
        eps_t = sb("eps_t", [P, BLK])
        xhat = sb("xhat", [P, BLK, C])
        z_half = xhat[:, :, :].rearrange("p q c -> p (q c)").rearrange("p (h t) -> p h t", h=2)
        xa = sb("xa", [P, HALVES, ROWS, SEQ + 1])
        sx = sb("sx", [P, HALVES, TOK])
        xx = sb("xx", [P, HALVES, TOK])
        t_mix = sb("t_mix", [P, 2, TOK])
        hi = sb("hi", [P, HALVES, TOK], F32R)
        lo = sb("lo", [P, HALVES, TOK], F32R)
        t_stack = sb("t_stack", [P, NMIX, TOK], F32R)
        v_stack = sb("v_stack", [P, 4, TOK], F32R)
        w2 = sb("w2", [3 * DM, RANK2_COLS], F32R)
        spread = sb("spread", [P, 4 * P], F32R)
        xf = sb("xf", [P, 2, HALVES, TOK])
        th = sb("th", [P, TOK])
        e_dec = sb("e_dec", [P, HALVES, TOK])
        w_prev = sb("w_prev", [P, 2, HALVES, TOK])
        k_sb = sb("k_sb", [P, 2, HALVES, TOK])
        v_sb = sb("v_sb", [P, HALVES, TOK])
        r_sb = sb("r_sb", [P, 2, HALVES, TOK])
        ruk = e_dec
        bonus = sb("bonus", [P, HALVES, TOK])
        gate = sb("gate", [P, 2, HALVES, TOK])
        a_in = sb("a_in", [P, 4, TOK])
        S = sb("S", [P, 4, TOK])
        rS = sb("rS", [P, 8, TOK])
        y_sb = sb("y_sb", [P, HALVES, TOK])
        row_c = sb("row_c", [P, HALVES * ROWS])
        c_one = sb("c_one", [P, 2 * TOK])
        c_two = sb("c_two", [P, HALVES, TOK])
        nw = sb("nw", [P, 3, P])
        o_sb = sb("o_sb", [P, HALVES, TOK])
        x1 = sb("x1", [P, BLK, C])
        xc = sb("xc", [P, HALVES, ROWS, SEQ + 1])
        kk = sb("kk", [P, HALVES, TOK])
        stats_c = sb("stats_c", [P, BLK, 6])
        mv_c = sb("mv_c", [P, BLK, 2])
        veps_c = sb("veps_c", [P, BLK])
        rstd_c = sb("rstd_c", [P, BLK])
        sq = c_one[:, :].rearrange("p (h t) -> p h t", h=2)
        x1hat = c_one[:, :].rearrange("p (q c) -> p q c", c=C)
        rr = x1hat
        xr2 = c_two
        raw_w2 = rS[:, :, :].rearrange("p s t -> p (s t)")
        bank = [ctx.enter_context(nc.psum_tensor(f"bank{i}", [P, TOK], F32)) for i in range(8)]
        bank_a, bank_c, bank_v, bank_y = bank[0:3], bank[3:5], bank[5:7], bank[7]

        def cols(t, table, name, i=0, n=None):
            a, b = table[name]
            return t[:, a + i * n:a + (i + 1) * n] if n else t[:, a:b]

        def A_(name, i=0, n=P):
            return cols(wa, COLS_A, name, i, n)

        def C_(name, i=0, n=P):
            return cols(wc, COLS_C, name, i, n)

        def K_(name, i=0, n=P):
            return cols(kc, COLS_K, name, i, n)

        def proj(table, t, name, k, m):
            a = table[name][0] + k * C + m * P
            return t[:, a:a + P]

        ident = K_("ident")

        consts_loaded = sem("consts_loaded")
        wa_valid, wc_valid = sem("wa_valid"), sem("wc_valid")
        wa_loaded, wc_loaded = sem("wa_loaded"), sem("wc_loaded")
        x_loaded, states_loaded = sem("x_loaded"), sem("states_loaded")
        res_loaded, row_loaded, stored = sem("res_loaded"), sem("row_loaded"), sem("stored")
        raw_loaded, w2_hi, w2_ready, w2_kept = map(sem, ("raw_loaded", "w2_hi", "w2_ready", "w2_kept"))
        spread_ready, init_done = sem("spread_ready"), sem("init_done")
        a_thi, a_tlo, t_wk_stacked, t_vr_stacked, a_vhi, a_vlo, v_stacked = map(
            sem, ("a_thi", "a_tlo", "t_wk_stacked", "t_vr_stacked", "a_vhi", "a_vlo", "v_stacked"))
        a_stats, a_mv, a_veps, a_rstd, a_xhat = map(sem, ("a_stats", "a_mv", "a_veps", "a_rstd", "a_xhat"))
        a_tr, a_prev, a_xa, a_sx, a_xx = map(sem, ("a_tr", "a_prev", "a_xa", "a_sx", "a_xx"))
        a_T, a_t, a_m, a_stt, a_xf = map(sem, ("a_T", "a_t", "a_m", "a_stt", "a_xf"))
        a_td1, a_th, a_td2, a_e, a_w = map(sem, ("a_td1", "a_th", "a_td2", "a_e", "a_w"))
        p_k, p_v, p_r, p_g = map(sem, ("p_k", "p_v", "p_r", "p_g"))
        a_k, a_v, a_r, a_ruk, a_ds, a_bonus = map(sem, ("a_k", "a_v", "a_r", "a_ruk", "a_ds", "a_bonus"))
        a_thg, a_z, a_gate_done = map(sem, ("a_thg", "a_z", "a_gate_done"))
        b_s0, b_v, b_a, b_S, b_rS = map(sem, ("b_s0", "b_v", "b_a", "b_S", "b_rS"))
        b_red, b_y = sem("b_red"), sem("b_y")
        c_cen, c_yc, c_sq, c_var, c_nw = map(sem, ("c_cen", "c_yc", "c_sq", "c_var", "c_nw"))
        c_R, c_o1, c_o, c_wo, c_x1 = map(sem, ("c_R", "c_o1", "c_o", "c_wo", "c_x1"))
        c_stats, c_mv, c_veps, c_rstd, c_xh = map(sem, ("c_stats", "c_mv", "c_veps", "c_rstd", "c_xh"))
        c_tr, c_prev, c_xc, c_sx, c_xk, c_xr = map(sem, ("c_tr", "c_prev", "c_xc", "c_sx", "c_xk", "c_xr"))
        c_fk, c_relu, c_kk, c_fr, c_rr, c_fv, c_tmp, c_out = map(
            sem, ("c_fk", "c_relu", "c_kk", "c_fr", "c_rr", "c_fv", "c_tmp", "c_out"))
        NEWTON = 12

        def count(n, per, k):
            v = n * per + k
            return max(v, 0) if isinstance(v, int) else v

        A_USES = ("tr0", "tr1", "t0", "t1", "mw0", "mw1", "mk0", "mk1", "td1", "mv0", "mv1", "td20", "td21", "k0", "k1",
                  "mr0", "mr1", "v0", "v1", "mg0", "mg1", "r0", "r1", "g0", "g1", "ds0", "ds1")
        assert len(A_USES) % 3 == 0
        in_bank_a = {name: bank_a[u % 3] for u, name in enumerate(A_USES)}

        def run_slots(eng, plan):
            order = sorted(plan, key=lambda row: row[0] % TICKS)

            def slot(items, parity):
                for tick, step, *which in order:
                    n = items[tick // TICKS]
                    if n is not None:
                        step(n, (parity + tick // TICKS) % 2, *which)

            slot((0, None, None), 0)
            slot((1, 0, None), 1)
            slot((2, 1, 0), 0)
            with eng.Fori(0, (ITEMS - 4) // 2) as i:
                s = 2 * i + 3
                slot((s, s - 1, s - 2), 1)
                slot((s + 1, s, s - 1), 0)
            slot((ITEMS - 1, ITEMS - 2, ITEMS - 3), 1)
            slot((None, ITEMS - 1, ITEMS - 2), 0)
            slot((None, None, ITEMS - 1), 1)

        block = ctx.enter_context(nc.Block())

        @block.sync
        def _(sp):
            def words(t):
                return t.bitcast(F32)

            def load_x(n, g, src):
                sp.wait_ge(a_xhat, count(n - 1, BLK, BLK))
                sp.dma_start(x_in[:, :, :], src[g]).then_inc(x_loaded, 16)

            def load_states(n, g, parity):
                sp.wait_ge(b_s0, count(n - 2, STEPS, STEPS))
                sp.wait_ge(a_prev, count(n - 2, 1, 1))
                sp.dma_start(states[:, parity, :], state[g, :, :HALVES * HALF_STATE]).then_inc(states_loaded, 16)

            def stack_t(n):
                sp.wait_ge(a_m, count(n - 1, 10, 10))
                sp.wait_ge(a_thi, count(n, 2, 1))
                for inputs, stacked in (((MW, MK), t_wk_stacked), ((MV, MR), t_vr_stacked)):
                    for f in inputs:
                        rows = slice(DM * f, DM * f + DM)
                        sp.dma_start(words(t_stack[0:DM, f, :]), words(hi[rows, 0, :])).then_inc(stacked, 16)
                        sp.dma_start(words(t_stack[2 * DM:3 * DM, f, :]), words(hi[rows, 0, :])).then_inc(stacked, 16)
                    sp.wait_ge(a_tlo, count(n, 2, 1))
                    for f in inputs:
                        rows = slice(DM * f, DM * f + DM)
                        sp.dma_start(words(t_stack[DM:2 * DM, f, :]), words(lo[rows, 0, :])).then_inc(stacked, 16)

            def stack_v(n):
                sp.wait_ge(b_v, count(n - 1, STEPS, STEPS))
                for part, src, made in ((0, hi, a_vhi), (1, lo, a_vlo)):
                    sp.wait_ge(made, count(n, 2, 2))
                    for pp in range(2):
                        sp.dma_start(words(v_stack[64 * part:64 * part + 64, pp:4:2, :]),
                                     words(src[64 * pp:64 * pp + 64, :, :])).then_inc(v_stacked, 16)

            def load_residual(n, g, src):
                sp.wait_ge(stored, count(n - 1, 16, 16))
                sp.dma_start(x1[:, :, :], src[g]).then_inc(res_loaded, 16)
                sp.wait_ge(c_prev, count(n - 1, 1, 1))
                sp.dma_start(row_c[:, :], state[g, :, HALVES * HALF_STATE:]).then_inc(row_loaded, 16)

            def store(n, g, dst):
                sp.wait_ge(c_out, count(n, 2, 2))
                sp.dma_start(dst[g], x1[:, :, :]).then_inc(stored, 16)

            sp.dma_start(x_in[:, :, :], x_t[0]).then_inc(x_loaded, 16)
            sp.dma_start(kc[:, :], consts).then_inc(consts_loaded, 16)
            sp.dma_start(states[:, 0, :], state[0, :, :HALVES * HALF_STATE]).then_inc(states_loaded, 16)
            sp.dma_start(wa[:, :], weights_a[0]).then_inc(wa_loaded, 16)
            for layer in range(LAYERS):
                sp.dma_start(raw_w2[0:3 * DM, layer * RANK2_COLS:(layer + 1) * RANK2_COLS], weights_2[layer])\
                    .then_inc(raw_loaded, 16)
            sp.dma_start(wc[:, :], weights_c[0]).then_inc(wc_loaded, 16)
            sp.wait_ge(w2_ready, 2)
            sp.dma_start(rank2_l1, words(t_stack[0:3 * DM, :, :].rearrange("p f t -> p (f t)")[:, :RANK2_COLS]))\
                .then_inc(w2_kept, 16)
            sp.wait_ge(wa_loaded, 16)
            sp.sem_inc(wa_valid, TILES)
            sp.wait_ge(wc_loaded, 16)
            sp.sem_inc(wc_valid, TILES)
            sp.wait_ge(w2_kept, 16)

            for s in range(ITEMS + 2):
                n = s + 1
                if n < ITEMS:
                    sp.wait_ge(stored, count(n - TILES, 16, 16))
                    load_x(n, n % TILES, x_t if n < TILES else mid_t)
                if s < ITEMS:
                    stack_t(s)
                    stack_v(s)
                if n < ITEMS:
                    load_states(n, n % TILES, n % 2)
                if n == TILES:
                    sp.wait_ge(a_ds, count(TILES - 1, 2, 2))
                    sp.wait_ge(p_g, count(TILES - 1, 2, 2))
                    sp.dma_start(wa[:, :], weights_a[1]).then_inc(wa_loaded, 16)
                    sp.dma_start(words(w2[:, :]), rank2_l1).then_inc(wa_loaded, 16)
                    sp.wait_ge(wa_loaded, 48)
                    sp.sem_inc(wa_valid, TILES)
                n = s - 2
                if 0 <= n < ITEMS:
                    store(n, n % TILES, mid_t if n < TILES else out_t)
                if n == TILES - 1:
                    sp.wait_ge(c_fv, count(TILES - 1, 2, 2))
                    sp.dma_start(wc[:, :], weights_c[1]).then_inc(wc_loaded, 16)
                    sp.wait_ge(wc_loaded, 32)
                    sp.sem_inc(wc_valid, TILES)
                n = s - 1
                if 0 <= n < ITEMS:
                    load_residual(n, n % TILES, x_t if n < TILES else mid_t)
            sp.wait_ge(stored, 16 * ITEMS)

        @block.tensor
        def _(pe):
            def mm(o, l, r, start=True, stop=True):
                return pe.matmul(o, l, r, start=start, stop=stop, skip_group_check=True)

            def a_transpose(n, c, h):
                if h == 0:
                    pe.wait_ge(a_xhat, count(n, BLK, BLK))
                    pe.wait_ge(a_z, count(n - 1, 2, 2))
                else:
                    pe.wait_ge(a_bonus, count(n - 1, 2, 1))
                for q in range(BLK):
                    m = pe.transpose(in_bank_a[f"tr{h}"][:, q * P:(q + 1) * P], xhat[:, q, h * P:(h + 1) * P], ident)
                m.then_inc(a_tr, 1)

            def a_rank1(n, c, i):
                if i == 0:
                    pe.wait_ge(a_xx, count(n, 2, 2))
                    pe.wait_ge(a_bonus, count(n - 1, 2, 2))
                else:
                    pe.wait_ge(a_xa, count(n, 2, 1))
                for k in range(HALVES):
                    m = mm(in_bank_a[f"t{i}"][:, :], A_(("w1a", "w1b")[i], k), xx[:, k, :], k == 0, k == 1)
                m.then_inc(a_T, 1)

            def a_rank2(n, c, f, h):
                mm(in_bank_a[f"{MIX_NAMES[f]}{h}"][:, :], w2[:, (2 * f + h) * P:(2 * f + h + 1) * P],
                   t_stack[0:3 * DM, f, :])\
                    .then_inc(a_m, 1)

            def a_rank2_w(n, c, h):
                if h == 0:
                    pe.wait_ge(t_wk_stacked, count(n, T_DMAS * 16, T_DMAS * 16))
                    pe.wait_ge(a_xa, count(n, 2, 2))
                else:
                    pe.wait_ge(a_t, count(n, 2, 1))
                a_rank2(n, c, MW, h)

            def a_rank2_k(n, c, h):
                if h == 0:
                    pe.wait_ge(a_t, count(n, 2, 2))
                else:
                    pe.wait_ge(a_stt, count(n, 10, 1))
                a_rank2(n, c, MK, h)

            def a_decay1(n, c):
                pe.wait_ge(a_xf, count(n, 10, 2))
                pe.wait_ge(a_stt, count(n, 10, 2))
                for k in range(HALVES):
                    m = mm(in_bank_a["td1"][:, :], A_("td1", k), xf[:, 0, k, :], k == 0, k == 1)
                m.then_inc(a_td1, 1)

            def a_rank2_v(n, c, h):
                if h == 0:
                    pe.wait_ge(t_vr_stacked, count(n, T_DMAS * 16, T_DMAS * 16))
                pe.wait_ge(a_stt, count(n, 10, 3 + h))
                a_rank2(n, c, MV, h)

            def a_decay2(n, c, h):
                if h == 0:
                    pe.wait_ge(a_th, count(n, 1, 1))
                else:
                    pe.wait_ge(a_stt, count(n, 10, 5))
                mm(in_bank_a[f"td2{h}"][:, :], A_("td2", h), th[:, :]).then_inc(a_td2, 1)

            def a_proj(n, c, f, name, h, done):
                for k in range(HALVES):
                    m = mm(in_bank_a[f"{name}{h}"][:, :], proj(COLS_A, wa, "w" + name, k, h), xf[:, f % 2, k, :],
                           k == 0, k == 1)
                m.then_inc(done, 1)

            def a_proj_k(n, c, h):
                if h == 0:
                    pe.wait_ge(a_xf, count(n, 10, 2 * MK + 2))
                    pe.wait_ge(a_stt, count(n, 10, 6))
                else:
                    pe.wait_ge(a_e, count(n, 2, 1))
                a_proj(n, c, MK, "k", h, p_k)

            def a_rank2_r(n, c, h):
                if h == 0:
                    pe.wait_ge(a_e, count(n, 2, 2))
                else:
                    pe.wait_ge(a_k, count(n, 2, 1))
                a_rank2(n, c, MR, h)

            def a_proj_v(n, c, h):
                if h == 0:
                    pe.wait_ge(a_xf, count(n, 10, 2 * MV + 2))
                    pe.wait_ge(a_k, count(n, 2, 2))
                else:
                    pe.wait_ge(a_stt, count(n, 10, 7))
                a_proj(n, c, MV, "v", h, p_v)

            def a_rank2_g(n, c, h):
                if h == 0:
                    pe.wait_ge(a_tlo, count(n, 2, 2))
                    pe.wait_ge(a_stt, count(n, 10, 8))
                else:
                    pe.wait_ge(a_vhi, count(n, 2, 1))
                a_rank2(n, c, MG, h)

            def a_proj_r(n, c, h):
                if h == 0:
                    pe.wait_ge(a_xf, count(n, 10, 2 * MR + 2))
                    pe.wait_ge(a_vhi, count(n, 2, 2))
                else:
                    pe.wait_ge(a_stt, count(n, 10, 9))
                a_proj(n, c, MR, "r", h, p_r)

            def a_proj_g(n, c, h):
                if h == 0:
                    pe.wait_ge(a_xf, count(n, 10, 2 * MG + 2))
                    pe.wait_ge(a_stt, count(n, 10, 10))
                else:
                    pe.wait_ge(a_r, count(n, 2, 1))
                a_proj(n, c, MG, "g", h, p_g)

            def a_headsum(n, c, h):
                pe.wait_ge(a_ruk, count(n, 2, h + 1))
                if h == 0:
                    pe.wait_ge(a_r, count(n, 2, 2))
                else:
                    pe.wait_ge(a_z, count(n, 2, 1))
                mm(in_bank_a[f"ds{h}"][:, :], K_("headsum"), ruk[:, h, :]).then_inc(a_ds, 1)

            def b_spread(n, c, i):
                h, j = divmod(i, HS)
                jq, jj = divmod(j, 4)
                if i == 0:
                    pe.wait_ge(v_stacked, count(n, V_DMAS * 16, V_DMAS * 16))
                if i >= 2:
                    pe.wait_ge(b_a, count(n, STEPS, i - 1))
                else:
                    pe.wait_ge(b_a, count(n - 1, STEPS, STEPS))
                m = 2 * (jj % 2) + jq
                mm(bank_v[i % 2][:, :], spread[:, m * P:(m + 1) * P], v_stack[:, 2 * h + jj // 2, :]).then_inc(b_v, 1)

            def b_reduce(n, c, q):
                h, jq = divmod(q, 2)
                pe.wait_ge(b_rS, count(n, STEPS, 4 * q + 4))
                if jq == 0:
                    if h == 1:
                        pe.wait_ge(b_y, count(n, 2, 1))
                    else:
                        pe.wait_ge(b_y, count(n - 1, 2, 2))
                for jj in range(4):
                    m = mm(bank_y[32 * jj:32 * jj + 32, :], K_("gather", jq, 32), rS[:, 4 * (q % 2) + jj, :],
                           jq == 0, jq == 1)
                m.then_inc(b_red, 1)

            def c_center(n, c, h):
                pe.wait_ge(b_y, count(n, 2, h + 1))
                pe.wait_ge(c_tmp, count(n - 1, 2, 2))
                mm(bank_c[h][:, :], K_("center"), y_sb[:, h, :]).then_inc(c_cen, 1)

            def c_variance(n, c):
                pe.wait_ge(c_sq, count(n, 2, 2))
                pe.wait_ge(c_yc, count(n, 2, 1))
                for q in range(BLK):
                    for h in range(HALVES):
                        m = mm(bank_c[0][32 * q:32 * q + 32, 0:P], K_("var", h, 32), sq[:, h, q * P:(q + 1) * P],
                               h == 0, h == 1)
                m.then_inc(c_var, 1)

            def c_rstd_spread(n, c, h):
                pe.wait_ge(c_nw, count(n, NEWTON, NEWTON))
                pe.wait_ge(c_yc, count(n, 2, 2))
                for q in range(BLK):
                    m = mm(bank_c[1 - h][:, q * P:(q + 1) * P], K_("rstd", 4 * h + q), nw[:, 1, :])
                m.then_inc(c_R, 1)

            def token_major(b, lhs, w, done):
                for q in (2 * b, 2 * b + 1):
                    for k in range(HALVES):
                        m = mm(bank_c[1 - b][:, (q % 2) * C:(q % 2 + 1) * C], lhs[:, k, q * P:(q + 1) * P],
                               C_(w, k, C), k == 0, k == 1)
                m.then_inc(done, 1)

            def c_out_proj(n, c, b):
                pe.wait_ge(c_o, count(n, 2, 2))
                token_major(b, o_sb, "wo", c_wo)

            def c_transpose(n, c, h):
                pe.wait_ge(c_xh, count(n, BLK, BLK))
                pe.wait_ge(c_x1, count(n, 2, 2))
                for q in range(BLK):
                    m = pe.transpose(bank_c[1 - h][:, q * P:(q + 1) * P], x1hat[:, q, h * P:(h + 1) * P], ident)
                m.then_inc(c_tr, 1)

            def c_ffn_key(n, c, h):
                pe.wait_ge(c_xk, count(n, 2, 2))
                pe.wait_ge(c_xc, count(n, 2, 2))
                for k in range(HALVES):
                    m = mm(bank_c[1 - h][:, :], proj(COLS_C, wc, "fk", k, h), o_sb[:, k, :], k == 0, k == 1)
                m.then_inc(c_fk, 1)

            def c_ffn_gate(n, c, b):
                pe.wait_ge(c_xr, count(n, 2, 2))
                pe.wait_ge(c_relu, count(n, 2, b + 1))
                token_major(b, xr2, "fr", c_fr)

            def c_ffn_value(n, c, b):
                pe.wait_ge(c_kk, count(n, 2, 2))
                pe.wait_ge(c_rr, count(n, 2, b + 1))
                token_major(b, kk, "fv", c_fv)

            plan_pe = (
                (213, a_transpose, 0), (248, a_transpose, 1), (319, a_rank1, 0), (371, a_rank1, 1),
                (474, a_rank2_w, 0), (502, a_rank2_w, 1), (581, a_rank2_k, 0), (589, a_rank2_k, 1),
                (659, a_rank2_v, 0), (663, a_decay1), (726, a_rank2_v, 1), (735, a_decay2, 0), (739, a_decay2, 1),
                (747, a_proj_k, 0), (781, a_proj_k, 1), (845, a_rank2_r, 0), (853, a_rank2_r, 1), (872, a_proj_v, 0),
                (884, a_proj_v, 1), (911, a_rank2_g, 0), (961, a_rank2_g, 1), (1010, a_proj_r, 0),
                (1079, a_proj_r, 1), (1150, a_proj_g, 0), (1410, a_proj_g, 1), (1477, a_headsum, 0),
                (1530, a_headsum, 1),
                *((1349 + 73 * i, b_spread, i) for i in range(STEPS)),
                *((1782 + 307 * i, b_reduce, i) for i in range(QUADS)),
                (2908, c_center, 0), (2915, c_center, 1), (3014, c_variance), (3190, c_rstd_spread, 0),
                (3197, c_rstd_spread, 1), (3277, c_out_proj, 0), (3331, c_out_proj, 1), (3576, c_transpose, 0),
                (3591, c_transpose, 1), (3828, c_ffn_key, 0), (3846, c_ffn_key, 1), (3944, c_ffn_gate, 0),
                (3962, c_ffn_gate, 1), (4057, c_ffn_value, 0), (4090, c_ffn_value, 1),
            )

            pe.wait_ge(consts_loaded, 16)
            pe.wait_ge(spread_ready, 1)
            pe.wait_ge(w2_ready, 2)
            run_slots(pe, plan_pe)

        @block.scalar
        def _(act):
            act.wait_ge(init_done, 4)

            def shift_row(t, src, done):
                act.copy(t[:, :, :, 0], src).then_inc(done, 1)

            def a_shift_row(n, c):
                act.wait_ge(states_loaded, count(n, 16, 16))
                act.wait_ge(a_xf, count(n - 1, 10, 10))
                shift_row(xa, states[:, c, :].rearrange("p (h x) -> p h x", h=HALVES)[:, :, HS * ROWS:], a_prev)

            def a_affine(n, c, h):
                if h == 0:
                    act.wait_ge(wa_valid, count(n, 1, 1))
                    act.wait_ge(a_xf, count(n - 1, 10, 10))
                act.wait_ge(a_tr, count(n, 2, h + 1))
                act.activation(xa[:, h, :, 1:], in_bank_a[f"tr{h}"][:, :].rearrange("p (b t) -> p b t", t=SEQ),
                               ACT.Identity, bias=A_("ln_b", h, 1), scale=A_("ln_w", h, 1)).then_inc(a_xa, 1)

            def a_tanh(n, c, i):
                act.wait_ge(a_tlo, count(n - 1, 2, i + 1))
                act.wait_ge(a_T, count(n, 2, i + 1))
                act.activation(t_mix[:, i, :], in_bank_a[f"t{i}"][:, :], ACT.Tanh).then_inc(a_t, 1)

            def a_ranks_hi(n, c, i):
                act.wait_ge(a_t, count(n, 2, i + 1))
                if i == 0:
                    act.wait_ge(v_stacked, count(n - 1, V_DMAS * 16, V_DMAS * 16))
                    act.copy(hi[:, 0, :], t_mix[:, 0, :]).then_inc(a_thi, 1)
                else:
                    act.wait_ge(a_m, count(n - 1, 10, 10))
                    act.copy(t_stack[0:3 * DM, 4, :], t_mix[0:3 * DM, 1, :]).then_inc(a_thi, 1)

            def a_decay_tanh(n, c):
                act.wait_ge(a_td1, count(n, 1, 1))
                act.wait_ge(a_td2, count(n - 1, 2, 2))
                act.activation(th[:, :], in_bank_a["td1"][:, :], ACT.Tanh).then_inc(a_th, 1)

            def a_decay_exp(n, c, h):
                act.wait_ge(a_ds, count(n - 1, 2, h + 1))
                act.wait_ge(a_td2, count(n, 2, h + 1))
                act.activation(e_dec[:, h, :], in_bank_a[f"td2{h}"][:, :], ACT.Exp,
                               bias=A_("decay", h, 1)).then_inc(a_e, 1)

            def a_decay(n, c, h):
                act.wait_ge(b_S, count(n - 2, STEPS, STEPS))
                act.wait_ge(a_e, count(n, 2, h + 1))
                act.activation(w_prev[:, c, h, :].rearrange("p (b t) -> p b t", t=SEQ)[:, :, 1:],
                               e_dec[:, h, :].rearrange("p (b t) -> p b t", t=SEQ)[:, :, :SEQ - 1],
                               ACT.Exp, scale=-1.0).then_inc(a_w, 1)

            def a_keys(n, c, h):
                act.wait_ge(b_a, count(n - 2, STEPS, STEPS))
                act.wait_ge(a_ruk, count(n - 2, 2, 2))
                act.wait_ge(p_k, count(n, 2, h + 1))
                act.copy(k_sb[:, c, h, :], in_bank_a[f"k{h}"][:, :]).then_inc(a_k, 1)

            def a_values(n, c, h):
                act.wait_ge(a_bonus, count(n - 1, 2, h + 1))
                act.wait_ge(t_wk_stacked, count(n, T_DMAS * 16, T_DMAS * 16))
                act.wait_ge(t_vr_stacked, count(n, T_DMAS * 16, T_DMAS * 16))
                act.wait_ge(p_v, count(n, 2, h + 1))
                act.copy(v_sb[:, h, :], in_bank_a[f"v{h}"][:, :]).then_inc(a_v, 1)
                act.copy(hi[:, h, :], in_bank_a[f"v{h}"][:, :]).then_inc(a_vhi, 1)

            def a_receptances(n, c, h):
                act.wait_ge(b_rS, count(n - 2, STEPS, STEPS))
                act.wait_ge(p_r, count(n, 2, h + 1))
                act.copy(r_sb[:, c, h, :], in_bank_a[f"r{h}"][:, :]).then_inc(a_r, 1)

            def a_gate(n, c, h):
                act.wait_ge(a_gate_done, count(n - 1, 2, 2))
                act.wait_ge(p_g, count(n, 2, h + 1))
                act.activation(xx[:, h, :], in_bank_a[f"g{h}"][:, :], ACT.Tanh, scale=0.5).then_inc(a_thg, 1)
                act.activation(z_half[:, h, :], in_bank_a[f"g{h}"][:, :], ACT.Copy, scale=0.5).then_inc(a_z, 1)

            def b_init(n, c, i):
                h, j = divmod(i, HS)
                if i == 0:
                    act.wait_ge(states_loaded, count(n, 16, 16))
                if i >= 4:
                    act.wait_ge(b_S, count(n, STEPS, i - 3))
                else:
                    act.wait_ge(b_S, count(n - 1, STEPS, STEPS))
                src = states[:, c, h * HALF_STATE + j * ROWS:h * HALF_STATE + (j + 1) * ROWS]
                act.copy(a_in[:, i % 4, :].rearrange("p (b t) -> p b t", t=SEQ)[:, :, 0], src).then_inc(b_s0, 1)

            def c_centred(n, c, h):
                act.wait_ge(c_fr, count(n - 1, 2, 2))
                act.wait_ge(c_cen, count(n, 2, h + 1))
                act.activation(c_two[:, h, :], bank_c[h][:, :], ACT.Copy).then_inc(c_yc, 1)

            def c_squares(n, c, h):
                act.wait_ge(c_tmp, count(n - 1, 2, 2))
                act.wait_ge(c_yc, count(n, 2, h + 1))
                act.activation(sq[:, h, :], c_two[:, h, :], ACT.Square).then_inc(c_sq, 1)

            def c_shift_row(n, c):
                act.wait_ge(c_xr, count(n - 1, 2, 2))
                act.wait_ge(row_loaded, count(n, 16, 16))
                shift_row(xc, row_c[:, :].rearrange("p (h b) -> p h b", h=HALVES), c_prev)

            def c_affine(n, c, h):
                act.wait_ge(c_xr, count(n - 1, 2, 2))
                act.wait_ge(c_tr, count(n, 2, h + 1))
                act.activation(xc[:, h, :, 1:], bank_c[1 - h][:, :].rearrange("p (b t) -> p b t", t=SEQ),
                               ACT.Identity, bias=C_("ln_b", h, 1), scale=C_("ln_w", h, 1)).then_inc(c_xc, 1)

            def c_relu_(n, c, h):
                act.wait_ge(c_fv, count(n - 1, 2, 2))
                act.wait_ge(c_fk, count(n, 2, h + 1))
                act.activation(kk[:, h, :], bank_c[1 - h][:, :], ACT.Relu).then_inc(c_relu, 1)

            def c_sigmoid(n, c, b):
                act.wait_ge(c_tr, count(n, 2, 2))
                act.wait_ge(c_fr, count(n, 2, b + 1))
                act.activation(rr[:, 2 * b:2 * b + 2, :], bank_c[1 - b][:, :].rearrange("p (q c) -> p q c", c=C),
                               ACT.Tanh, scale=0.5).then_inc(c_rr, 1)

            plan_act = (
                (169, a_shift_row), (176, a_affine, 0), (251, a_affine, 1), (263, a_tanh, 0), (306, a_ranks_hi, 0),
                (439, a_tanh, 1), (568, a_ranks_hi, 1), (593, a_decay_tanh), (608, a_decay_exp, 0),
                (637, a_decay_exp, 1), (664, a_keys, 0), (723, a_keys, 1), (807, a_values, 0), (852, a_values, 1),
                (976, a_receptances, 0), (1062, a_decay, 0), (1096, a_decay, 1), (1138, a_receptances, 1),
                (1270, a_gate, 0), (1330, a_gate, 1),
                *((1203 + 81 * i, b_init, i) for i in range(STEPS)),
                (2862, c_centred, 0), (2993, c_squares, 0), (3006, c_centred, 1), (3026, c_squares, 1),
                (3427, c_shift_row), (3479, c_affine, 0), (3560, c_affine, 1), (3790, c_relu_, 0),
                (3795, c_relu_, 1), (3925, c_sigmoid, 0), (4016, c_sigmoid, 1),
            )

            act.wait_ge(consts_loaded, 16)
            act.copy(spread[:, :], K_("spread", 0, 4 * P)).then_inc(spread_ready, 1)
            act.wait_ge(raw_loaded, 32)
            act.copy(w2[:, :], raw_w2[0:3 * DM, 0:RANK2_COLS]).then_inc(w2_hi, 1)
            act.copy(t_stack[0:3 * DM, :, :].rearrange("p f t -> p (f t)")[:, :RANK2_COLS],
                     raw_w2[0:3 * DM, RANK2_COLS:2 * RANK2_COLS]).then_inc(w2_hi, 1)
            act.wait_ge(w2_kept, 16)
            run_slots(act, plan_act)

        @block.gpsimd
        def _(pool):
            def rstd(n, mv, veps, rs, mv_sem, veps_sem, rs_sem, used, per):
                pool.wait_ge(mv_sem, count(n, BLK, BLK))
                pool.wait_ge(used, count(n - 1, per, per))
                pool.tensor_tensor(veps[:, :], mv[:, :, 1], eps_t[:, :], ALU.add).then_inc(veps_sem, 1)
                pool.wait_ge(veps_sem, count(n, 1, 1))
                pool.tensor_tensor(rs[:, :], veps[:, :], mhalf[:, :], ALU.pow).then_inc(rs_sem, 1)

            def a_rstd_(n, c):
                rstd(n, mv_a, veps_a, rstd_a, a_mv, a_veps, a_rstd, a_xhat, BLK)

            def c_rstd_(n, c):
                rstd(n, mv_c, veps_c, rstd_c, c_mv, c_veps, c_rstd, c_xh, BLK)

            def a_shift(n, c, h):
                pool.wait_ge(a_prev, count(n, 1, 1))
                pool.wait_ge(a_stt, count(n - 1, 10, 10))
                pool.wait_ge(a_xa, count(n, 2, h + 1))
                pool.tensor_tensor(sx[:, h, :].rearrange("p (b t) -> p b t", t=SEQ), xa[:, h, :, :SEQ],
                                   xa[:, h, :, 1:], ALU.subtract).then_inc(a_sx, 1)

            def c_shift(n, c, h):
                pool.wait_ge(c_o, count(n, 2, 2))
                pool.wait_ge(c_prev, count(n, 1, 1))
                pool.wait_ge(c_xc, count(n, 2, h + 1))
                pool.tensor_tensor(c_two[:, h, :].rearrange("p (b t) -> p b t", t=SEQ), xc[:, h, :, :SEQ],
                                   xc[:, h, :, 1:], ALU.subtract).then_inc(c_sx, 1)

            def a_mix_add(n, c, f, h):
                o = xf[:, f % 2, h, :].rearrange("p (b t) -> p b t", t=SEQ)
                pool.wait_ge(a_stt, count(n, 10, 2 * f + h + 1))
                pool.tensor_tensor(o, o, xa[:, h, :, 1:], ALU.add).then_inc(a_xf, 1)

            def a_values_lo(n, c, h):
                pool.wait_ge(t_wk_stacked, count(n, T_DMAS * 16, T_DMAS * 16))
                pool.wait_ge(t_vr_stacked, count(n, T_DMAS * 16, T_DMAS * 16))
                pool.wait_ge(a_vhi, count(n, 2, h + 1))
                pool.tensor_tensor(lo[:, h, :], v_sb[:, h, :], hi[:, h, :].bitcast(F32), ALU.subtract).then_inc(a_vlo, 1)

            def b_product(n, c, i):
                if i == 0:
                    pool.wait_ge(a_r, count(n, 2, 2))
                pool.wait_ge(b_S, count(n, STEPS, i + 1))
                if i % 4 == 0:
                    if i >= 8:
                        pool.wait_ge(b_red, count(n, QUADS, i // 4 - 1))
                    else:
                        pool.wait_ge(b_red, count(n - 1, QUADS, QUADS))
                pool.tensor_tensor(rS[:, i % 8, :], S[:, i % 4, :], r_sb[:, c, i // HS, :], ALU.mult).then_inc(b_rS, 1)

            def c_square_relu(n, c, h):
                pool.wait_ge(c_relu, count(n, 2, h + 1))
                pool.tensor_tensor(kk[:, h, :], kk[:, h, :], kk[:, h, :], ALU.mult).then_inc(c_kk, 1)

            plan_pool = (
                (15, a_rstd_), (81, a_shift, 0), (91, a_shift, 1), (553, a_mix_add, MW, 0), (584, a_mix_add, MW, 1),
                (620, a_mix_add, MK, 0), (644, a_mix_add, MK, 1), (696, a_mix_add, MV, 0), (722, a_mix_add, MV, 1),
                (885, a_mix_add, MR, 0), (938, a_mix_add, MR, 1), (959, a_values_lo, 0), (1012, a_values_lo, 1),
                (1053, a_mix_add, MG, 0), (1098, a_mix_add, MG, 1),
                *((1415 + 81 * i, b_product, i) for i in range(STEPS)),
                (3484, c_rstd_), (3592, c_shift, 0), (3659, c_shift, 1), (3865, c_square_relu, 0),
                (3990, c_square_relu, 1),
            )

            pool.memset(mhalf[:, :], -0.5).then_inc(init_done, 1)
            pool.memset(eps_t[:, :], EPS).then_inc(init_done, 1)
            pool.memset(w_prev[:, 0, :, :], 0.0).then_inc(init_done, 1)
            pool.memset(w_prev[:, 1, :, :], 0.0).then_inc(init_done, 1)
            pool.wait_ge(init_done, 4)
            run_slots(pool, plan_pool)

        @block.vector
        def _(dve):
            def stats(n, src, st, mv, st_sem, mv_sem, used):
                dve.wait_ge(used, count(n - 1, BLK, BLK))
                for q in range(BLK):
                    dve.bn_stats(st[:, q, :], src[:, q, :]).then_inc(st_sem, 1)
                dve.wait_ge(st_sem, count(n, BLK + 1, BLK))
                dve.tensor_copy(held[:, :], st[:, BLK - 1, 0:1]).then_inc(st_sem, 1)
                for q in range(BLK):
                    dve.bn_aggr(mv[:, q, :], st[:, q, :]).then_inc(mv_sem, 1)

            def norm(n, src, dst, mv, rs, rs_sem, done):
                dve.wait_ge(rs_sem, count(n, 1, 1))
                for q in range(BLK):
                    dve.tensor_scalar(dst[:, q, :], src[:, q, :], mv[:, q, 0:1], rs[:, q:q + 1], ALU.subtract,
                                      ALU.mult).then_inc(done, 1)

            def a_stats_(n, c):
                dve.wait_ge(x_loaded, count(n, 16, 16))
                stats(n, x_in, stats_a, mv_a, a_stats, a_mv, a_xhat)

            def a_norm(n, c):
                dve.wait_ge(a_gate_done, count(n - 1, 2, 2))
                norm(n, x_in, xhat, mv_a, rstd_a, a_rstd, a_xhat)

            def a_xx_(n, c, h):
                if h == 0:
                    dve.wait_ge(a_gate_done, count(n - 1, 2, 2))
                dve.wait_ge(a_sx, count(n, 2, h + 1))
                dve.scalar_tensor_tensor(xx[:, h, :].rearrange("p (b t) -> p b t", t=SEQ),
                                         sx[:, h, :].rearrange("p (b t) -> p b t", t=SEQ), A_("maa_x", h, 1),
                                         xa[:, h, :, 1:], ALU.mult, ALU.add).then_inc(a_xx, 1)

            def a_ranks_lo(n, c, i):
                dve.wait_ge(a_thi, count(n, 2, i + 1))
                if i == 0:
                    dve.wait_ge(v_stacked, count(n - 1, V_DMAS * 16, V_DMAS * 16))
                    dve.tensor_tensor(lo[:, 0, :], t_mix[:, 0, :], hi[:, 0, :].bitcast(F32), ALU.subtract)\
                        .then_inc(a_tlo, 1)
                else:
                    mid_rows = t_stack[DM:2 * DM, 4, :]
                    dve.tensor_tensor(mid_rows, t_mix[DM:2 * DM, 1, :], mid_rows.bitcast(F32), ALU.subtract)\
                        .then_inc(a_tlo, 1)

            def a_mix(n, c, f, h):
                if h == 0:
                    if f == MV:
                        dve.wait_ge(a_td1, count(n, 1, 1))
                    elif f == MR:
                        dve.wait_ge(p_k, count(n, 2, 2))
                    elif f == MG:
                        dve.wait_ge(p_v, count(n, 2, 2))
                    elif f == MW:
                        dve.wait_ge(p_g, count(n - 1, 2, 2))
                    else:
                        dve.wait_ge(p_r, count(n - 1, 2, 2))
                dve.wait_ge(a_m, count(n, 10, 2 * f + h + 1))
                dve.scalar_tensor_tensor(xf[:, f % 2, h, :], in_bank_a[f"{MIX_NAMES[f]}{h}"][:, :],
                                         A_("maa", 2 * f + h, 1), sx[:, h, :], ALU.add, ALU.mult).then_inc(a_stt, 1)

            def a_ruk_(n, c, h):
                dve.wait_ge(a_k, count(n, 2, h + 1))
                dve.wait_ge(a_w, count(n, 2, h + 1))
                dve.wait_ge(a_r, count(n, 2, h + 1))
                dve.scalar_tensor_tensor(ruk[:, h, :], r_sb[:, c, h, :], A_("u", h, 1), k_sb[:, c, h, :],
                                         ALU.mult, ALU.mult).then_inc(a_ruk, 1)

            def a_bonus_(n, c, h):
                dve.wait_ge(a_v, count(n, 2, h + 1))
                dve.wait_ge(b_y, count(n - 1, 2, h + 1))
                dve.wait_ge(a_ds, count(n, 2, h + 1))
                dve.tensor_tensor(bonus[:, h, :], in_bank_a[f"ds{h}"][:, :], v_sb[:, h, :], ALU.mult)\
                    .then_inc(a_bonus, 1)

            def a_gate_(n, c, h):
                dve.wait_ge(c_o, count(n - 2, 2, 2))
                dve.wait_ge(a_thg, count(n, 2, h + 1))
                dve.wait_ge(a_z, count(n, 2, h + 1))
                dve.scalar_tensor_tensor(gate[:, c, h, :], xx[:, h, :], 1.0, z_half[:, h, :], ALU.add,
                                         ALU.mult).then_inc(a_gate_done, 1)

            def b_outer(n, c, i):
                h = i // HS
                if i == 0:
                    dve.wait_ge(a_k, count(n, 2, 2))
                dve.wait_ge(b_v, count(n, STEPS, i + 1))
                if i >= 4:
                    dve.wait_ge(b_S, count(n, STEPS, i - 3))
                else:
                    dve.wait_ge(b_S, count(n - 1, STEPS, STEPS))
                cut = lambda t, a: t.rearrange("p (b t) -> p b t", t=SEQ)[:, :, a:a + SEQ - 1]
                dve.tensor_tensor(cut(a_in[:, i % 4, :], 1), cut(bank_v[i % 2][:, :], 0), cut(k_sb[:, c, h, :], 0),
                                  ALU.mult).then_inc(b_a, 1)

            def b_scan(n, c, i):
                if i == 0:
                    dve.wait_ge(a_w, count(n, 2, 2))
                dve.wait_ge(b_a, count(n, STEPS, i + 1))
                dve.wait_ge(b_s0, count(n, STEPS, i + 1))
                if i >= 4:
                    dve.wait_ge(b_rS, count(n, STEPS, i - 3))
                else:
                    dve.wait_ge(b_rS, count(n - 1, STEPS, STEPS))
                dve.tensor_tensor_scan(S[:, i % 4, :], w_prev[:, c, i // HS, :], a_in[:, i % 4, :], 0.0,
                                       ALU.mult, ALU.add).then_inc(b_S, 1)

            def b_out(n, c, h):
                dve.wait_ge(b_red, count(n, QUADS, 2 * h + 2))
                dve.wait_ge(a_bonus, count(n, 2, h + 1))
                dve.wait_ge(c_cen, count(n - 1, 2, 2))
                dve.tensor_tensor(y_sb[:, h, :], bank_y[:, :], bonus[:, h, :], ALU.add).then_inc(b_y, 1)

            def c_newton(n, c, k):
                v, y, t = nw[:, 0, :], nw[:, 1, :], nw[:, 2, :]
                if k == 0:
                    dve.wait_ge(c_var, count(n, 1, 1))
                    dve.wait_ge(c_R, count(n - 1, 2, 2))
                    dve.tensor_scalar(v, bank_c[0][:, 0:P], EPS, None, ALU.add).then_inc(c_nw, 1)
                    return
                dve.wait_ge(c_nw, count(n, NEWTON, k))
                if k == 1:
                    dve.tensor_scalar(t.bitcast(I32), v.bitcast(I32), 1, None, ALU.logical_shift_right)\
                        .then_inc(c_nw, 1)
                elif k == 2:
                    dve.tensor_scalar(y.bitcast(I32), t.bitcast(I32), -1.0, float(0x5F3759DF), ALU.mult, ALU.add)\
                        .then_inc(c_nw, 1)
                elif k % 3 == 0:
                    dve.tensor_tensor(t, y, y, ALU.mult).then_inc(c_nw, 1)
                elif k % 3 == 1:
                    dve.scalar_tensor_tensor(t, t, -0.5, v, ALU.mult, ALU.mult).then_inc(c_nw, 1)
                else:
                    dve.scalar_tensor_tensor(y, t, 1.5, y, ALU.add, ALU.mult).then_inc(c_nw, 1)

            def c_scaled(n, c, h):
                if h == 0:
                    dve.wait_ge(wc_valid, count(n, 1, 1))
                    dve.wait_ge(c_fk, count(n - 1, 2, 2))
                dve.wait_ge(c_R, count(n, 2, h + 1))
                dve.scalar_tensor_tensor(o_sb[:, h, :], bank_c[1 - h][:, :], C_("gn_w", h, 1), c_two[:, h, :],
                                         ALU.mult, ALU.mult).then_inc(c_o1, 1)

            def c_gated(n, c, h):
                dve.wait_ge(c_o1, count(n, 2, h + 1))
                dve.scalar_tensor_tensor(o_sb[:, h, :], o_sb[:, h, :], C_("gn_b", h, 1), gate[:, c, h, :],
                                         ALU.add, ALU.mult).then_inc(c_o, 1)

            def c_residual(n, c, b):
                dve.wait_ge(res_loaded, count(n, 16, 16))
                dve.wait_ge(c_wo, count(n, 2, b + 1))
                dve.tensor_tensor(x1[:, 2 * b:2 * b + 2, :], bank_c[1 - b][:, :].rearrange("p (q c) -> p q c", c=C),
                                  x1[:, 2 * b:2 * b + 2, :], ALU.add).then_inc(c_x1, 1)

            def c_stats_(n, c):
                dve.wait_ge(c_x1, count(n, 2, 2))
                stats(n, x1, stats_c, mv_c, c_stats, c_mv, c_xh)

            def c_norm(n, c):
                dve.wait_ge(c_var, count(n, 1, 1))
                norm(n, x1, x1hat, mv_c, rstd_c, c_rstd, c_xh)

            def c_mix_key(n, c, h):
                dve.wait_ge(c_wo, count(n, 2, 2))
                dve.wait_ge(c_sx, count(n, 2, h + 1))
                dve.scalar_tensor_tensor(o_sb[:, h, :].rearrange("p (b t) -> p b t", t=SEQ),
                                         c_two[:, h, :].rearrange("p (b t) -> p b t", t=SEQ), C_("mix_k", h, 1),
                                         xc[:, h, :, 1:], ALU.mult, ALU.add).then_inc(c_xk, 1)

            def c_mix_gate(n, c, h):
                dve.wait_ge(c_xk, count(n, 2, h + 1))
                dve.scalar_tensor_tensor(xr2[:, h, :].rearrange("p (b t) -> p b t", t=SEQ),
                                         c_two[:, h, :].rearrange("p (b t) -> p b t", t=SEQ), C_("mix_r", h, 1),
                                         xc[:, h, :, 1:], ALU.mult, ALU.add).then_inc(c_xr, 1)

            def c_gated_value(n, c, b):
                dve.wait_ge(c_fv, count(n, 2, b + 1))
                dve.wait_ge(c_rr, count(n, 2, b + 1))
                dve.scalar_tensor_tensor(rr[:, 2 * b:2 * b + 2, :], rr[:, 2 * b:2 * b + 2, :], 1.0,
                                         bank_c[1 - b][:, :].rearrange("p (q c) -> p q c", c=C), ALU.add,
                                         ALU.mult).then_inc(c_tmp, 1)

            def c_output(n, c, b):
                dve.wait_ge(c_tmp, count(n, 2, b + 1))
                dve.scalar_tensor_tensor(x1[:, 2 * b:2 * b + 2, :], rr[:, 2 * b:2 * b + 2, :], 0.5,
                                         x1[:, 2 * b:2 * b + 2, :], ALU.mult, ALU.add).then_inc(c_out, 1)

            plan_dve = (
                (30, a_stats_), (98, a_norm), (266, a_xx_, 0), (272, a_xx_, 1), (462, a_ranks_lo, 0),
                (565, a_mix, MW, 0), (569, a_mix, MW, 1), (573, a_mix, MK, 0), (592, a_mix, MK, 1),
                (716, a_mix, MV, 0), (740, a_mix, MV, 1), (773, a_ranks_lo, 1), (892, a_mix, MR, 0),
                (932, a_mix, MR, 1), (971, a_mix, MG, 0), (1119, a_mix, MG, 1), (1171, a_ruk_, 0), (1198, a_ruk_, 1),
                (1375, a_gate_, 0), (1430, a_gate_, 1), (1528, a_bonus_, 0), (1683, a_bonus_, 1),
                *((1326 + 85 * i, b_outer, i) for i in range(STEPS)),
                *((1412 + 82 * i, b_scan, i) for i in range(STEPS)), (2242, b_out, 0), (2693, b_out, 1),
                *((2974 + 11 * i, c_newton, i) for i in range(NEWTON)), (3188, c_scaled, 0), (3230, c_gated, 0),
                (3234, c_scaled, 1), (3240, c_gated, 1), (3416, c_residual, 0), (3433, c_residual, 1),
                (3482, c_stats_), (3536, c_norm), (3804, c_mix_key, 0), (3819, c_mix_key, 1), (3968, c_mix_gate, 0),
                (3997, c_mix_gate, 1), (4094, c_gated_value, 0), (4111, c_output, 0), (4126, c_gated_value, 1),
                (4127, c_output, 1),
            )

            dve.wait_ge(w2_hi, 2)
            dve.tensor_tensor(w2[2 * DM:, :], raw_w2[2 * DM:3 * DM, 0:RANK2_COLS], w2[2 * DM:, :].bitcast(F32),
                              ALU.subtract).then_inc(w2_ready, 1)
            w2_other = t_stack[2 * DM:3 * DM, :, :].rearrange("p f t -> p (f t)")[:, :RANK2_COLS]
            dve.tensor_tensor(w2_other, raw_w2[2 * DM:3 * DM, RANK2_COLS:2 * RANK2_COLS], w2_other.bitcast(F32),
                              ALU.subtract).then_inc(w2_ready, 1)
            dve.wait_ge(init_done, 4)
            run_slots(dve, plan_dve)


def by_rows(w):
    return np.concatenate([w[k * P:(k + 1) * P] for k in range(w.shape[0] // P)], axis=1)


def vec(*vs):
    return np.concatenate([np.asarray(v).reshape(HALVES, P).T for v in vs], axis=1)


def packed(a, axis):
    return np.take(a, np.concatenate([PACKED + h * P for h in range(HALVES)]), axis=axis)


def stage_a(maa_x, maa, w1, decay, td1, td2, u, wr, wk, wv, wg, ln_w, ln_b, order):
    w1 = w1.reshape(C, NMIX, DM)[:, order]
    td2_rows = np.zeros((P, C), np.float32)
    td2_rows[:DD] = td2
    return np.concatenate([
        by_rows(w1[:, :4].reshape(C, 4 * DM)), by_rows(np.tile(w1[:, 4], (1, 4))),
        by_rows(np.tile(td1, (1, 2))), td2_rows,
        by_rows(wk.T), by_rows(packed(wv.T, 1)), by_rows(wr.T), by_rows(packed(wg.T, 1)),
        vec(ln_w, ln_b, maa_x, *maa, decay, u.reshape(C)),
    ], axis=1)


def stage_c(wo, fk, fr, fv, gn_w, gn_b, ln_w, ln_b, mix_k, mix_r):
    return np.concatenate([
        by_rows(packed(wo.T, 0)), by_rows(fk.T), by_rows(fr.T), by_rows(fv.T),
        vec(packed(gn_w, 0), packed(gn_b, 0), ln_w, ln_b, mix_k, mix_r),
    ], axis=1)


def constants():
    out = np.zeros((P, COLS_K["total"]), np.float32)
    put = lambda name, i, m: out.__setitem__((slice(None), slice(COLS_K[name][0] + i * m.shape[1],
                                                                 COLS_K[name][0] + (i + 1) * m.shape[1])), m)
    ch = np.arange(P)
    head = ch // HS
    p_head = PACKED // HS
    put("ident", 0, np.eye(P, dtype=np.float32))
    for m in range(4):
        row = ch % 64
        put("spread", m, ((row[:, None] // HPH == m) & (row[:, None] % HPH == head[None])).astype(np.float32))
    for jq in range(2):
        m = np.zeros((P, 32), np.float32)
        m[ch, HPH * jq + head] = 1
        put("gather", jq, m)
    same = (p_head[:, None] == p_head[None]).astype(np.float32)
    put("center", 0, np.eye(P, dtype=np.float32) - same / np.float32(HS))
    put("headsum", 0, (head[:, None] == p_head[None]).astype(np.float32))
    for h in range(HALVES):
        m = np.zeros((P, 32), np.float32)
        m[ch, HPH * h + p_head] = 1 / HS
        put("var", h, m)
        for q in range(BLK):
            m = np.zeros((P, P), np.float32)
            m[32 * q + HPH * h + p_head, ch] = 1
            put("rstd", 4 * h + q, m)
    return out


def kernel(**inputs):
    import concourse.bacc as bacc
    from concourse.bass_utils import run_bass_kernel_spmd

    a = {k: np.asarray(v) for k, v in inputs.items()}
    l0 = {k[len("L0_xattn_"):]: v for k, v in a.items() if k.startswith("L0_xattn_")}
    l1 = {k[len("L1_xattn_"):]: v for k, v in a.items() if k.startswith("L1_xattn_")}
    stack = l0["maa_stack"].reshape(NMIX, C)
    order0 = [1, 0, 2, 3, 4]
    order1 = [0, 1, 2, 3, 4]
    weights_a = np.stack([
        stage_a(l0["maa_x"], [stack[i] for i in order0], l0["maa_w1"], l0["time_decay"], l0["td_w1"],
                l0["td_w2"], l0["u"], l0["Wr"], l0["Wk"], l0["Wv"], l0["Wg"], l0["ln1_w"], l0["ln1_b"], order0),
        stage_a(l1["maa_x"], [l1["maa_w"], l1["maa_k"], l1["maa_v"], l1["maa_r"], l1["maa_g"]], l1["maa_w1"],
                l1["time_decay"], l1["decay_w1"], l1["decay_w2"], l1["faaaa"], l1["Wr"], l1["Wk"],
                l1["Wv"], l1["Wg"], l1["ln1_w"], l1["ln1_b"], order1)])
    weights_2 = np.stack([np.tile(l["maa_w2"][order].transpose(1, 0, 2).reshape(DM, RANK2_COLS), (3, 1))
                          for l, order in ((l0, order0), (l1, order1))])
    weights_c = np.stack([
        stage_c(l0["Wo"], l0["Wfk"], l0["Wfr"], l0["Wfv"], l0["gn_w"], l0["gn_b"], l0["ln2_w"], l0["ln2_b"],
                l0["ffn_maa_k"], l0["ffn_maa_r"]),
        stage_c(l1["Wo"], l1["fWk"], l1["fWr"], l1["fWv"], l1["gn_w"], l1["gn_b"], l1["ln2_w"], l1["ln2_b"],
                l1["fmaa_k"], l1["fmaa_r"])])
    ctx = a["ctx_2048"]
    s0 = ctx[:, 2:2 + HS].reshape(TILES, ROWS, HALVES, HPH, HS, HS).transpose(0, 3, 4, 2, 5, 1)
    s0 = s0.reshape(TILES, P, HALVES, HS * ROWS)
    rows = ctx[:, :2].reshape(TILES, ROWS, 2, HALVES, P).transpose(2, 0, 4, 3, 1)
    state = np.concatenate([np.concatenate([s0, rows[1]], axis=3).reshape(TILES, P, HALVES * HALF_STATE),
                            rows[0].reshape(TILES, P, HALVES * ROWS)], axis=2)
    arrays = {
        "x": a["x"].reshape(BATCH * SEQ, C), "state": state, "weights_a": weights_a, "weights_2": weights_2, "weights_c": weights_c,
        "consts": constants(),
    }
    arrays = {k: np.ascontiguousarray(v) for k, v in arrays.items()}
    nc = bacc.Bacc("TRN2", target_bir_lowering=False, num_devices=1)
    args = [nc.dram_tensor(k, v.shape, F32, kind="ExternalInput").ap() for k, v in arrays.items()]
    out = nc.dram_tensor("out", [BATCH * SEQ, C], F32, kind="ExternalOutput").ap()
    build(nc, *args, out)
    r = run_bass_kernel_spmd(nc, [arrays], core_ids=[0])
    return r.results[0]["out"].reshape(BATCH, SEQ, C)
```

```python
from contextlib import ExitStack

import numpy as np

import concourse.bass as bass
from concourse import mybir

F32 = mybir.dt.float32
I32 = mybir.dt.int32
F32R = mybir.dt.float32r
ALU = mybir.AluOpType
ACT = mybir.ActivationFunctionType

P = 128
BATCH, SEQ, C = 64, 64, 256
HEADS, HS = 32, 8
DM = 32
NMIX = 5
LAYERS = 2
EPS = 1e-5

HALVES = C // P
HPH = HEADS // HALVES
ROWS = 8
TILES = BATCH // ROWS
TOK = ROWS * SEQ
BLK = TOK // P
ITEMS = LAYERS * TILES
STEPS = HALVES * HS
QUADS = STEPS // 4
T_DMAS, G_DMAS, V_DMAS = 6, 3 * BLK, 4
TICKS = 1440

MW, MK, MV, MR, MG = range(NMIX)
MIX_NAMES = ("mw", "mk", "mv", "mr", "mg")


def columns(parts):
    at, out = 0, {}
    for name, n in parts:
        out[name] = (at, at + n)
        at += n
    out["total"] = at
    return out


COLS_A = columns([("ln_w", 2), ("ln_b", 2), ("maa_x", 2), ("w1a", 2 * P), ("w1b", 2 * DM),
                  ("maa", 2 * NMIX), ("decay", 2), ("u", 2), ("td1", 2 * P),
                  ("wk", 2 * C), ("wv", 2 * C), ("wr", 2 * C), ("wg", 2 * C)])
REST_A, PROJ_A = COLS_A["maa"][0], COLS_A["wk"][0]
COLS_C = columns([("wo", 2 * C), ("fk", 2 * C), ("fr", 2 * C), ("fv", 2 * C),
                  ("gn_w", 2), ("gn_b", 2), ("ln_w", 2), ("ln_b", 2), ("mix_k", 2), ("mix_r", 2)])
COLS_K = columns([("ident", P), ("gather", 2 * 32), ("center", P), ("headsum", P), ("var", 2 * 32)])
COLS_R = columns([("spread", 4 * P), ("rstd", 8 * P)])
HALF_STATE = HS * ROWS + ROWS
STATE_COLS = HALVES * (HALF_STATE + ROWS)
RANK2_COLS = NMIX * HALVES * P


def packed_channel(pi):
    jj, rest = divmod(pi, 32)
    jq, head = divmod(rest, HPH)
    return head * HS + 4 * jq + jj


PACKED = np.array([packed_channel(pi) for pi in range(P)])


def build(nc, x, state, weights_a, weights_2, decay_2, weights_c, consts,
          consts_r, out):
    decay2_l1 = nc.dram_tensor("decay2_l1", [P, 2 * C], F32, kind="Internal").ap()
    rank2_l1 = nc.dram_tensor("rank2_l1", [3 * DM, RANK2_COLS], F32, kind="Internal").ap()
    mid = nc.dram_tensor("layer0_out", [BATCH * SEQ, C], F32, kind="Internal").ap()
    tiled = lambda t: t.rearrange("(g q p) c -> g p q c", p=P, q=BLK)
    x_t, mid_t, out_t = tiled(x), tiled(mid), tiled(out)

    with ExitStack() as ctx:
        def sb(name, shape, dt=F32):
            return ctx.enter_context(nc.sbuf_tensor(name, shape, dt))

        def sem(name):
            return ctx.enter_context(nc.semaphore(name))

        wa = sb("wa", [P, COLS_A["total"]])
        wc = sb("wc", [P, COLS_C["total"]])
        kc = sb("kc", [P, COLS_K["total"]])
        x_in = sb("x_in", [P, BLK, C])
        states = sb("states", [P, 2, HALVES * HALF_STATE])
        stats_a = sb("stats_a", [P, BLK, 6])
        mv_a = sb("mv_a", [P, BLK, 2])
        veps_a = sb("veps_a", [P, BLK])
        rstd_a = sb("rstd_a", [P, BLK])
        shift_a = sb("shift_a", [P, BLK])
        mhalf = sb("mhalf", [P, BLK])
        held = sb("held", [P, 1])
        eps_t = sb("eps_t", [P, BLK])
        xhat = sb("xhat", [P, BLK, C])
        xa = sb("xa", [P, HALVES, ROWS, SEQ + 1])
        sx = sb("sx", [P, HALVES, TOK])
        xx = sb("xx", [P, HALVES, TOK])
        t_mix = sb("t_mix", [P, TOK])
        t_mix_g = sb("t_mix_g", [P, P])
        hi = sb("hi", [P, HALVES, TOK], F32R)
        lo = sb("lo", [P, HALVES, TOK], F32R)
        hi_g = sb("hi_g", [P, P], F32R)
        lo_g = sb("lo_g", [P, P], F32R)
        t_stack = sb("t_stack", [P, NMIX, TOK], F32R)
        v_stack = sb("v_stack", [P, 4, TOK], F32R)
        w2 = sb("w2", [3 * DM, RANK2_COLS], F32R)
        wd = sb("wd", [P, 2 * C], F32R)
        kr = sb("kr", [P, COLS_R["total"]], F32R)
        xf = sb("xf", [P, 2, HALVES, TOK])
        th = sb("th", [P, TOK])
        th_parts = sb("th_parts", [P, TOK], F32R)
        e_dec = sb("e_dec", [P, HALVES, TOK])
        w_prev = sb("w_prev", [P, 2, HALVES, TOK])
        k_sb = sb("k_sb", [P, 2, HALVES, TOK])
        v_sb = sb("v_sb", [P, HALVES, TOK])
        r_sb = sb("r_sb", [P, 2, HALVES, TOK])
        ruk = e_dec
        bonus = sb("bonus", [P, HALVES, TOK])
        z_half = sb("z_half", [P, TOK])
        gate = sb("gate", [P, 2, HALVES, TOK])
        a_in = sb("a_in", [P, 4, TOK])
        S = sb("S", [P, 4, TOK])
        rS = sb("rS", [P, 8, TOK])
        y_sb = sb("y_sb", [P, HALVES, TOK])
        row_c = sb("row_c", [P, HALVES * ROWS])
        row_a = sb("row_a", [P, HALVES * ROWS])
        c_one = sb("c_one", [P, 2 * TOK])
        c_two = sb("c_two", [P, HALVES, TOK])
        nw = sb("nw", [P, 3, P])
        rstd_parts = sb("rstd_parts", [P, 2, P], F32R)
        o_sb = sb("o_sb", [P, HALVES, TOK])
        x1 = sb("x1", [P, BLK, C])
        xc = sb("xc", [P, HALVES, ROWS, SEQ + 1])
        kk = sb("kk", [P, HALVES, TOK])
        stats_c = sb("stats_c", [P, BLK, 6])
        mv_c = sb("mv_c", [P, BLK, 2])
        veps_c = sb("veps_c", [P, BLK])
        rstd_c = sb("rstd_c", [P, BLK])
        shift_c = sb("shift_c", [P, BLK])
        sq = c_one[:, :].rearrange("p (h t) -> p h t", h=2)
        x1hat = c_one[:, :].rearrange("p (q c) -> p q c", c=C)
        rr = x1hat
        xr2 = c_two
        raw = rS[:, :, :].rearrange("p s t -> p (s t)")
        raw_w2 = [raw[0:3 * DM, layer * RANK2_COLS:(layer + 1) * RANK2_COLS] for layer in range(LAYERS)]
        raw_kr = raw[:, LAYERS * RANK2_COLS:]
        assert raw_kr.shape[1] == COLS_R["total"]
        raw_wd = S[:, :, :].rearrange("p s t -> p (s t)")
        other = v_stack[:, :, :].rearrange("p f t -> p (f t)")
        w2_other, wd_other = other[0:3 * DM, :RANK2_COLS], other[:, RANK2_COLS:RANK2_COLS + 2 * C]
        bank = [ctx.enter_context(nc.psum_tensor(f"bank{i}", [P, TOK], F32)) for i in range(8)]
        bank_a, bank_c, bank_v, bank_y = bank[0:3], bank[3:5], bank[5:7], bank[7]

        def cols(t, table, name, i=0, n=None):
            a, b = table[name]
            return t[:, a + i * n:a + (i + 1) * n] if n else t[:, a:b]

        def A_(name, i=0, n=P):
            return cols(wa, COLS_A, name, i, n)

        def C_(name, i=0, n=P):
            return cols(wc, COLS_C, name, i, n)

        def K_(name, i=0, n=P):
            return cols(kc, COLS_K, name, i, n)

        def proj(table, t, name, k, m):
            a = table[name][0] + k * C + m * P
            return t[:, a:a + P]

        def R_(name, i=0, n=P):
            return cols(kr, COLS_R, name, i, n)

        ident = K_("ident")

        consts_loaded = sem("consts_loaded")
        wa_valid, wc_valid = sem("wa_valid"), sem("wc_valid")
        wa_loaded, wc_loaded = sem("wa_loaded"), sem("wc_loaded")
        x_loaded, states_loaded = sem("x_loaded"), sem("states_loaded")
        res_loaded, row_loaded, stored = sem("res_loaded"), sem("row_loaded"), sem("stored")
        row_a_loaded = sem("row_a_loaded")
        wa_front_valid, wa_front_loaded = sem("wa_front_valid"), sem("wa_front_loaded")
        wa_proj_valid, wa_proj_loaded = sem("wa_proj_valid"), sem("wa_proj_loaded")
        raw0_loaded, raw1_loaded, raw_kr_loaded = map(sem, ("raw0_loaded", "raw1_loaded", "raw_kr_loaded"))
        w2_hi, w2_ready, w2_kept, kr_ready, init_done = map(
            sem, ("w2_hi", "w2_ready", "w2_kept", "kr_ready", "init_done"))
        raw_wd_loaded, wd_hi, wd_ready, wd_kept = map(sem, ("raw_wd_loaded", "wd_hi", "wd_ready", "wd_kept"))
        a_thp = sem("a_thp")
        a_thi, a_tlo, t_wk_stacked, t_vr_stacked, t_g_stacked, a_vhi, a_vlo, v_stacked = map(
            sem, ("a_thi", "a_tlo", "t_wk_stacked", "t_vr_stacked", "t_g_stacked", "a_vhi", "a_vlo", "v_stacked"))
        a_stats, a_mv, a_veps, a_rstd, a_shift, a_xhat = map(
            sem, ("a_stats", "a_mv", "a_veps", "a_rstd", "a_shift", "a_xhat"))
        a_tr, a_prev, a_xa, a_sx, a_xx = map(sem, ("a_tr", "a_prev", "a_xa", "a_sx", "a_xx"))
        a_T, a_t, a_m, a_stt, a_xf = map(sem, ("a_T", "a_t", "a_m", "a_stt", "a_xf"))
        a_td1, a_th, a_td2, a_e, a_w = map(sem, ("a_td1", "a_th", "a_td2", "a_e", "a_w"))
        p_k, p_v, p_r, p_g = map(sem, ("p_k", "p_v", "p_r", "p_g"))
        a_k, a_v, a_r, a_ruk, a_ds, a_bonus = map(sem, ("a_k", "a_v", "a_r", "a_ruk", "a_ds", "a_bonus"))
        a_thg, a_z, a_gate_done = map(sem, ("a_thg", "a_z", "a_gate_done"))
        b_s0, b_v, b_a, b_S, b_rS = map(sem, ("b_s0", "b_v", "b_a", "b_S", "b_rS"))
        b_red, b_y = sem("b_red"), sem("b_y")
        c_cen, c_yc, c_sq, c_var, c_nw = map(sem, ("c_cen", "c_yc", "c_sq", "c_var", "c_nw"))
        c_R, c_o1, c_o, c_wo, c_x1 = map(sem, ("c_R", "c_o1", "c_o", "c_wo", "c_x1"))
        c_stats, c_mv, c_veps, c_rstd, c_shift, c_xh = map(
            sem, ("c_stats", "c_mv", "c_veps", "c_rstd", "c_shift", "c_xh"))
        c_tr, c_prev, c_xc, c_sx, c_xk, c_xr = map(sem, ("c_tr", "c_prev", "c_xc", "c_sx", "c_xk", "c_xr"))
        c_fk, c_relu, c_kk, c_fr, c_rr, c_fv, c_tmp, c_out = map(
            sem, ("c_fk", "c_relu", "c_kk", "c_fr", "c_rr", "c_fv", "c_tmp", "c_out"))
        NEWTON = 14

        def count(n, per, k):
            v = n * per + k
            return max(v, 0) if isinstance(v, int) else v

        A_USES = ("mw0", "mw1", "mk0", "mk1", "td1", "mv0", "mv1", "td20", "td21", "k0", "k1", "mr0", "mr1", "v0", "v1",
                  "mg0", "mg1", "tr0", "tr1", "r0", "r1", "t0", "t1", "g0", "g1", "ds0", "ds1")
        assert len(A_USES) % 3 == 0
        in_bank_a = {name: bank_a[u % 3] for u, name in enumerate(A_USES)}

        def has_next(n):
            return not isinstance(n, int) or n + 1 < ITEMS

        def run_slots(eng, plan, opening=()):
            def slot(items, parity, opening=()):
                for tick, step, *which in sorted(plan + opening, key=lambda row: row[0] % TICKS):
                    n = items[tick // TICKS]
                    if n is not None:
                        step(n, (parity + tick // TICKS) % 2, *which)

            slot((0, None, None, None), 0, opening)
            slot((1, 0, None, None), 1)
            slot((2, 1, 0, None), 0)
            slot((3, 2, 1, 0), 1)
            with eng.Fori(0, (ITEMS - 4) // 2) as i:
                s = 2 * i + 4
                slot((s, s - 1, s - 2, s - 3), 0)
                slot((s + 1, s, s - 1, s - 2), 1)
            slot((None, ITEMS - 1, ITEMS - 2, ITEMS - 3), 0)
            slot((None, None, ITEMS - 1, ITEMS - 2), 1)
            slot((None, None, None, ITEMS - 1), 0)

        block = ctx.enter_context(nc.Block())

        @block.sync
        def _(sp):
            def words(t):
                return t.bitcast(F32)

            def load_x(n, g, src):
                sp.wait_ge(a_xhat, count(n - 1, BLK, BLK))
                sp.dma_start(x_in[:, :, :], src[g]).then_inc(x_loaded, 16)

            def load_states(n, g, parity):
                sp.wait_ge(b_s0, count(n - 2, STEPS, STEPS))
                sp.dma_start(states[:, parity, :], state[g, :, :HALVES * HALF_STATE]).then_inc(states_loaded, 16)

            def load_row_a(n, g):
                sp.wait_ge(a_prev, count(n - 1, 1, 1))
                for h in range(HALVES):
                    sp.dma_start(row_a[:, h * ROWS:(h + 1) * ROWS],
                                 state[g, :, (h + 1) * HALF_STATE - ROWS:(h + 1) * HALF_STATE]).then_inc(row_a_loaded, 16)

            def stack_t(n):
                sp.wait_ge(a_m, count(n - 1, 10, 10))
                sp.wait_ge(a_thi, count(n, 2, 1))
                for inputs, stacked in (((MW, MK), t_wk_stacked), ((MV, MR), t_vr_stacked)):
                    for f in inputs:
                        rows = slice(DM * f, DM * f + DM)
                        sp.dma_start(words(t_stack[0:DM, f, :]), words(hi[rows, 0, :])).then_inc(stacked, 16)
                        sp.dma_start(words(t_stack[2 * DM:3 * DM, f, :]), words(hi[rows, 0, :])).then_inc(stacked, 16)
                    sp.wait_ge(a_tlo, count(n, 2, 1))
                    for f in inputs:
                        rows = slice(DM * f, DM * f + DM)
                        sp.dma_start(words(t_stack[DM:2 * DM, f, :]), words(lo[rows, 0, :])).then_inc(stacked, 16)
                sp.wait_ge(a_thi, count(n, 2, 2))
                for q in range(BLK):
                    rows, tokens = slice(DM * q, DM * q + DM), slice(P * q, P * q + P)
                    for to in (0, 2 * DM):
                        sp.dma_start(words(t_stack[to:to + DM, MG, tokens]), words(hi_g[rows, :])).then_inc(t_g_stacked, 16)
                sp.wait_ge(a_tlo, count(n, 2, 2))
                for q in range(BLK):
                    rows, tokens = slice(DM * q, DM * q + DM), slice(P * q, P * q + P)
                    sp.dma_start(words(t_stack[DM:2 * DM, MG, tokens]), words(lo_g[rows, :])).then_inc(t_g_stacked, 16)

            def stack_v(n):
                sp.wait_ge(b_v, count(n - 1, STEPS, STEPS))
                for part, src, made in ((0, hi, a_vhi), (1, lo, a_vlo)):
                    sp.wait_ge(made, count(n, 2, 2))
                    for pp in range(2):
                        sp.dma_start(words(v_stack[64 * part:64 * part + 64, pp:4:2, :]),
                                     words(src[64 * pp:64 * pp + 64, :, :])).then_inc(v_stacked, 16)

            def load_residual(n, g, src):
                sp.wait_ge(stored, count(n - 1, 16, 16))
                sp.dma_start(x1[:, :, :], src[g]).then_inc(res_loaded, 16)
                sp.wait_ge(c_prev, count(n - 1, 1, 1))
                sp.dma_start(row_c[:, :], state[g, :, HALVES * HALF_STATE:]).then_inc(row_loaded, 16)

            def store(n, g, dst):
                sp.wait_ge(c_out, count(n, 2, 2))
                sp.dma_start(dst[g], x1[:, :, :]).then_inc(stored, 16)

            sp.dma_start(x_in[:, :, :], x_t[0]).then_inc(x_loaded, 16)
            sp.dma_start(kc[:, :], consts).then_inc(consts_loaded, 16)
            load_row_a(0, 0)
            sp.dma_start(wa[:, :REST_A], weights_a[0, :, :REST_A]).then_inc(wa_front_loaded, 16)
            sp.dma_start(wa[:, REST_A:PROJ_A], weights_a[0, :, REST_A:PROJ_A]).then_inc(wa_loaded, 16)
            sp.dma_start(raw_w2[0], weights_2[0]).then_inc(raw0_loaded, 16)
            sp.dma_start(raw_wd[:, :LAYERS * 2 * C], decay_2).then_inc(raw_wd_loaded, 16)
            sp.dma_start(wa[:, PROJ_A:], weights_a[0, :, PROJ_A:]).then_inc(wa_proj_loaded, 16)
            sp.dma_start(raw_w2[1], weights_2[1]).then_inc(raw1_loaded, 16)
            sp.dma_start(raw_kr, consts_r).then_inc(raw_kr_loaded, 16)
            sp.dma_start(wc[:, :], weights_c[0]).then_inc(wc_loaded, 16)
            sp.wait_ge(wa_front_loaded, 16)
            sp.sem_inc(wa_front_valid, TILES)
            sp.wait_ge(wa_loaded, 16)
            sp.sem_inc(wa_valid, TILES)
            sp.wait_ge(wa_proj_loaded, 16)
            sp.sem_inc(wa_proj_valid, TILES)
            load_x(1, 1, x_t)
            load_row_a(1, 1)
            load_residual(0, 0, x_t)
            load_states(0, 0, 0)
            sp.wait_ge(w2_ready, 2)
            sp.dma_start(rank2_l1, words(w2_other)).then_inc(w2_kept, 16)
            sp.wait_ge(wd_ready, 2)
            sp.dma_start(decay2_l1, words(wd_other)).then_inc(wd_kept, 16)
            stack_t(0)
            sp.wait_ge(wc_loaded, 16)
            sp.sem_inc(wc_valid, TILES)
            sp.wait_ge(w2_kept, 16)
            sp.wait_ge(wd_kept, 16)

            for s in range(ITEMS + 3):
                n = s + 1
                if 1 < n < ITEMS:
                    sp.wait_ge(stored, count(n - TILES, 16, 16))
                    load_x(n, n % TILES, x_t if n < TILES else mid_t)
                    load_row_a(n, n % TILES)
                if 0 < s < ITEMS:
                    stack_t(s)
                n = s - 3
                if 0 <= n < ITEMS:
                    store(n, n % TILES, mid_t if n < TILES else out_t)
                if n == TILES - 1:
                    sp.wait_ge(c_fv, count(TILES - 1, 2, 2))
                    sp.dma_start(wc[:, :], weights_c[1]).then_inc(wc_loaded, 16)
                    sp.wait_ge(wc_loaded, 32)
                    sp.sem_inc(wc_valid, TILES)
                n = s - 2
                if 0 < n < ITEMS:
                    load_residual(n, n % TILES, x_t if n < TILES else mid_t)
                if s < ITEMS:
                    stack_v(s)
                if 0 < s < ITEMS:
                    load_states(s, s % TILES, s % 2)
                if s == TILES - 1:
                    sp.wait_ge(a_T, count(s, 2, 2))
                    sp.dma_start(wa[:, :REST_A], weights_a[1, :, :REST_A]).then_inc(wa_front_loaded, 16)
                    sp.wait_ge(wa_front_loaded, 32)
                    sp.sem_inc(wa_front_valid, TILES)
                    sp.wait_ge(a_ruk, count(s, 2, 2))
                    sp.wait_ge(a_m, count(s, 10, 10))
                    sp.wait_ge(a_e, count(s, 2, 2))
                    sp.wait_ge(a_stt, count(s, 10, 10))
                    sp.dma_start(wa[:, REST_A:PROJ_A], weights_a[1, :, REST_A:PROJ_A]).then_inc(wa_loaded, 16)
                    sp.dma_start(words(w2[:, :]), rank2_l1).then_inc(wa_loaded, 16)
                    sp.dma_start(words(wd[:, :]), decay2_l1).then_inc(wa_loaded, 16)
                    sp.wait_ge(p_g, count(s, 2, 2))
                    sp.dma_start(wa[:, PROJ_A:], weights_a[1, :, PROJ_A:]).then_inc(wa_proj_loaded, 16)
                    sp.wait_ge(wa_loaded, 64)
                    sp.sem_inc(wa_valid, TILES)
                    sp.wait_ge(wa_proj_loaded, 32)
                    sp.sem_inc(wa_proj_valid, TILES)
            sp.wait_ge(stored, 16 * ITEMS)

        @block.tensor
        def _(pe):
            def mm(o, l, r, start=True, stop=True):
                return pe.matmul(o, l, r, start=start, stop=stop, skip_group_check=True)

            def a_transpose(n, c, h):
                if h == 0:
                    pe.wait_ge(a_xhat, count(n, BLK, BLK))
                    pe.wait_ge(a_vhi, count(n - 1, 2, 2))
                    pe.wait_ge(a_v, count(n - 1, 2, 2))
                else:
                    pe.wait_ge(a_stt, count(n - 1, 10, 9))
                for q in range(BLK):
                    m = pe.transpose(in_bank_a[f"tr{h}"][:, q * P:(q + 1) * P], xhat[:, q, h * P:(h + 1) * P], ident)
                m.then_inc(a_tr, 1)

            def a_rank1(n, c, i):
                if i == 0:
                    pe.wait_ge(a_xx, count(n, 2, 2))
                    pe.wait_ge(a_xa, count(n, 2, 2))
                else:
                    pe.wait_ge(a_r, count(n - 1, 2, 1))
                for k in range(HALVES):
                    if i == 0:
                        m = mm(in_bank_a["t0"][:, :], A_("w1a", k), xx[:, k, :], k == 0, k == 1)
                    else:
                        for q in range(BLK):
                            m = mm(in_bank_a["t1"][DM * q:DM * q + DM, 0:P], A_("w1b", k, DM),
                                   xx[:, k, q * P:(q + 1) * P], k == 0, k == 1)
                m.then_inc(a_T, 1)

            def a_rank2(n, c, f, h):
                mm(in_bank_a[f"{MIX_NAMES[f]}{h}"][:, :], w2[:, (2 * f + h) * P:(2 * f + h + 1) * P],
                   t_stack[0:3 * DM, f, :])\
                    .then_inc(a_m, 1)

            def a_rank2_w(n, c, h):
                pe.wait_ge(a_t, count(n, 2, h + 1))
                if h == 0:
                    pe.wait_ge(wa_valid, count(n, 1, 1))
                    pe.wait_ge(w2_ready, 1)
                    pe.wait_ge(t_wk_stacked, count(n, T_DMAS * 16, T_DMAS * 16))
                    pe.wait_ge(a_z, count(n - 1, 2, 2))
                else:
                    pe.wait_ge(a_bonus, count(n - 1, 2, 1))
                a_rank2(n, c, MW, h)

            def a_rank2_k(n, c, h):
                if h == 0:
                    pe.wait_ge(a_bonus, count(n - 1, 2, 2))
                else:
                    pe.wait_ge(a_stt, count(n, 10, 1))
                a_rank2(n, c, MK, h)

            def a_decay1(n, c):
                pe.wait_ge(a_xf, count(n, 10, 2))
                pe.wait_ge(a_stt, count(n, 10, 2))
                for k in range(HALVES):
                    m = mm(in_bank_a["td1"][:, :], A_("td1", k), xf[:, 0, k, :], k == 0, k == 1)
                m.then_inc(a_td1, 1)

            def a_rank2_v(n, c, h):
                if h == 0:
                    pe.wait_ge(t_vr_stacked, count(n, T_DMAS * 16, T_DMAS * 16))
                pe.wait_ge(a_stt, count(n, 10, 3 + h))
                a_rank2(n, c, MV, h)

            def a_decay2(n, c, h):
                if h == 0:
                    pe.wait_ge(wd_ready, 1)
                    pe.wait_ge(a_thp, count(n, 2, 2))
                else:
                    pe.wait_ge(a_stt, count(n, 10, 5))
                for part in range(2):
                    m = mm(in_bank_a[f"td2{h}"][:, :], wd[:, part * C + h * P:part * C + (h + 1) * P],
                           th_parts[:, :], part == 0, part == 1)
                m.then_inc(a_td2, 1)

            def a_proj(n, c, f, name, h, done):
                for k in range(HALVES):
                    m = mm(in_bank_a[f"{name}{h}"][:, :], proj(COLS_A, wa, "w" + name, k, h), xf[:, f % 2, k, :],
                           k == 0, k == 1)
                m.then_inc(done, 1)

            def a_proj_k(n, c, h):
                if h == 0:
                    pe.wait_ge(wa_proj_valid, count(n, 1, 1))
                    pe.wait_ge(a_xf, count(n, 10, 2 * MK + 2))
                    pe.wait_ge(a_stt, count(n, 10, 6))
                else:
                    pe.wait_ge(a_e, count(n, 2, 1))
                a_proj(n, c, MK, "k", h, p_k)

            def a_rank2_r(n, c, h):
                if h == 0:
                    pe.wait_ge(a_e, count(n, 2, 2))
                else:
                    pe.wait_ge(a_k, count(n, 2, 1))
                a_rank2(n, c, MR, h)

            def a_proj_v(n, c, h):
                if h == 0:
                    pe.wait_ge(a_xf, count(n, 10, 2 * MV + 2))
                    pe.wait_ge(a_k, count(n, 2, 2))
                else:
                    pe.wait_ge(a_stt, count(n, 10, 7))
                a_proj(n, c, MV, "v", h, p_v)

            def a_rank2_g(n, c, h):
                if h == 0:
                    pe.wait_ge(t_g_stacked, count(n, G_DMAS * 16, G_DMAS * 16))
                    pe.wait_ge(a_stt, count(n, 10, 8))
                else:
                    pe.wait_ge(a_vhi, count(n, 2, 1))
                a_rank2(n, c, MG, h)

            def a_proj_r(n, c, h):
                if h == 0:
                    pe.wait_ge(a_xf, count(n, 10, 2 * MR + 2))
                    pe.wait_ge(a_stt, count(n, 10, 10))
                elif has_next(n):
                    pe.wait_ge(a_xa, count(n + 1, 2, 1))
                a_proj(n, c, MR, "r", h, p_r)

            def a_proj_g(n, c, h):
                if h == 0:
                    pe.wait_ge(a_xf, count(n, 10, 2 * MG + 2))
                    pe.wait_ge(a_r, count(n, 2, 2))
                elif has_next(n):
                    pe.wait_ge(a_t, count(n + 1, 2, 1))
                a_proj(n, c, MG, "g", h, p_g)

            def a_headsum(n, c, h):
                pe.wait_ge(a_ruk, count(n, 2, h + 1))
                if h == 1:
                    pe.wait_ge(a_z, count(n, 2, 1))
                elif has_next(n):
                    pe.wait_ge(a_t, count(n + 1, 2, 2))
                mm(in_bank_a[f"ds{h}"][:, :], K_("headsum"), ruk[:, h, :]).then_inc(a_ds, 1)

            def b_spread(n, c, i):
                h, j = divmod(i, HS)
                jq, jj = divmod(j, 4)
                if i == 0:
                    pe.wait_ge(kr_ready, 1)
                    pe.wait_ge(v_stacked, count(n, V_DMAS * 16, V_DMAS * 16))
                if i >= 2:
                    pe.wait_ge(b_a, count(n, STEPS, i - 1))
                else:
                    pe.wait_ge(b_a, count(n - 1, STEPS, STEPS))
                m = 2 * (jj % 2) + jq
                mm(bank_v[i % 2][:, :], R_("spread", m), v_stack[:, 2 * h + jj // 2, :]).then_inc(b_v, 1)

            def b_reduce(n, c, q):
                h, jq = divmod(q, 2)
                pe.wait_ge(b_rS, count(n, STEPS, 4 * q + 4))
                if jq == 0:
                    if h == 1:
                        pe.wait_ge(b_y, count(n, 2, 1))
                    else:
                        pe.wait_ge(b_y, count(n - 1, 2, 2))
                for jj in range(4):
                    m = mm(bank_y[32 * jj:32 * jj + 32, :], K_("gather", jq, 32), rS[:, 4 * (q % 2) + jj, :],
                           jq == 0, jq == 1)
                m.then_inc(b_red, 1)

            def c_center(n, c, h):
                pe.wait_ge(b_y, count(n, 2, h + 1))
                pe.wait_ge(c_tmp, count(n - 1, 2, 2))
                mm(bank_c[h][:, :], K_("center"), y_sb[:, h, :]).then_inc(c_cen, 1)

            def c_variance(n, c):
                pe.wait_ge(c_sq, count(n, 2, 2))
                pe.wait_ge(c_yc, count(n, 2, 1))
                for q in range(BLK):
                    for h in range(HALVES):
                        m = mm(bank_c[0][32 * q:32 * q + 32, 0:P], K_("var", h, 32), sq[:, h, q * P:(q + 1) * P],
                               h == 0, h == 1)
                m.then_inc(c_var, 1)

            def c_rstd_spread(n, c, h):
                pe.wait_ge(c_nw, count(n, NEWTON, NEWTON))
                pe.wait_ge(c_yc, count(n, 2, 2))
                for q in range(BLK):
                    for part in range(2):
                        m = mm(bank_c[1 - h][:, q * P:(q + 1) * P], R_("rstd", 4 * h + q), rstd_parts[:, part, :],
                               part == 0, part == 1)
                m.then_inc(c_R, 1)

            def token_major(b, lhs, w, done):
                for q in (2 * b, 2 * b + 1):
                    for k in range(HALVES):
                        m = mm(bank_c[1 - b][:, (q % 2) * C:(q % 2 + 1) * C], lhs[:, k, q * P:(q + 1) * P],
                               C_(w, k, C), k == 0, k == 1)
                m.then_inc(done, 1)

            def c_out_proj(n, c, b):
                pe.wait_ge(c_o, count(n, 2, 2))
                token_major(b, o_sb, "wo", c_wo)

            def c_transpose(n, c, h):
                pe.wait_ge(c_xh, count(n, BLK, BLK))
                pe.wait_ge(c_x1, count(n, 2, 2))
                for q in range(BLK):
                    m = pe.transpose(bank_c[1 - h][:, q * P:(q + 1) * P], x1hat[:, q, h * P:(h + 1) * P], ident)
                m.then_inc(c_tr, 1)

            def c_ffn_key(n, c, h):
                pe.wait_ge(c_xk, count(n, 2, 2))
                pe.wait_ge(c_xc, count(n, 2, 2))
                for k in range(HALVES):
                    m = mm(bank_c[1 - h][:, :], proj(COLS_C, wc, "fk", k, h), o_sb[:, k, :], k == 0, k == 1)
                m.then_inc(c_fk, 1)

            def c_ffn_gate(n, c, b):
                pe.wait_ge(c_xr, count(n, 2, 2))
                pe.wait_ge(c_relu, count(n, 2, b + 1))
                token_major(b, xr2, "fr", c_fr)

            def c_ffn_value(n, c, b):
                pe.wait_ge(c_kk, count(n, 2, 2))
                pe.wait_ge(c_rr, count(n, 2, b + 1))
                token_major(b, kk, "fv", c_fv)

            plan_pe = (
                (245, a_transpose, 0), (291, a_transpose, 1), (584, a_rank1, 0), (755, a_rank1, 1),
                (926, a_rank2_w, 0), (928, a_rank2_w, 1), (971, a_rank2_k, 0), (973, a_rank2_k, 1), (1050, a_decay1),
                (1063, a_rank2_v, 0), (1222, a_rank2_v, 1), (1234, a_decay2, 0), (1255, a_decay2, 1),
                (1362, a_proj_k, 0), (1407, a_proj_k, 1), (1483, a_rank2_r, 0), (1508, a_rank2_r, 1),
                (1534, a_proj_v, 0), (1584, a_proj_v, 1), (1590, a_rank2_g, 0), (1614, a_rank2_g, 1),
                (1680, a_proj_r, 0), (1885, a_proj_r, 1), (2009, a_proj_g, 0), (2142, a_proj_g, 1),
                (2227, a_headsum, 0), (2238, a_headsum, 1),
                *((1815 + 50 * i, b_spread, i) for i in range(STEPS)),
                *((2199 + 386 * i, b_reduce, i) for i in range(QUADS)),
                (3964, c_center, 0), (4000, c_center, 1), (4215, c_variance), (4527, c_rstd_spread, 0),
                (4535, c_rstd_spread, 1), (4661, c_out_proj, 0), (4699, c_out_proj, 1), (4992, c_transpose, 0),
                (5005, c_transpose, 1), (5122, c_ffn_key, 0), (5163, c_ffn_key, 1), (5173, c_ffn_gate, 0),
                (5279, c_ffn_gate, 1), (5306, c_ffn_value, 0), (5334, c_ffn_value, 1),
            )

            pe.wait_ge(consts_loaded, 16)
            run_slots(pe, plan_pe)

        @block.scalar
        def _(act):
            act.wait_ge(init_done, 4)

            def shift_row(t, src, done):
                act.copy(t[:, :, :, 0], src).then_inc(done, 1)

            def norm(n, src, dst, rs, shift, ready, done):
                act.wait_ge(ready, count(n, 1, 1))
                for q in range(BLK):
                    act.activation(dst[:, q, :], src[:, q, :], ACT.Identity, bias=shift[:, q:q + 1],
                                   scale=rs[:, q:q + 1]).then_inc(done, 1)

            def a_norm(n, c):
                act.wait_ge(a_tr, count(n - 1, 2, 2))
                norm(n, x_in, xhat, rstd_a, shift_a, a_shift, a_xhat)

            def c_norm(n, c):
                act.wait_ge(c_var, count(n, 1, 1))
                norm(n, x1, x1hat, rstd_c, shift_c, c_shift, c_xh)

            def a_shift_row(n, c):
                act.wait_ge(row_a_loaded, count(n, 32, 32))
                act.wait_ge(a_xf, count(n - 1, 10, 10))
                shift_row(xa, row_a[:, :].rearrange("p (h b) -> p h b", h=HALVES), a_prev)

            def a_affine(n, c, h):
                if h == 0:
                    act.wait_ge(wa_front_valid, count(n, 1, 1))
                    act.wait_ge(a_xf, count(n - 1, 10, 10))
                act.wait_ge(a_tr, count(n, 2, h + 1))
                act.activation(xa[:, h, :, 1:], in_bank_a[f"tr{h}"][:, :].rearrange("p (b t) -> p b t", t=SEQ),
                               ACT.Identity, bias=A_("ln_b", h, 1), scale=A_("ln_w", h, 1)).then_inc(a_xa, 1)

            def a_tanh(n, c, i):
                act.wait_ge(a_tlo, count(n - 1, 2, i + 1))
                act.wait_ge(a_T, count(n, 2, i + 1))
                if i == 0:
                    act.activation(t_mix[:, :], in_bank_a["t0"][:, :], ACT.Tanh).then_inc(a_t, 1)
                else:
                    act.activation(t_mix_g[:, :], in_bank_a["t1"][:, 0:P], ACT.Tanh).then_inc(a_t, 1)

            def a_ranks_hi(n, c, i):
                act.wait_ge(a_t, count(n, 2, i + 1))
                if i == 0:
                    act.wait_ge(v_stacked, count(n - 1, V_DMAS * 16, V_DMAS * 16))
                    act.copy(hi[:, 0, :], t_mix[:, :]).then_inc(a_thi, 1)
                else:
                    act.wait_ge(t_g_stacked, count(n - 1, G_DMAS * 16, G_DMAS * 16))
                    act.copy(hi_g[:, :], t_mix_g[:, :]).then_inc(a_thi, 1)

            def a_decay_tanh(n, c):
                act.wait_ge(a_td1, count(n, 1, 1))
                act.wait_ge(a_thp, count(n - 1, 2, 2))
                act.activation(th[:, :], in_bank_a["td1"][:, :], ACT.Tanh).then_inc(a_th, 1)

            def a_decay_hi(n, c):
                act.wait_ge(a_td2, count(n - 1, 2, 2))
                act.wait_ge(a_th, count(n, 1, 1))
                act.copy(th_parts[:, :], th[:, :]).then_inc(a_thp, 1)

            def a_decay_exp(n, c, h):
                act.wait_ge(a_ds, count(n - 1, 2, h + 1))
                act.wait_ge(a_td2, count(n, 2, h + 1))
                act.activation(e_dec[:, h, :], in_bank_a[f"td2{h}"][:, :], ACT.Exp,
                               bias=A_("decay", h, 1)).then_inc(a_e, 1)

            def a_decay(n, c, h):
                act.wait_ge(b_S, count(n - 2, STEPS, STEPS))
                act.wait_ge(a_e, count(n, 2, h + 1))
                act.activation(w_prev[:, c, h, :].rearrange("p (b t) -> p b t", t=SEQ)[:, :, 1:],
                               e_dec[:, h, :].rearrange("p (b t) -> p b t", t=SEQ)[:, :, :SEQ - 1],
                               ACT.Exp, scale=-1.0).then_inc(a_w, 1)

            def a_keys(n, c, h):
                act.wait_ge(b_a, count(n - 2, STEPS, STEPS))
                act.wait_ge(a_ruk, count(n - 2, 2, 2))
                act.wait_ge(p_k, count(n, 2, h + 1))
                act.copy(k_sb[:, c, h, :], in_bank_a[f"k{h}"][:, :]).then_inc(a_k, 1)

            def a_values(n, c, h):
                act.wait_ge(a_bonus, count(n - 1, 2, h + 1))
                act.wait_ge(t_wk_stacked, count(n, T_DMAS * 16, T_DMAS * 16))
                act.wait_ge(t_vr_stacked, count(n, T_DMAS * 16, T_DMAS * 16))
                act.wait_ge(p_v, count(n, 2, h + 1))
                act.copy(v_sb[:, h, :], in_bank_a[f"v{h}"][:, :]).then_inc(a_v, 1)
                act.copy(hi[:, h, :], in_bank_a[f"v{h}"][:, :]).then_inc(a_vhi, 1)

            def a_receptances(n, c, h):
                act.wait_ge(b_rS, count(n - 2, STEPS, STEPS))
                act.wait_ge(p_r, count(n, 2, h + 1))
                act.copy(r_sb[:, c, h, :], in_bank_a[f"r{h}"][:, :]).then_inc(a_r, 1)

            def a_gate(n, c, h):
                act.wait_ge(c_o, count(n - 2, 2, 2))
                act.wait_ge(p_g, count(n, 2, h + 1))
                act.activation(gate[:, c, h, :], in_bank_a[f"g{h}"][:, :], ACT.Tanh, scale=0.5).then_inc(a_thg, 1)
                if h == 0:
                    act.wait_ge(a_gate_done, count(n - 1, 2, 2))
                else:
                    act.wait_ge(a_gate_done, count(n, 2, 1))
                act.activation(z_half[:, :], in_bank_a[f"g{h}"][:, :], ACT.Copy, scale=0.5).then_inc(a_z, 1)

            def b_init(n, c, i):
                h, j = divmod(i, HS)
                if i == 0:
                    act.wait_ge(states_loaded, count(n, 16, 16))
                if i >= 4:
                    act.wait_ge(b_S, count(n, STEPS, i - 3))
                else:
                    act.wait_ge(b_S, count(n - 1, STEPS, STEPS))
                src = states[:, c, h * HALF_STATE + j * ROWS:h * HALF_STATE + (j + 1) * ROWS]
                act.copy(a_in[:, i % 4, :].rearrange("p (b t) -> p b t", t=SEQ)[:, :, 0], src).then_inc(b_s0, 1)

            def c_centred(n, c, h):
                act.wait_ge(c_fr, count(n - 1, 2, 2))
                act.wait_ge(c_cen, count(n, 2, h + 1))
                act.activation(c_two[:, h, :], bank_c[h][:, :], ACT.Copy).then_inc(c_yc, 1)

            def c_squares(n, c, h):
                act.wait_ge(c_out, count(n - 1, 2, 2))
                act.wait_ge(c_yc, count(n, 2, h + 1))
                act.activation(sq[:, h, :], c_two[:, h, :], ACT.Square).then_inc(c_sq, 1)

            def c_shift_row(n, c):
                act.wait_ge(c_xr, count(n - 1, 2, 2))
                act.wait_ge(row_loaded, count(n, 16, 16))
                shift_row(xc, row_c[:, :].rearrange("p (h b) -> p h b", h=HALVES), c_prev)

            def c_affine(n, c, h):
                act.wait_ge(c_xr, count(n - 1, 2, 2))
                act.wait_ge(c_tr, count(n, 2, h + 1))
                act.activation(xc[:, h, :, 1:], bank_c[1 - h][:, :].rearrange("p (b t) -> p b t", t=SEQ),
                               ACT.Identity, bias=C_("ln_b", h, 1), scale=C_("ln_w", h, 1)).then_inc(c_xc, 1)

            def c_relu_(n, c, h):
                act.wait_ge(c_fv, count(n - 1, 2, 2))
                act.wait_ge(c_fk, count(n, 2, h + 1))
                act.activation(kk[:, h, :], bank_c[1 - h][:, :], ACT.Relu).then_inc(c_relu, 1)

            def c_sigmoid(n, c, b):
                act.wait_ge(c_tr, count(n, 2, 2))
                act.wait_ge(c_fr, count(n, 2, b + 1))
                act.activation(rr[:, 2 * b:2 * b + 2, :], bank_c[1 - b][:, :].rearrange("p (q c) -> p q c", c=C),
                               ACT.Tanh, scale=0.5).then_inc(c_rr, 1)

            plan_act = (
                (191, a_norm), (369, a_shift_row), (408, a_affine, 0), (423, a_affine, 1), (696, a_tanh, 0),
                (777, a_ranks_hi, 0), (827, a_tanh, 1), (1020, a_ranks_hi, 1), (1164, a_decay_tanh),
                (1201, a_decay_hi), (1380, a_decay_exp, 0), (1383, a_decay_exp, 1), (1384, a_keys, 0),
                (1524, a_keys, 1), (1535, a_values, 0), (1567, a_values, 1), (1589, a_decay, 0), (1640, a_decay, 1),
                (1649, a_receptances, 0), (2050, a_receptances, 1), (2122, a_gate, 0), (2282, a_gate, 1),
                *((1879 + 58 * i, b_init, i) for i in range(STEPS)),
                (4089, c_centred, 0), (4191, c_centred, 1), (4192, c_squares, 0), (4198, c_squares, 1),
                (4871, c_shift_row), (5001, c_norm), (5030, c_affine, 0), (5056, c_affine, 1), (5203, c_relu_, 0),
                (5237, c_relu_, 1), (5317, c_sigmoid, 0), (5343, c_sigmoid, 1),
            )

            def rank2_hi(n, c):
                act.wait_ge(raw0_loaded, 16)
                act.copy(w2[:, :], raw_w2[0]).then_inc(w2_hi, 1)

            def rank2_l1_hi(n, c):
                act.wait_ge(raw1_loaded, 16)
                act.copy(w2_other, raw_w2[1]).then_inc(w2_hi, 1)

            def constants_r(n, c):
                act.wait_ge(raw_kr_loaded, 16)
                act.copy(kr[:, :], raw_kr).then_inc(kr_ready, 1)

            def decay2_hi(n, c):
                act.wait_ge(raw_wd_loaded, 16)
                act.copy(wd[:, :], raw_wd[:, :2 * C]).then_inc(wd_hi, 1)
                act.copy(wd_other, raw_wd[:, 2 * C:LAYERS * 2 * C]).then_inc(wd_hi, 1)

            opening_act = ((1325, constants_r), (278, rank2_hi), (450, rank2_l1_hi), (594, decay2_hi))
            run_slots(act, plan_act, opening_act)

        @block.gpsimd
        def _(pool):
            def rstd(n, mv, veps, rs, mv_sem, veps_sem, rs_sem, used, per):
                pool.wait_ge(mv_sem, count(n, BLK, BLK))
                pool.wait_ge(used, count(n - 1, per, per))
                pool.tensor_tensor(veps[:, :], mv[:, :, 1], eps_t[:, :], ALU.add).then_inc(veps_sem, 1)
                pool.wait_ge(veps_sem, count(n, 1, 1))
                pool.tensor_tensor(rs[:, :], veps[:, :], mhalf[:, :], ALU.pow).then_inc(rs_sem, 1)

            def a_rstd_(n, c):
                rstd(n, mv_a, veps_a, rstd_a, a_mv, a_veps, a_rstd, a_xhat, BLK)

            def c_rstd_(n, c):
                rstd(n, mv_c, veps_c, rstd_c, c_mv, c_veps, c_rstd, c_xh, BLK)

            def a_before(n, c, h):
                pool.wait_ge(a_prev, count(n, 1, 1))
                pool.wait_ge(a_stt, count(n - 1, 10, 10))
                pool.wait_ge(a_xa, count(n, 2, h + 1))
                pool.tensor_tensor(sx[:, h, :].rearrange("p (b t) -> p b t", t=SEQ), xa[:, h, :, :SEQ],
                                   xa[:, h, :, 1:], ALU.subtract).then_inc(a_sx, 1)

            def c_before(n, c, h):
                pool.wait_ge(c_o, count(n, 2, 2))
                pool.wait_ge(c_prev, count(n, 1, 1))
                pool.wait_ge(c_xc, count(n, 2, h + 1))
                pool.tensor_tensor(c_two[:, h, :].rearrange("p (b t) -> p b t", t=SEQ), xc[:, h, :, :SEQ],
                                   xc[:, h, :, 1:], ALU.subtract).then_inc(c_sx, 1)

            def a_mix_add(n, c, f, h):
                o = xf[:, f % 2, h, :].rearrange("p (b t) -> p b t", t=SEQ)
                pool.wait_ge(a_stt, count(n, 10, 2 * f + h + 1))
                pool.tensor_tensor(o, o, xa[:, h, :, 1:], ALU.add).then_inc(a_xf, 1)

            def a_values_lo(n, c, h):
                pool.wait_ge(t_wk_stacked, count(n, T_DMAS * 16, T_DMAS * 16))
                pool.wait_ge(t_vr_stacked, count(n, T_DMAS * 16, T_DMAS * 16))
                pool.wait_ge(a_vhi, count(n, 2, h + 1))
                pool.tensor_tensor(lo[:, h, :], v_sb[:, h, :], hi[:, h, :].bitcast(F32), ALU.subtract).then_inc(a_vlo, 1)

            def b_product(n, c, i):
                if i == 0:
                    pool.wait_ge(kr_ready, 1)
                    pool.wait_ge(w2_ready, 2)
                    pool.wait_ge(a_r, count(n, 2, 2))
                pool.wait_ge(b_S, count(n, STEPS, i + 1))
                if i % 4 == 0:
                    if i >= 8:
                        pool.wait_ge(b_red, count(n, QUADS, i // 4 - 1))
                    else:
                        pool.wait_ge(b_red, count(n - 1, QUADS, QUADS))
                pool.tensor_tensor(rS[:, i % 8, :], S[:, i % 4, :], r_sb[:, c, i // HS, :], ALU.mult).then_inc(b_rS, 1)

            def c_square_relu(n, c, h):
                pool.wait_ge(c_relu, count(n, 2, h + 1))
                pool.tensor_tensor(kk[:, h, :], kk[:, h, :], kk[:, h, :], ALU.mult).then_inc(c_kk, 1)

            plan_pool = (
                (37, a_rstd_), (265, a_before, 0), (315, a_before, 1), (1033, a_mix_add, MW, 0),
                (1046, a_mix_add, MW, 1), (1108, a_mix_add, MK, 0), (1119, a_mix_add, MK, 1),
                (1174, a_mix_add, MV, 0), (1446, a_mix_add, MV, 1), (1479, a_mix_add, MR, 0),
                (1506, a_mix_add, MR, 1), (1554, a_values_lo, 0), (1577, a_values_lo, 1), (1609, a_mix_add, MG, 0),
                (1616, a_mix_add, MG, 1),
                *((1785 + 75 * i, b_product, i) for i in range(STEPS)),
                (4639, c_rstd_), (4921, c_before, 0), (4959, c_before, 1), (5123, c_square_relu, 0),
                (5213, c_square_relu, 1),
            )

            pool.memset(mhalf[:, :], -0.5).then_inc(init_done, 1)
            pool.memset(eps_t[:, :], EPS).then_inc(init_done, 1)
            pool.memset(w_prev[:, 0, :, :], 0.0).then_inc(init_done, 1)
            pool.memset(w_prev[:, 1, :, :], 0.0).then_inc(init_done, 1)
            pool.wait_ge(init_done, 4)
            run_slots(pool, plan_pool)

        @block.vector
        def _(dve):
            def stats(n, src, st, mv, st_sem, mv_sem, used):
                dve.wait_ge(used, count(n - 1, BLK, BLK))
                for q in range(BLK):
                    dve.bn_stats(st[:, q, :], src[:, q, :]).then_inc(st_sem, 1)
                dve.wait_ge(st_sem, count(n, BLK + 1, BLK))
                dve.tensor_copy(held[:, :], st[:, BLK - 1, 0:1]).then_inc(st_sem, 1)
                for q in range(BLK):
                    dve.bn_aggr(mv[:, q, :], st[:, q, :]).then_inc(mv_sem, 1)

            def norm_shift(n, mv, rs, dst, rs_sem, done, used):
                dve.wait_ge(rs_sem, count(n, 1, 1))
                dve.wait_ge(used, count(n - 1, BLK, BLK))
                dve.scalar_tensor_tensor(dst[:, :], mv[:, :, 0], -1.0, rs[:, :], ALU.mult, ALU.mult).then_inc(done, 1)

            def a_stats_(n, c):
                dve.wait_ge(x_loaded, count(n, 16, 16))
                stats(n, x_in, stats_a, mv_a, a_stats, a_mv, a_xhat)

            def a_norm_shift(n, c):
                norm_shift(n, mv_a, rstd_a, shift_a, a_rstd, a_shift, a_xhat)

            def a_xx_(n, c, h):
                if h == 0:
                    dve.wait_ge(a_T, count(n - 1, 2, 2))
                dve.wait_ge(a_sx, count(n, 2, h + 1))
                dve.scalar_tensor_tensor(xx[:, h, :].rearrange("p (b t) -> p b t", t=SEQ),
                                         sx[:, h, :].rearrange("p (b t) -> p b t", t=SEQ), A_("maa_x", h, 1),
                                         xa[:, h, :, 1:], ALU.mult, ALU.add).then_inc(a_xx, 1)

            def a_ranks_lo(n, c, i):
                dve.wait_ge(a_thi, count(n, 2, i + 1))
                if i == 0:
                    dve.wait_ge(v_stacked, count(n - 1, V_DMAS * 16, V_DMAS * 16))
                    dve.tensor_tensor(lo[:, 0, :], t_mix[:, :], hi[:, 0, :].bitcast(F32), ALU.subtract)\
                        .then_inc(a_tlo, 1)
                else:
                    dve.wait_ge(t_g_stacked, count(n - 1, G_DMAS * 16, G_DMAS * 16))
                    dve.tensor_tensor(lo_g[:, :], t_mix_g[:, :], hi_g[:, :].bitcast(F32), ALU.subtract)\
                        .then_inc(a_tlo, 1)

            def a_decay_lo(n, c):
                dve.wait_ge(a_thp, count(n, 2, 1))
                lo_rows = th_parts[P // 2:, :]
                dve.tensor_tensor(lo_rows, th[P // 2:, :], lo_rows.bitcast(F32), ALU.subtract).then_inc(a_thp, 1)

            def a_mix(n, c, f, h):
                if h == 0:
                    if f == MV:
                        dve.wait_ge(a_td1, count(n, 1, 1))
                    elif f == MR:
                        dve.wait_ge(p_k, count(n, 2, 2))
                    elif f == MG:
                        dve.wait_ge(p_v, count(n, 2, 2))
                    elif f == MW:
                        dve.wait_ge(p_g, count(n - 1, 2, 2))
                    else:
                        dve.wait_ge(p_r, count(n - 1, 2, 2))
                dve.wait_ge(a_m, count(n, 10, 2 * f + h + 1))
                dve.scalar_tensor_tensor(xf[:, f % 2, h, :], in_bank_a[f"{MIX_NAMES[f]}{h}"][:, :],
                                         A_("maa", 2 * f + h, 1), sx[:, h, :], ALU.add, ALU.mult).then_inc(a_stt, 1)

            def a_ruk_(n, c, h):
                dve.wait_ge(a_k, count(n, 2, h + 1))
                dve.wait_ge(a_w, count(n, 2, h + 1))
                dve.wait_ge(a_r, count(n, 2, h + 1))
                dve.scalar_tensor_tensor(ruk[:, h, :], r_sb[:, c, h, :], A_("u", h, 1), k_sb[:, c, h, :],
                                         ALU.mult, ALU.mult).then_inc(a_ruk, 1)

            def a_bonus_(n, c, h):
                dve.wait_ge(a_v, count(n, 2, h + 1))
                dve.wait_ge(b_y, count(n - 1, 2, h + 1))
                dve.wait_ge(a_ds, count(n, 2, h + 1))
                dve.tensor_tensor(bonus[:, h, :], in_bank_a[f"ds{h}"][:, :], v_sb[:, h, :], ALU.mult)\
                    .then_inc(a_bonus, 1)

            def a_gate_(n, c, h):
                dve.wait_ge(a_thg, count(n, 2, h + 1))
                dve.wait_ge(a_z, count(n, 2, h + 1))
                dve.scalar_tensor_tensor(gate[:, c, h, :], gate[:, c, h, :], 1.0, z_half[:, :], ALU.add,
                                         ALU.mult).then_inc(a_gate_done, 1)

            def b_outer(n, c, i):
                h = i // HS
                if i == 0:
                    dve.wait_ge(a_k, count(n, 2, 2))
                dve.wait_ge(b_v, count(n, STEPS, i + 1))
                if i >= 4:
                    dve.wait_ge(b_S, count(n, STEPS, i - 3))
                else:
                    dve.wait_ge(b_S, count(n - 1, STEPS, STEPS))
                cut = lambda t, a: t.rearrange("p (b t) -> p b t", t=SEQ)[:, :, a:a + SEQ - 1]
                dve.tensor_tensor(cut(a_in[:, i % 4, :], 1), cut(bank_v[i % 2][:, :], 0), cut(k_sb[:, c, h, :], 0),
                                  ALU.mult).then_inc(b_a, 1)

            def b_scan(n, c, i):
                if i == 0:
                    dve.wait_ge(wd_ready, 2)
                    dve.wait_ge(a_w, count(n, 2, 2))
                dve.wait_ge(b_a, count(n, STEPS, i + 1))
                dve.wait_ge(b_s0, count(n, STEPS, i + 1))
                if i >= 4:
                    dve.wait_ge(b_rS, count(n, STEPS, i - 3))
                else:
                    dve.wait_ge(b_rS, count(n - 1, STEPS, STEPS))
                dve.tensor_tensor_scan(S[:, i % 4, :], w_prev[:, c, i // HS, :], a_in[:, i % 4, :], 0.0,
                                       ALU.mult, ALU.add).then_inc(b_S, 1)

            def b_out(n, c, h):
                dve.wait_ge(b_red, count(n, QUADS, 2 * h + 2))
                dve.wait_ge(a_bonus, count(n, 2, h + 1))
                dve.wait_ge(c_cen, count(n - 1, 2, 2))
                dve.tensor_tensor(y_sb[:, h, :], bank_y[:, :], bonus[:, h, :], ALU.add).then_inc(b_y, 1)

            def c_newton(n, c, k):
                v, y, t = nw[:, 0, :], nw[:, 1, :], nw[:, 2, :]
                if k == 0:
                    dve.wait_ge(c_var, count(n, 1, 1))
                    dve.wait_ge(c_R, count(n - 1, 2, 2))
                    dve.tensor_scalar(v, bank_c[0][:, 0:P], EPS, None, ALU.add).then_inc(c_nw, 1)
                    return
                dve.wait_ge(c_nw, count(n, NEWTON, k))
                if k == 1:
                    dve.tensor_scalar(t.bitcast(I32), v.bitcast(I32), 1, None, ALU.logical_shift_right)\
                        .then_inc(c_nw, 1)
                elif k == 2:
                    dve.tensor_scalar(y.bitcast(I32), t.bitcast(I32), -1.0, float(0x5F3759DF), ALU.mult, ALU.add)\
                        .then_inc(c_nw, 1)
                elif k == NEWTON - 2:
                    dve.tensor_copy(rstd_parts[:, 0, :], y).then_inc(c_nw, 1)
                elif k == NEWTON - 1:
                    dve.tensor_tensor(rstd_parts[:, 1, :], y, rstd_parts[:, 0, :].bitcast(F32), ALU.subtract)\
                        .then_inc(c_nw, 1)
                elif k % 3 == 0:
                    dve.tensor_tensor(t, y, y, ALU.mult).then_inc(c_nw, 1)
                elif k % 3 == 1:
                    dve.scalar_tensor_tensor(t, t, -0.5, v, ALU.mult, ALU.mult).then_inc(c_nw, 1)
                else:
                    dve.scalar_tensor_tensor(y, t, 1.5, y, ALU.add, ALU.mult).then_inc(c_nw, 1)

            def c_scaled(n, c, h):
                if h == 0:
                    dve.wait_ge(wc_valid, count(n, 1, 1))
                    dve.wait_ge(c_fk, count(n - 1, 2, 2))
                dve.wait_ge(c_R, count(n, 2, h + 1))
                dve.scalar_tensor_tensor(o_sb[:, h, :], bank_c[1 - h][:, :], C_("gn_w", h, 1), c_two[:, h, :],
                                         ALU.mult, ALU.mult).then_inc(c_o1, 1)

            def c_gated(n, c, h):
                dve.wait_ge(c_o1, count(n, 2, h + 1))
                dve.scalar_tensor_tensor(o_sb[:, h, :], o_sb[:, h, :], C_("gn_b", h, 1), gate[:, c, h, :],
                                         ALU.add, ALU.mult).then_inc(c_o, 1)

            def c_residual(n, c, b):
                dve.wait_ge(res_loaded, count(n, 16, 16))
                dve.wait_ge(c_wo, count(n, 2, b + 1))
                dve.tensor_tensor(x1[:, 2 * b:2 * b + 2, :], bank_c[1 - b][:, :].rearrange("p (q c) -> p q c", c=C),
                                  x1[:, 2 * b:2 * b + 2, :], ALU.add).then_inc(c_x1, 1)

            def c_stats_(n, c):
                dve.wait_ge(c_x1, count(n, 2, 2))
                stats(n, x1, stats_c, mv_c, c_stats, c_mv, c_xh)

            def c_norm_shift(n, c):
                norm_shift(n, mv_c, rstd_c, shift_c, c_rstd, c_shift, c_xh)

            def c_mix_key(n, c, h):
                dve.wait_ge(c_wo, count(n, 2, 2))
                dve.wait_ge(c_sx, count(n, 2, h + 1))
                dve.scalar_tensor_tensor(o_sb[:, h, :].rearrange("p (b t) -> p b t", t=SEQ),
                                         c_two[:, h, :].rearrange("p (b t) -> p b t", t=SEQ), C_("mix_k", h, 1),
                                         xc[:, h, :, 1:], ALU.mult, ALU.add).then_inc(c_xk, 1)

            def c_mix_gate(n, c, h):
                dve.wait_ge(c_xk, count(n, 2, h + 1))
                dve.scalar_tensor_tensor(xr2[:, h, :].rearrange("p (b t) -> p b t", t=SEQ),
                                         c_two[:, h, :].rearrange("p (b t) -> p b t", t=SEQ), C_("mix_r", h, 1),
                                         xc[:, h, :, 1:], ALU.mult, ALU.add).then_inc(c_xr, 1)

            def c_gated_value(n, c, b):
                dve.wait_ge(c_fv, count(n, 2, b + 1))
                dve.wait_ge(c_rr, count(n, 2, b + 1))
                dve.scalar_tensor_tensor(rr[:, 2 * b:2 * b + 2, :], rr[:, 2 * b:2 * b + 2, :], 1.0,
                                         bank_c[1 - b][:, :].rearrange("p (q c) -> p q c", c=C), ALU.add,
                                         ALU.mult).then_inc(c_tmp, 1)

            def c_output(n, c, b):
                dve.wait_ge(c_tmp, count(n, 2, b + 1))
                dve.scalar_tensor_tensor(x1[:, 2 * b:2 * b + 2, :], rr[:, 2 * b:2 * b + 2, :], 0.5,
                                         x1[:, 2 * b:2 * b + 2, :], ALU.mult, ALU.add).then_inc(c_out, 1)

            plan_dve = (
                (65, a_stats_), (145, a_norm_shift), (440, a_xx_, 0), (533, a_xx_, 1), (944, a_ranks_lo, 0),
                (1127, a_mix, MW, 0), (1140, a_mix, MW, 1), (1214, a_mix, MK, 0), (1267, a_mix, MK, 1),
                (1295, a_ranks_lo, 1), (1347, a_mix, MV, 0), (1365, a_decay_lo), (1410, a_mix, MV, 1),
                (1510, a_mix, MR, 0), (1547, a_mix, MR, 1), (1605, a_mix, MG, 0), (1627, a_mix, MG, 1),
                (1784, a_ruk_, 0), (2199, a_ruk_, 1), (2206, a_gate_, 0), (2468, a_bonus_, 0), (2500, a_bonus_, 1),
                (3227, a_gate_, 1),
                *((1862 + 70 * i, b_outer, i) for i in range(STEPS)),
                *((2003 + 62 * i, b_scan, i) for i in range(STEPS)), (2922, b_out, 0), (3488, b_out, 1),
                *((4349 + 10 * i, c_newton, i) for i in range(NEWTON)), (4525, c_scaled, 0), (4544, c_gated, 0),
                (4545, c_scaled, 1), (4619, c_gated, 1), (4719, c_residual, 0), (4765, c_residual, 1),
                (4878, c_stats_), (4938, c_norm_shift), (5182, c_mix_key, 0), (5212, c_mix_key, 1),
                (5225, c_mix_gate, 0), (5293, c_mix_gate, 1), (5607, c_gated_value, 0), (5620, c_output, 0),
                (5624, c_gated_value, 1), (5663, c_output, 1),
            )

            def rank2_lo(n, c):
                dve.wait_ge(w2_hi, 1)
                dve.tensor_tensor(w2[2 * DM:, :], raw_w2[0][2 * DM:, :], w2[2 * DM:, :].bitcast(F32), ALU.subtract)\
                    .then_inc(w2_ready, 1)

            def rank2_l1_lo(n, c):
                dve.wait_ge(w2_hi, 2)
                dve.tensor_tensor(w2_other[2 * DM:, :], raw_w2[1][2 * DM:, :], w2_other[2 * DM:, :].bitcast(F32),
                                  ALU.subtract).then_inc(w2_ready, 1)

            def decay2_lo(n, c):
                dve.wait_ge(wd_hi, 2)
                for layer, to in enumerate((wd[:, C:], wd_other[:, C:])):
                    dve.tensor_tensor(to, raw_wd[:, (2 * layer + 1) * C:(2 * layer + 2) * C], to.bitcast(F32),
                                      ALU.subtract).then_inc(wd_ready, 1)

            opening_dve = ((255, rank2_lo), (560, decay2_lo), (867, rank2_l1_lo))
            dve.wait_ge(init_done, 4)
            run_slots(dve, plan_dve, opening_dve)


def by_rows(w):
    return np.concatenate([w[k * P:(k + 1) * P] for k in range(w.shape[0] // P)], axis=1)


def vec(*vs):
    return np.concatenate([np.asarray(v).reshape(HALVES, P).T for v in vs], axis=1)


def packed(a, axis):
    return np.take(a, np.concatenate([PACKED + h * P for h in range(HALVES)]), axis=axis)


def stage_a(maa_x, maa, w1, decay, td1, u, wr, wk, wv, wg, ln_w, ln_b, order):
    w1 = w1.reshape(C, NMIX, DM)[:, order]
    return np.concatenate([
        vec(ln_w, ln_b, maa_x), by_rows(w1[:, :4].reshape(C, 4 * DM)), by_rows(w1[:, 4]),
        vec(*maa, decay, u.reshape(C)),
        by_rows(np.tile(td1, (1, 2))),
        by_rows(wk.T), by_rows(packed(wv.T, 1)), by_rows(wr.T), by_rows(packed(wg.T, 1)),
    ], axis=1)


def decay_rows(td2):
    return np.concatenate([np.tile(td2, (2, 1)), np.concatenate([td2, np.zeros_like(td2)], axis=0)], axis=1)


def stage_c(wo, fk, fr, fv, gn_w, gn_b, ln_w, ln_b, mix_k, mix_r):
    return np.concatenate([
        by_rows(packed(wo.T, 0)), by_rows(fk.T), by_rows(fr.T), by_rows(fv.T),
        vec(packed(gn_w, 0), packed(gn_b, 0), ln_w, ln_b, mix_k, mix_r),
    ], axis=1)


def constants():
    out = np.zeros((P, COLS_K["total"]), np.float32)
    out_r = np.zeros((P, COLS_R["total"]), np.float32)

    def put(name, i, m):
        to, table = (out_r, COLS_R) if name in COLS_R else (out, COLS_K)
        at = table[name][0] + i * m.shape[1]
        to[:, at:at + m.shape[1]] = m

    ch = np.arange(P)
    head = ch // HS
    p_head = PACKED // HS
    put("ident", 0, np.eye(P, dtype=np.float32))
    for m in range(4):
        row = ch % 64
        put("spread", m, ((row[:, None] // HPH == m) & (row[:, None] % HPH == head[None])).astype(np.float32))
    for jq in range(2):
        m = np.zeros((P, 32), np.float32)
        m[ch, HPH * jq + head] = 1
        put("gather", jq, m)
    same = (p_head[:, None] == p_head[None]).astype(np.float32)
    put("center", 0, np.eye(P, dtype=np.float32) - same / np.float32(HS))
    put("headsum", 0, (head[:, None] == p_head[None]).astype(np.float32))
    for h in range(HALVES):
        m = np.zeros((P, 32), np.float32)
        m[ch, HPH * h + p_head] = 1 / HS
        put("var", h, m)
        for q in range(BLK):
            m = np.zeros((P, P), np.float32)
            m[32 * q + HPH * h + p_head, ch] = 1
            put("rstd", 4 * h + q, m)
    return out, out_r


def kernel(**inputs):
    import concourse.bacc as bacc
    from concourse.bass_utils import run_bass_kernel_spmd

    a = {k: np.asarray(v) for k, v in inputs.items()}
    l0 = {k[len("L0_xattn_"):]: v for k, v in a.items() if k.startswith("L0_xattn_")}
    l1 = {k[len("L1_xattn_"):]: v for k, v in a.items() if k.startswith("L1_xattn_")}
    stack = l0["maa_stack"].reshape(NMIX, C)
    order0 = [1, 0, 2, 3, 4]
    order1 = [0, 1, 2, 3, 4]
    weights_a = np.stack([
        stage_a(l0["maa_x"], [stack[i] for i in order0], l0["maa_w1"], l0["time_decay"], l0["td_w1"],
                l0["u"], l0["Wr"], l0["Wk"], l0["Wv"], l0["Wg"], l0["ln1_w"], l0["ln1_b"], order0),
        stage_a(l1["maa_x"], [l1["maa_w"], l1["maa_k"], l1["maa_v"], l1["maa_r"], l1["maa_g"]], l1["maa_w1"],
                l1["time_decay"], l1["decay_w1"], l1["faaaa"], l1["Wr"], l1["Wk"],
                l1["Wv"], l1["Wg"], l1["ln1_w"], l1["ln1_b"], order1)])
    weights_2 = np.stack([np.tile(l["maa_w2"][order].transpose(1, 0, 2).reshape(DM, RANK2_COLS), (3, 1))
                          for l, order in ((l0, order0), (l1, order1))])
    decay_2 = np.concatenate([decay_rows(l0["td_w2"]), decay_rows(l1["decay_w2"])], axis=1)
    weights_c = np.stack([
        stage_c(l0["Wo"], l0["Wfk"], l0["Wfr"], l0["Wfv"], l0["gn_w"], l0["gn_b"], l0["ln2_w"], l0["ln2_b"],
                l0["ffn_maa_k"], l0["ffn_maa_r"]),
        stage_c(l1["Wo"], l1["fWk"], l1["fWr"], l1["fWv"], l1["gn_w"], l1["gn_b"], l1["ln2_w"], l1["ln2_b"],
                l1["fmaa_k"], l1["fmaa_r"])])
    ctx = a["ctx_2048"]
    s0 = ctx[:, 2:2 + HS].reshape(TILES, ROWS, HALVES, HPH, HS, HS).transpose(0, 3, 4, 2, 5, 1)
    s0 = s0.reshape(TILES, P, HALVES, HS * ROWS)
    rows = ctx[:, :2].reshape(TILES, ROWS, 2, HALVES, P).transpose(2, 0, 4, 3, 1)
    state = np.concatenate([np.concatenate([s0, rows[1]], axis=3).reshape(TILES, P, HALVES * HALF_STATE),
                            rows[0].reshape(TILES, P, HALVES * ROWS)], axis=2)
    consts, consts_r = constants()
    arrays = {
        "x": a["x"].reshape(BATCH * SEQ, C), "state": state, "weights_a": weights_a,
        "weights_2": weights_2, "decay_2": decay_2, "weights_c": weights_c,
        "consts": consts, "consts_r": consts_r,
    }
    arrays = {k: np.ascontiguousarray(v) for k, v in arrays.items()}
    nc = bacc.Bacc("TRN2", target_bir_lowering=False, num_devices=1)
    args = [nc.dram_tensor(k, v.shape, F32, kind="ExternalInput").ap() for k, v in arrays.items()]
    out = nc.dram_tensor("out", [BATCH * SEQ, C], F32, kind="ExternalOutput").ap()
    build(nc, *args, out)
    r = run_bass_kernel_spmd(nc, [arrays], core_ids=[0])
    return r.results[0]["out"].reshape(BATCH, SEQ, C)
```
